# Optimizing a Trainium2 kernel written in Bass

```python
import numpy as np
import jax
import jax.numpy as jnp

def _softmax(x, axis=-1):
    return jax.nn.softmax(x, axis=axis)

def _gelu(x):
    return jax.nn.gelu(x, approximate=True)

def _silu(x):
    return jax.nn.silu(x)

def _sigmoid(x):
    return jax.nn.sigmoid(x)

def _layernorm(x, axis=-1, eps=1e-05):
    m = jnp.mean(x, axis=axis, keepdims=True)
    v = jnp.var(x, axis=axis, keepdims=True)
    return (x - m) / jnp.sqrt(v + eps)

def _scatter_add(tgt, idx, src, axis=0):
    return tgt.at[idx].add(src)

def _segment_sum(src, seg, n):
    return jax.ops.segment_sum(src, seg, n)
kernel_name = 'mk_perceiver_d2_seqx_r2_b8dc39'

def setup_inputs(seed: int=0):
    np.random.seed(seed)
    _w = jnp.asarray

    def _rec_inputs():
        import jax
        import jax.numpy as jnp
        _rk = jax.random.key(seed)
        x = 0.000341 + 1 * jax.random.normal(jax.random.fold_in(_rk, 1), (4, 128, 512), jnp.float32)
        _lenS = 128 - jax.random.randint(jax.random.fold_in(_rk, 7), (4,), 0, max(1, 128 // 4) + 1, jnp.int32)
        _lenS2 = 2048 - jax.random.randint(jax.random.fold_in(_rk, 8), (4,), 0, max(1, 2048 // 4) + 1, jnp.int32)
        _ctx_1024P = jax.random.normal(jax.random.fold_in(_rk, 11), (4, 16, 512), jnp.float32)
        _ctx_1024c = jax.random.dirichlet(jax.random.fold_in(_rk, 511), 0.3 * jnp.ones((16,), jnp.float32), (4, 2048))
        _ctx_1024t = jnp.einsum('bsk,bkd->bsd', _ctx_1024c, _ctx_1024P)
        _ctx_1024t = _ctx_1024t * jax.lax.rsqrt(jnp.mean(jnp.square(_ctx_1024t)) + 1e-12) * 0.953939
        ctx_1024 = -0.000392918 + 0.999932 * (_ctx_1024t + 0.3 * jax.random.normal(jax.random.fold_in(_rk, 611), (4, 2048, 512), jnp.float32))
        _validS = jnp.arange(128)[None, :] < _lenS[:, None]
        _validS2 = jnp.arange(2048)[None, :] < _lenS2[:, None]
        _causal = jnp.tril(jnp.ones((128, 128), dtype=bool))
        mask_1_bf0 = jnp.logical_not(jnp.ones((1,), dtype=bool))
        return (x, ctx_1024, mask_1_bf0)
    x, ctx_1024, mask_1_bf0 = _rec_inputs()

    def _L0_xattn_setup():
        import jax, jax.numpy as jnp
        import numpy as np
        B, SQ, SK, D_IN, D_H, D_OUT = (8, 1024, 1024, 512, 512, 512)
        key0 = jax.random.key(seed)
        ks = jax.random.split(key0, 8)
        return {'key': jax.random.normal(ks[0], (B, SK, D_IN), jnp.float32), 'value': jax.random.normal(ks[1], (B, SK, D_H), jnp.float32), 'query': jax.random.normal(ks[2], (B, SQ, D_IN), jnp.float32), 'mask': jnp.zeros((1,), jnp.bool_), 'inv_scale_factor': 32, 'W1': jax.random.normal(ks[3], (D_H, D_IN), jnp.float32) * (1.0 / np.sqrt(D_IN)), 'b1': jax.random.normal(ks[4], (D_H,), jnp.float32) * 0.01, 'W2': jax.random.normal(ks[5], (D_H, D_IN), jnp.float32) * (1.0 / np.sqrt(D_IN)), 'b2': jax.random.normal(ks[6], (D_H,), jnp.float32) * 0.01, 'W3': jax.random.normal(ks[7], (D_OUT, D_H), jnp.float32) * (1.0 / np.sqrt(D_H))}
    _L0_xattn_all = _L0_xattn_setup()
    _L0_xattn_in = {k: v for k, v in _L0_xattn_all.items() if k in ('W1', 'b1', 'W2', 'b2', 'W3')}
    del _L0_xattn_all

    def _L0_attn_setup():
        import jax, jax.numpy as jnp
        import numpy as np
        import math
        D_MODEL = 512
        N_HEADS = 16
        D_HEAD = D_MODEL // N_HEADS
        SEQ = 1024
        BATCH = 2
        key = jax.random.key(seed)
        ks = jax.random.split(key, 8)
        xav = math.sqrt(2.0 / (D_MODEL + D_MODEL))

        def lin(k):
            return jax.random.normal(k, (D_MODEL, D_MODEL), jnp.float32) * xav
        zeros = jnp.zeros((D_MODEL,), jnp.float32)
        return {'x': jax.random.normal(ks[0], (SEQ, BATCH, D_MODEL), jnp.float32), 'beta': jax.random.normal(ks[1], (N_HEADS,), jnp.float32) * 0.1, 'Wq': lin(ks[2]), 'bq': zeros, 'Wk': lin(ks[3]), 'bk': zeros, 'Wv': lin(ks[4]), 'bv': zeros, 'Wo': lin(ks[5]), 'bo': zeros}
    _L0_attn_all = _L0_attn_setup()
    _L0_attn_in = {k: v for k, v in _L0_attn_all.items() if k in ('beta', 'Wq', 'bq', 'Wk', 'bk', 'Wv', 'bv', 'Wo', 'bo')}
    del _L0_attn_all

    def _L0_ffn_setup():
        import jax, jax.numpy as jnp
        import numpy as np
        B, S, D = (4, 512, 512)
        E, K = (8, 2)
        H = 2 * D
        key = jax.random.key(seed)
        ks = jax.random.split(key, 5)
        x = jax.random.normal(ks[0], (B, S, D), dtype=jnp.float32)
        Wg = jax.random.normal(ks[1], (E, D), dtype=jnp.float32) * 0.02
        W1 = jax.random.normal(ks[2], (E, H, D), dtype=jnp.float32) * 0.02
        W2 = jax.random.normal(ks[3], (E, H, D), dtype=jnp.float32) * 0.02
        W3 = jax.random.normal(ks[4], (E, D, H), dtype=jnp.float32) * 0.02
        return {'x': x, 'Wg': Wg, 'W1': W1, 'W2': W2, 'W3': W3}
    _L0_ffn_all = _L0_ffn_setup()
    _L0_ffn_in = {k: v for k, v in _L0_ffn_all.items() if k in ('Wg', 'W1', 'W2', 'W3')}
    del _L0_ffn_all

    def _L1_xattn_setup():
        import jax, jax.numpy as jnp
        import numpy as np
        D_MODEL = 512
        N_HEADS = 16
        D_HEAD = D_MODEL // N_HEADS
        key = jax.random.key(seed)
        ks = jax.random.split(key, 6)
        query = jax.random.normal(ks[0], (2, 1024, D_MODEL), dtype=jnp.float32)
        context = jax.random.normal(ks[1], (2, 2048, D_MODEL), dtype=jnp.float32)
        s = 1.0 / np.sqrt(D_MODEL)
        Wq = jax.random.normal(ks[2], (D_MODEL, D_MODEL), dtype=jnp.float32) * s
        Wk = jax.random.normal(ks[3], (D_MODEL, D_MODEL), dtype=jnp.float32) * s
        Wv = jax.random.normal(ks[4], (D_MODEL, D_MODEL), dtype=jnp.float32) * s
        Wo = jax.random.normal(ks[5], (D_MODEL, D_MODEL), dtype=jnp.float32) * s
        return {'query': query, 'context': context, 'Wq': Wq, 'Wk': Wk, 'Wv': Wv, 'Wo': Wo}
    _L1_xattn_all = _L1_xattn_setup()
    _L1_xattn_in = {k: v for k, v in _L1_xattn_all.items() if k in ('Wq', 'Wk', 'Wv', 'Wo')}
    del _L1_xattn_all

    def _L1_attn_setup():
        import jax, jax.numpy as jnp
        import numpy as np
        D_MODEL = 512
        N_HEADS = 16
        D_HEAD = 64
        B, S = (8, 512)
        EPS = 1.1920929e-07
        key = jax.random.key(seed)
        k1, k2, k3 = jax.random.split(key, 3)
        x = jax.random.normal(k1, (B, S, D_MODEL), dtype=jnp.float32)
        W_qkv = jax.random.normal(k2, (3 * N_HEADS * D_HEAD, D_MODEL), dtype=jnp.float32) * 0.02
        b_qkv = jnp.zeros((3 * N_HEADS * D_HEAD,), dtype=jnp.float32)
        W_o = jax.random.normal(k3, (D_MODEL, N_HEADS * D_HEAD), dtype=jnp.float32) * 0.02
        b_o = jnp.zeros((D_MODEL,), dtype=jnp.float32)
        return {'x': x, 'W_qkv': W_qkv, 'b_qkv': b_qkv, 'W_o': W_o, 'b_o': b_o}
    _L1_attn_all = _L1_attn_setup()
    _L1_attn_in = {k: v for k, v in _L1_attn_all.items() if k in ('W_qkv', 'b_qkv', 'W_o', 'b_o')}
    del _L1_attn_all

    def _L1_ffn_setup():
        import jax, jax.numpy as jnp
        import numpy as np
        EPS = 1e-05

        def rmsnorm(x):
            return x * jax.lax.rsqrt(jnp.mean(x * x, axis=-1, keepdims=True) + EPS)

        def act_quant(x):
            scale = 127.0 / jnp.clip(jnp.max(jnp.abs(x), axis=-1, keepdims=True), 1e-05)
            q = jnp.clip(jnp.round(x * scale), -128.0, 127.0) / scale
            return x + jax.lax.stop_gradient(q - x)

        def weight_quant(w):
            scale = 1.0 / jnp.clip(jnp.mean(jnp.abs(w)), 1e-05)
            q = jnp.clip(jnp.round(w * scale), -1.0, 1.0) / scale
            return w + jax.lax.stop_gradient(q - w)

        def bitlinear(x, w, b):
            xq = act_quant(rmsnorm(x))
            wq = weight_quant(w)
            return jnp.einsum('bsd,fd->bsf', xq, wq) + b
        key = jax.random.key(seed)
        k0, k1, k2 = jax.random.split(key, 3)
        B, S, D, F = (2, 4096, 512, 2048)
        x = jax.random.normal(k0, (B, S, D), dtype=jnp.float32)
        w1 = jax.random.normal(k1, (F, D), dtype=jnp.float32) * (1.0 / np.sqrt(D))
        b1 = jnp.zeros((F,), dtype=jnp.float32)
        w2 = jax.random.normal(k2, (D, F), dtype=jnp.float32) * (1.0 / np.sqrt(F))
        b2 = jnp.zeros((D,), dtype=jnp.float32)
        return {'x': x, 'w1': w1, 'b1': b1, 'w2': w2, 'b2': b2}
    _L1_ffn_all = _L1_ffn_setup()
    _L1_ffn_in = {k: v for k, v in _L1_ffn_all.items() if k in ('w1', 'b1', 'w2', 'b2')}
    del _L1_ffn_all
    return {'x': x, 'ctx_1024': ctx_1024, 'mask_1_bf0': mask_1_bf0, 'L0_xattn_W1': _L0_xattn_in['W1'], 'L0_xattn_b1': _L0_xattn_in['b1'], 'L0_xattn_W2': _L0_xattn_in['W2'], 'L0_xattn_b2': _L0_xattn_in['b2'], 'L0_xattn_W3': _L0_xattn_in['W3'], 'L0_attn_beta': _L0_attn_in['beta'], 'L0_attn_Wq': _L0_attn_in['Wq'], 'L0_attn_bq': _L0_attn_in['bq'], 'L0_attn_Wk': _L0_attn_in['Wk'], 'L0_attn_bk': _L0_attn_in['bk'], 'L0_attn_Wv': _L0_attn_in['Wv'], 'L0_attn_bv': _L0_attn_in['bv'], 'L0_attn_Wo': _L0_attn_in['Wo'], 'L0_attn_bo': _L0_attn_in['bo'], 'L0_ffn_Wg': _L0_ffn_in['Wg'], 'L0_ffn_W1': _L0_ffn_in['W1'], 'L0_ffn_W2': _L0_ffn_in['W2'], 'L0_ffn_W3': _L0_ffn_in['W3'], 'L1_xattn_Wq': _L1_xattn_in['Wq'], 'L1_xattn_Wk': _L1_xattn_in['Wk'], 'L1_xattn_Wv': _L1_xattn_in['Wv'], 'L1_xattn_Wo': _L1_xattn_in['Wo'], 'L1_attn_W_qkv': _L1_attn_in['W_qkv'], 'L1_attn_b_qkv': _L1_attn_in['b_qkv'], 'L1_attn_W_o': _L1_attn_in['W_o'], 'L1_attn_b_o': _L1_attn_in['b_o'], 'L1_ffn_w1': _L1_ffn_in['w1'], 'L1_ffn_b1': _L1_ffn_in['b1'], 'L1_ffn_w2': _L1_ffn_in['w2'], 'L1_ffn_b2': _L1_ffn_in['b2']}

def reference(x, ctx_1024, mask_1_bf0, L0_xattn_W1, L0_xattn_b1, L0_xattn_W2, L0_xattn_b2, L0_xattn_W3, L0_attn_beta, L0_attn_Wq, L0_attn_bq, L0_attn_Wk, L0_attn_bk, L0_attn_Wv, L0_attn_bv, L0_attn_Wo, L0_attn_bo, L0_ffn_Wg, L0_ffn_W1, L0_ffn_W2, L0_ffn_W3, L1_xattn_Wq, L1_xattn_Wk, L1_xattn_Wv, L1_xattn_Wo, L1_attn_W_qkv, L1_attn_b_qkv, L1_attn_W_o, L1_attn_b_o, L1_ffn_w1, L1_ffn_b1, L1_ffn_w2, L1_ffn_b2):
    import jax
    import jax.numpy as jnp

    def _L0_xattn_ref(key, value, query, mask, inv_scale_factor, W1, b1, W2, b2, W3):
        import jax, jax.numpy as jnp
        import numpy as np
        B, SQ, SK, D_IN, D_H, D_OUT = (8, 1024, 1024, 512, 512, 512)
        q = jnp.einsum('bqd,hd->bqh', query, W1) + b1
        k = jnp.einsum('bkd,hd->bkh', key, W2) + b2
        qk = jnp.einsum('bqh,bkh->bqk', q, k) / inv_scale_factor
        attn = jax.nn.softmax(qk, axis=-1)
        ctx = jnp.einsum('bqk,bkh->bqh', attn, value)
        out = jnp.einsum('bqh,oh->bqo', ctx, W3)
        return out

    def _L0_attn_ref(x, beta, Wq, bq, Wk, bk, Wv, bv, Wo, bo):
        import jax, jax.numpy as jnp
        import numpy as np
        import math
        D_MODEL = 512
        N_HEADS = 16
        D_HEAD = D_MODEL // N_HEADS
        SEQ = 1024
        BATCH = 2
        s, b, d = x.shape
        h, dh = (N_HEADS, D_HEAD)

        def proj(W, bias):
            y = x @ W.T + bias
            return y.reshape(s, b, h, dh).transpose(1, 2, 0, 3)
        q = proj(Wq, bq)
        k = proj(Wk, bk)
        v = proj(Wv, bv)
        scale = math.sqrt(dh) * jnp.exp(beta)[None, :, None, None]
        q = jax.nn.softplus(q / scale)
        k = jax.nn.softplus(k / scale)
        kv = jnp.cumsum(k[..., :, None] * v[..., None, :], axis=2)
        kn = jnp.cumsum(k, axis=2)
        num = jnp.einsum('bhsk,bhskv->bhsv', q, kv)
        den = jnp.einsum('bhsk,bhsk->bhs', q, kn)
        out = num / den[..., None]
        out = out.transpose(2, 0, 1, 3).reshape(s, b, d)
        return out @ Wo.T + bo

    def _L0_ffn_ref(x, Wg, W1, W2, W3):
        import jax, jax.numpy as jnp
        import numpy as np
        B, S, D = (4, 512, 512)
        E, K = (8, 2)
        H = 2 * D
        gate_out = jnp.einsum('bsd,ed->bse', x, Wg)
        top_v, top_i = jax.lax.top_k(gate_out, K)
        probs = jax.nn.softmax(top_v, axis=-1)
        out = jnp.zeros_like(x)
        for e in range(E):
            w_e = jnp.sum(probs * (top_i == e), axis=-1)
            h1 = jnp.einsum('bsd,hd->bsh', x, W1[e])
            h2 = jnp.einsum('bsd,hd->bsh', x, W2[e])
            g = h1 * jax.nn.sigmoid(h1) * h2
            y = jnp.einsum('bsh,dh->bsd', g, W3[e])
            out = out + y * w_e[..., None]
        return out

    def _L1_xattn_ref(query, context, Wq, Wk, Wv, Wo):
        import jax, jax.numpy as jnp
        import numpy as np
        D_MODEL = 512
        N_HEADS = 16
        D_HEAD = D_MODEL // N_HEADS
        B, T_q, D = query.shape
        T_c = context.shape[1]
        Q = (query @ Wq.T).reshape(B, T_q, N_HEADS, D_HEAD)
        K = (context @ Wk.T).reshape(B, T_c, N_HEADS, D_HEAD)
        V = (context @ Wv.T).reshape(B, T_c, N_HEADS, D_HEAD)
        scale = jnp.sqrt(jnp.asarray(D_HEAD, dtype=query.dtype))
        scores = jnp.einsum('bqhd,bkhd->bhqk', Q, K) / scale
        attn = jax.nn.softmax(scores, axis=-1)
        out = jnp.einsum('bhqk,bkhd->bqhd', attn, V).reshape(B, T_q, D)
        return out @ Wo.T

    def _L1_attn_ref(x, W_qkv, b_qkv, W_o, b_o):
        import jax, jax.numpy as jnp
        import numpy as np
        D_MODEL = 512
        N_HEADS = 16
        D_HEAD = 64
        B, S = (8, 512)
        EPS = 1.1920929e-07
        normed = x * jax.lax.rsqrt(jnp.mean(x * x, axis=-1, keepdims=True) + EPS)
        qkv = normed @ W_qkv.T + b_qkv
        qkv = qkv.reshape(*qkv.shape[:-1], N_HEADS, D_HEAD, 3)
        q, k, v = (qkv[..., 0], qkv[..., 1], qkv[..., 2])
        scores = jnp.einsum('bqhd,bkhd->bhqk', q, k)
        seq = x.shape[-2]
        causal_mask = jnp.triu(jnp.ones((seq, seq), dtype=bool), k=1)
        scores = jnp.where(causal_mask, -jnp.inf, scores)
        attn = jax.nn.softmax(scores, axis=-2)
        z = jnp.einsum('bhqk,bkhd->bqhd', attn, v)
        z = z.reshape(*z.shape[:-2], N_HEADS * D_HEAD)
        return z @ W_o.T + b_o

    def _L1_ffn_ref(x, w1, b1, w2, b2):
        import jax, jax.numpy as jnp
        import numpy as np
        EPS = 1e-05

        def rmsnorm(x):
            return x * jax.lax.rsqrt(jnp.mean(x * x, axis=-1, keepdims=True) + EPS)

        def act_quant(x):
            scale = 127.0 / jnp.clip(jnp.max(jnp.abs(x), axis=-1, keepdims=True), 1e-05)
            q = jnp.clip(jnp.round(x * scale), -128.0, 127.0) / scale
            return x + jax.lax.stop_gradient(q - x)

        def weight_quant(w):
            scale = 1.0 / jnp.clip(jnp.mean(jnp.abs(w)), 1e-05)
            q = jnp.clip(jnp.round(w * scale), -1.0, 1.0) / scale
            return w + jax.lax.stop_gradient(q - w)

        def bitlinear(x, w, b):
            xq = act_quant(rmsnorm(x))
            wq = weight_quant(w)
            return jnp.einsum('bsd,fd->bsf', xq, wq) + b
        h = bitlinear(x, w1, b1)
        h = jax.nn.gelu(h, approximate=False)
        return bitlinear(h, w2, b2)
    x = x + _L0_xattn_ref(ctx_1024, ctx_1024, _layernorm(x, axis=-1), mask_1_bf0, 32, L0_xattn_W1, L0_xattn_b1, L0_xattn_W2, L0_xattn_b2, L0_xattn_W3)
    x = x + _L0_attn_ref(_layernorm(x, axis=-1), L0_attn_beta, L0_attn_Wq, L0_attn_bq, L0_attn_Wk, L0_attn_bk, L0_attn_Wv, L0_attn_bv, L0_attn_Wo, L0_attn_bo)
    x = x + _L0_ffn_ref(_layernorm(x, axis=-1), L0_ffn_Wg, L0_ffn_W1, L0_ffn_W2, L0_ffn_W3)
    x = x + _L1_xattn_ref(_layernorm(x, axis=-1), ctx_1024, L1_xattn_Wq, L1_xattn_Wk, L1_xattn_Wv, L1_xattn_Wo)
    x = x + _L1_attn_ref(_layernorm(x, axis=-1), L1_attn_W_qkv, L1_attn_b_qkv, L1_attn_W_o, L1_attn_b_o)
    x = x + _L1_ffn_ref(_layernorm(x, axis=-1), L1_ffn_w1, L1_ffn_b1, L1_ffn_w2, L1_ffn_b2)
    return x

_drawn_inputs = setup_inputs


def setup_inputs(seed=0):
    import zlib

    import numpy as np

    out = dict(_drawn_inputs(seed))
    spreads = {'L0_attn_bq': (0.0, 2.0),
     'L0_attn_bk': (0.0, 2.0),
     'L0_attn_bv': (0.0, 0.1),
     'L0_attn_bo': (0.0, 0.1),
     'L1_attn_b_qkv': (0.0, 0.1),
     'L1_attn_b_o': (0.0, 0.1),
     'L1_ffn_b1': (0.0, 0.1),
     'L1_ffn_b2': (0.0, 0.1)}
    factors = {'L0_xattn_b1': 32.3,
     'L0_xattn_b2': 64.0,
     'L0_attn_beta': 8.0,
     'L0_attn_Wq': 8.0,
     'L0_attn_Wk': 4.724}
    for name, (base, spread) in spreads.items():
        noise = np.random.default_rng([zlib.crc32(name.encode()), seed]).standard_normal(out[name].shape)
        drawn = base * np.exp(spread * noise) if base else spread * noise
        out[name] = jnp.asarray(drawn.astype(out[name].dtype))
    for name, factor in factors.items():
        out[name] = (out[name] * factor).astype(out[name].dtype)
    return out
```

```python
from contextlib import ExitStack

import concourse.bass as bass
from concourse import mybir
from concourse.alu_op_type import AluOpType as ALU

ACT = mybir.ActivationFunctionType
AX = mybir.AxisListType.X
F32 = mybir.dt.float32
F32R = mybir.dt.float32r
BF16 = mybir.dt.bfloat16

P = 128
D = 512
KC = D // P
NB = 4
T = NB * P
SK = 2048
CH = 512
NCH = SK // CH
NE = 8
HE = 1024
UE = HE // P
H0, DH0 = 16, 32
H1, DH1 = 16, 64
DQ = H1 * DH1
FF = 2048
FC = FF // P
KB = 256
MAGIC = 1.5 * 2.0 ** 23
NEG = -3.0e38
AHEAD = 1
LAST = 6


def build(nc, a, out, stages=LAST):
    ctx = ExitStack()
    with ctx:
        def sb(name, shape, dt=F32):
            return ctx.enter_context(nc.sbuf_tensor(name, shape, dt))

        def sem(name):
            return ctx.enter_context(nc.semaphore(name))

        X = sb("X", [P, NB, D])
        Y = sb("Y", [P, NB, D])
        XT = sb("XT", [P, KC, T])
        BI = sb("BI", [P, 8 * KB])
        FA = sb("FA", [P, 104 * KB])
        RA = sb("RA", [P, 64 * KB], F32R)
        ident = sb("ident", [P, P])
        identb = sb("identb", [P, P], BF16)
        caus = sb("caus", [P, P])
        ones = sb("ones", [P, P])
        rev8 = sb("rev8", [P, NE])
        st = sb("st", [P, NB, 6])
        mv = sb("mv", [P, NB, 2])
        rstd = sb("rstd", [P, NB])
        root = sb("root", [P, NB])
        rtmp = sb("rtmp", [P, NB])
        sm = sb("sm", [P, 256])
        bcol = sb("bcol", [P, 32])
        PS = ctx.enter_context(nc.psum_tensor("PS", [P, 8 * 512], F32))

        TB = (4, 5, 7, 4)

        def bank(i, n=1):
            return PS[:, 512 * i:512 * (i + n)]

        def fa(kb, n):
            return FA[:, kb * KB:(kb + n) * KB]

        def ra(kb, n):
            return RA[:, kb * KB:(kb + n) * KB]

        def v3(ap, n):
            return ap.rearrange("p (a n) -> p a n", a=n)

        b1c, b2c = bcol[:, 0:4], bcol[:, 4:8]
        bqc, bkc = bcol[:, 8:16], bcol[:, 16:24]

        a_ct = [v3(fa(8 * i, 8), KC) for i in range(4)]
        a_cn = [v3(fa(32 + 8 * i, 8), 4) for i in range(4)]
        a_p = fa(64, 8)
        a_pt = v3(fa(72, 8), 16)
        a_qt = v3(fa(80, 8), KC)
        a_ao = v3(fa(80, 8), NB)
        a_wa = v3(fa(88, 8), KC)
        a_wb = v3(fa(96, 8), KC)
        a_qp = v3(BI[:, :], KC)
        b_w = [v3(fa(8 * i, 8), KC) for i in range(4)]
        b_z = v3(fa(32, 16), 8)
        b_v = v3(fa(48, 8), NB)
        b_s1, b_s2, b_s3 = fa(56, 16), fa(72, 16), fa(88, 16)
        b_ao = v3(fa(88, 8), NB)
        NST = 4
        c_st = [v3(fa(6 * i, 6), 3) for i in range(NST)]
        c_sg, c_tt, c_g = fa(24, 2), fa(26, 2), fa(28, 2)
        c_wg = fa(30, 1)[:, 0:KC * NE].rearrange("p (k e) -> p k e", k=KC)
        c_xh, c_xl = v3(ra(0, 8), KC), v3(ra(8, 8), KC)
        c_wh = [v3(ra(16 + 12 * i, 6), 3) for i in range(2)]
        c_wl = [v3(ra(22 + 12 * i, 6), 3) for i in range(2)]
        c_gh = [ra(40 + 4 * i, 2) for i in range(2)]
        c_gl = [ra(42 + 4 * i, 2) for i in range(2)]
        d_st = [v3(fa(8 * i, 8), KC) for i in range(2)]
        d_kt = v3(fa(16, 32), KC)
        d_v = v3(fa(48, 32), 16)
        d_p = [fa(80 + 8 * i, 8) for i in range(2)]
        d_wq = v3(fa(80, 8), KC)
        d_ws = [v3(fa(48 + 8 * i, 8), KC) for i in range(2)]
        d_pt = v3(BI[:, :], 16)
        d_qz = v3(fa(96, 8), 16)
        d_wo = v3(fa(16, 8), KC)
        d_wh = [v3(ra(16 * i, 8), KC) for i in range(2)]
        d_wl = [v3(ra(8 + 16 * i, 8), KC) for i in range(2)]
        d_ch = [v3(ra(32 + 16 * i, 8), KC) for i in range(2)]
        d_cl = [v3(ra(40 + 16 * i, 8), KC) for i in range(2)]
        d_rx = sb("d_rx", [P, D])
        g_ = sb("per_token", [P, 192])
        e_w = [v3(fa(16 * i, 16), KC) for i in range(3)]
        e_qt, e_kt = v3(fa(48, 16), 8), v3(fa(64, 16), 8)
        e_v = v3(fa(80, 16), NB)
        e_wo = v3(fa(0, 16), 8)
        e_e = v3(fa(16, 32), 64)
        e_zt = v3(fa(48, 16), 8)

        def e_head(g, j):
            return 8 * (g // 2) + 2 * j + g % 2

        def e_place(h):
            return 8 * (h // 8) + 4 * (h % 2) + h % 8 // 2

        e_nm, e_rs, e_ri = g_[:, 0:64], g_[:, 64:128], g_[:, 128:192]
        f_w1 = v3(fa(0, 32), KC)
        f_w2 = v3(fa(32, 32), FC)
        f_w1b = v3(fa(64, 16).bitcast(BF16), KC)
        f_w2b = v3(fa(80, 16).bitcast(BF16), FC)
        f_h = [fa(8 * i, 8) for i in range(2)]
        f_sq = fa(16, 8)
        f_hb = [fa(24 + 4 * i, 4).bitcast(BF16) for i in range(2)]
        f_ht = [v3(fa(32 + 4 * i, 4).bitcast(BF16), FC) for i in range(2)]
        f_yb = v3(fa(40, 4).bitcast(BF16), NB)
        f_yt = v3(fa(44, 4).bitcast(BF16), KC)

        const_ready = sem("const_ready")
        const_step = sem("const_step")
        x_landed = sem("x_landed")
        out_stored = sem("out_stored")
        dve = sem("dve_chain")
        root_asked = sem("root_asked")
        root_done = sem("root_done")
        ln_done = sem("ln_done")
        ln_turned = sem("ln_turned")
        xt_act = sem("xt_act")
        xt_dve = sem("xt_dve")

        aw_landed = [sem(f"a_w{i}_landed") for i in range(3)]
        ab_landed = sem("a_b_landed")
        act_landed = [sem(f"a_ct{i}_landed") for i in range(4)]
        acn_landed = [sem(f"a_cn{i}_landed") for i in range(4)]
        a_q = sem("a_q")
        a_qev = sem("a_qev")
        a_qpd = sem("a_qpd")
        a_qb = sem("a_qb")
        a_qpe_act = sem("a_qpe_act")
        a_qpe_dve = sem("a_qpe_dve")
        a_s = sem("a_s")
        a_nb = sem("a_nb")
        a_exp = sem("a_exp")
        a_t = sem("a_t")
        a_pte = sem("a_pte")
        a_pto = sem("a_pto")
        a_pv = sem("a_pv")
        a_o = sem("a_o")
        o_turned = sem("o_turned")
        o_act = sem("o_act")
        o_dve = sem("o_dve")
        proj_done = sem("proj_done")
        x_added = sem("x_added")

        bw_landed = [sem(f"b_w{i}_landed") for i in range(4)]
        bb_landed = sem("b_b_landed")
        b_p = sem("b_p")
        b_zq = sem("b_zq")
        b_beta = sem("b_beta")
        b_zs = sem("b_zs")
        b_u = sem("b_u")
        b_w1p = sem("b_w1p")
        b_ln = sem("b_ln")
        b_o = sem("b_o")

        cg_landed = sem("c_wg_landed")
        c_landed = [sem(f"c_w{i}_landed") for i in range(NST)]
        c_gate = sem("c_gate")
        c_diff = sem("c_diff")
        c_e = sem("c_e")
        c_xhd = sem("c_xh_done")
        c_xld = sem("c_xl_done")
        c_hi12 = sem("c_hi12")
        c_lo12 = sem("c_lo12")
        c_hi3 = sem("c_hi3")
        c_lo3 = sem("c_lo3")
        c_h = sem("c_h")
        c_sig = sem("c_sig")
        c_t = sem("c_t")
        c_gd = sem("c_gd")
        c_ghd = sem("c_ghd")
        c_gld = sem("c_gld")
        c_y = sem("c_y")
        c_acc = sem("c_acc")

        dw_landed = [sem(f"d_w{i}_landed") for i in range(4)]
        d_landed = [sem(f"d_ct{i}_landed") for i in range(2)]
        d_whd = sem("d_whd")
        d_wld = sem("d_wld")
        d_hi = sem("d_hi")
        d_lo = sem("d_lo")
        d_q = sem("d_q")
        d_qev = sem("d_qev")
        d_zero = sem("d_zero")
        d_qzd = sem("d_qzd")
        d_pj = sem("d_pj")
        d_kev = sem("d_kev")
        d_vev = sem("d_vev")
        d_s = sem("d_s")
        d_mx = sem("d_mx")
        d_nb = sem("d_nb")
        d_exp = sem("d_exp")
        d_t = sem("d_t")
        d_pte = sem("d_pte")
        d_pto = sem("d_pto")
        d_pv = sem("d_pv")
        d_sum = sem("d_sum")
        d_rxd = sem("d_rxd")
        d_rt = sem("d_rt")
        d_o = sem("d_o")

        ew_landed = [sem(f"e_w{i}_landed") for i in range(4)]
        eb_landed = sem("e_b_landed")
        e_pj = sem("e_pj")
        e_eva = sem("e_eva")
        e_evd = sem("e_evd")
        e_s = sem("e_s")
        e_m = sem("e_m")
        e_mx = sem("e_mx")
        e_exp = sem("e_exp")
        e_vs = sem("e_vs")
        e_z = sem("e_z")
        e_zev = sem("e_zev")
        e_zevd = sem("e_zevd")

        fw_landed = [sem(f"f_w{i}_landed") for i in range(2)]
        fb_landed = sem("f_b_landed")
        f_abs = sem("f_abs")
        f_tot = sem("f_tot")
        f_wq = sem("f_wq")
        f_ybd = sem("f_ybd")
        f_yt_t = sem("f_yt_t")
        f_ytd = sem("f_ytd")
        f_m1 = sem("f_m1")
        f_hd = sem("f_hd")
        f_gel = sem("f_gel")
        f_hsq = sem("f_hsq")
        f_hbd = sem("f_hbd")
        f_t = sem("f_t")
        f_htd = sem("f_htd")
        f_m2 = sem("f_m2")

        block = ctx.enter_context(nc.Block())

        @block.sync
        def _(sp):
            sp.dma_start(X[:, :, :], a["x"].rearrange("b p d -> p b d")).then_inc(x_landed, 16)
            sp.dma_start(a_wa, a["w1t"]).then_inc(aw_landed[0], 16)
            sp.dma_start(bcol[:, :], a["bcols"]).then_inc(ab_landed, 16)
            sp.dma_start(a_wb, a["w2n"]).then_inc(aw_landed[1], 16)
            for b in range(NB):
                for c in range(NCH):
                    if b:
                        sp.wait_ge(a_s, 4 * (b - 1) + c + 1)
                    sp.dma_start(a_ct[c], a["ctx_t"][NCH * b + c]).then_inc(act_landed[c], 16)
                if b == 0:
                    sp.wait_ge(a_q, 4)
                    sp.dma_start(a_wa, a["w3t"]).then_inc(aw_landed[2], 16)
                for c in range(NCH):
                    if b:
                        sp.wait_ge(a_pv, 4 * (b - 1) + c + 1)
                    sp.dma_start(a_cn[c], a["ctx_n"][NCH * b + c]).then_inc(acn_landed[c], 16)
            if stages >= 2:
                for i in range(4):
                    sp.wait_ge(a_s, 4 * (NB - 1) + i + 1)
                    sp.dma_start(b_w[i], a["l0a_w"][i]).then_inc(bw_landed[i], 16)
                sp.wait_ge(a_s, 16)
                for i, name in enumerate(("l0a_bq", "l0a_bk", "l0a_bv", "l0a_bo")):
                    sp.dma_start(BI[:, D * i:D * (i + 1)], a[name].partition_broadcast(P)).then_inc(bb_landed, 16)
                sp.dma_start(sm[:, 64:80], a["beta"].partition_broadcast(P)).then_inc(bb_landed, 16)
            if stages >= 3:
                sp.wait_ge(b_p, 12)
                for u in range(NST):
                    sp.dma_start(c_st[u], a["moe_w"][u]).then_inc(c_landed[u], 16)
                sp.wait_ge(proj_done, 8)
                sp.dma_start(c_wg, a["wgt"]).then_inc(cg_landed, 16)
                with sp.Fori(1, NE * UE // NST) as q:
                    for j in range(NST):
                        sp.wait_ge(c_lo3, q * NST + (j - NST + 1))
                        sp.dma_start(c_st[j].unsqueeze(1), a["moe_w"][bass.ds(q * NST + j, 1)].rearrange(
                            "u p a n -> p u a n")).then_inc(c_landed[j], 16)
            if stages >= 4:
                sp.wait_ge(c_lo3, NE * UE)
                sp.wait_ge(c_acc, NE + AHEAD)
                for i in range(2):
                    sp.dma_start(d_ws[i], a["l1x_w"][1 + i]).then_inc(dw_landed[1 + i], 16)
                sp.dma_start(d_wq, a["l1x_w"][0]).then_inc(dw_landed[0], 16)
                for j in range(2):
                    sp.dma_start(d_st[j], a["ctx_t"][j]).then_inc(d_landed[j], 16)
                with sp.Fori(1, NB * NCH // 2) as q:
                    for j in range(2):
                        sp.wait_ge(d_lo, q * 2 + (j - 1))
                        sp.dma_start(d_st[j].unsqueeze(1), a["ctx_t"][bass.ds(q * 2 + j, 1)].rearrange(
                            "u p a n -> p u a n")).then_inc(d_landed[j], 16)
                sp.wait_ge(d_s, 4 * H0 * NB + AHEAD)
                sp.dma_start(d_wo, a["l1x_w"][3]).then_inc(dw_landed[3], 16)
            if stages >= 5:
                sp.wait_ge(d_lo, NB * NCH)
                sp.dma_start(e_w[0], a["l1a_w"][0]).then_inc(ew_landed[0], 16)
                sp.wait_ge(proj_done, 12)
                for i in range(1, 3):
                    sp.dma_start(e_w[i], a["l1a_w"][i]).then_inc(ew_landed[i], 16)
                sp.dma_start(BI[:, 0:DQ], a["l1a_bv"].partition_broadcast(P)).then_inc(eb_landed, 16)
                sp.dma_start(BI[:, DQ:DQ + D], a["l1a_bo"].partition_broadcast(P)).then_inc(eb_landed, 16)
                sp.wait_ge(e_pj, 8)
                sp.dma_start(e_wo, a["l1a_wo"]).then_inc(ew_landed[3], 16)
            if stages >= 6:
                sp.wait_ge(proj_done, 16)
                sp.dma_start(f_w1, a["w1t_f"]).then_inc(fw_landed[0], 16)
                sp.dma_start(f_w2, a["w2t_f"]).then_inc(fw_landed[1], 16)
                sp.wait_ge(x_added, 16)
                sp.dma_start(BI[:, :], a["l1f_b1"].partition_broadcast(P)).then_inc(fb_landed, 16)
                sp.dma_start(d_rx[:, :], a["l1f_b2"].partition_broadcast(P)).then_inc(fb_landed, 16)
            sp.wait_ge(x_added, 4 * stages if stages < 3 else 4 * (stages - 1))
            if stages == 3:
                sp.wait_ge(c_acc, NE + AHEAD)
            sp.dma_start(out.rearrange("b p d -> p b d"), X[:, :, :]).then_inc(out_stored, 16)
            sp.wait_ge(out_stored, 16)

        @block.gpsimd
        def _(pool):
            pool.memset(ident[:, :], 0.0).then_inc(const_step, 1)
            pool.memset(caus[:, :], 0.0).then_inc(const_step, 1)
            pool.memset(ones[:, :], 1.0).then_inc(const_ready, 1)
            for e in range(NE):
                pool.memset(rev8[:, e:e + 1], float(NE - e)).then_inc(const_ready, 1)
            pool.wait_ge(const_step, 2)
            pool.affine_select(out=ident[:, :], in_=ident[:, :], compare_op=ALU.not_equal, fill=1.0, base=0,
                               pattern=[[-1, P]], channel_multiplier=1).then_inc(const_step, 1)
            pool.affine_select(out=caus[:, :], in_=caus[:, :], compare_op=ALU.is_ge, fill=NEG, base=0,
                               pattern=[[1, P]], channel_multiplier=-1).then_inc(const_ready, 1)
            pool.wait_ge(const_step, 3)
            pool.tensor_copy(identb[:, :], ident[:, :]).then_inc(const_ready, 1)
            if stages >= 4:
                pool.wait_ge(c_acc, NE + AHEAD)
                pool.memset(fa(96, 8), 0.0).then_inc(d_zero, 1)
                pool.wait_ge(d_zero, 1)
                pool.wait_ge(d_qev, 4)
                with pool.Fori(0, NB) as b:
                    pool.wait_ge(d_s, b * (4 * H0) + AHEAD)
                    for j in range(4):
                        dst = d_qz.rearrange("p (g j) n -> p g j n", j=4)[32 * j:32 * j + 32, :, j, :]
                        pool.tensor_copy(dst, Y[32 * j:32 * j + 32, :, bass.ds(b * P, P)]).then_inc(d_qzd, 1)

        N_CONST = 1 + NE + 2

        @block.tensor
        def _(pe):
            for signal in (c_h, c_y, d_s):
                pe.sem_inc(signal, AHEAD)
            def turn_tokens(n):
                for t in range(NB):
                    pe.wait_ge(ln_done, NB * n + t + 1)
                    for c in range(KC):
                        last = pe.transpose(bank(c)[:, P * t:P * (t + 1)], Y[:, t, P * c:P * (c + 1)], ident[:, :])
                last.then_inc(ln_turned, 1)

            def wait_xt(n):
                pe.wait_ge(xt_act, 2 * n + 2)
                pe.wait_ge(xt_dve, 2 * n + 2)

            def gemm(dst, lhs, rhs, k):
                for i in range(k):
                    last = pe.matmul(dst, lhs(i), rhs(i), start=(i == 0), stop=(i == k - 1))
                return last

            def three(dst, k, lh, ll, rh, rl):
                for i in range(k):
                    pe.matmul(dst, lh(i), rh(i), start=(i == 0), stop=False)
                    pe.matmul(dst, lh(i), rl(i), start=False, stop=False)
                    last = pe.matmul(dst, ll(i), rh(i), start=False, stop=(i == k - 1))
                return last

            def turn_out(src, n):
                for t in range(NB):
                    for c in range(KC):
                        last = pe.transpose(bank(c)[:, P * t:P * (t + 1)], src[:, t, P * c:P * (c + 1)], ident[:, :])
                last.then_inc(o_turned, 1)

            def project_out(w, k, src=XT, first=4):
                for t in range(NB):
                    gemm(bank(first + t), lambda i: src[:, i, P * t:P * (t + 1)], lambda i: w[:, i, :], k) \
                        .then_inc(proj_done, 1)

            pe.wait_ge(const_ready, N_CONST)
            turn_tokens(0)
            pe.wait_ge(aw_landed[0], 16)
            wait_xt(0)
            for oc in range(KC):
                gemm(bank(4 + oc), lambda i: a_wa[:, i, P * oc:P * (oc + 1)], lambda i: XT[:, i, :], KC).then_inc(a_q, 1)
            pe.wait_ge(a_qev, 4)
            pe.wait_ge(aw_landed[1], 16)
            for oc in range(KC):
                gemm(bank(oc), lambda i: a_wb[:, i, P * oc:P * (oc + 1)], lambda i: a_qt[:, i, :], KC).then_inc(a_qpd, 1)
            for t in range(NB):
                last = gemm(bank(4)[:, t:t + 1], lambda i: a_qt[:, i, P * t:P * (t + 1)],
                            lambda i: b2c[:, i:i + 1], KC)
            last.then_inc(a_qb, 1)
            pe.wait_ge(a_qpe_act, 2)
            pe.wait_ge(a_qpe_dve, 3)

            def a_scores(b):
                for c in range(NCH):
                    pe.wait_ge(act_landed[c], 16 * (b + 1))
                    if b:
                        pe.wait_ge(a_exp, 2 * (b - 1) + 1 + c // 2)
                    gemm(bank(c), lambda i: a_qp[:, i, P * b:P * (b + 1)], lambda i: a_ct[c][:, i, :], KC).then_inc(a_s, 1)

            def a_turn(b):
                for g in range(4):
                    pe.wait_ge(a_exp, 2 * b + 1 + g // 2)
                    if 2 * b + g // 2 > 0:
                        pe.wait_ge(a_pto if g % 2 else a_pte, 2 * b + g // 2)
                    for j in range(4):
                        last = pe.transpose(bank(5 + g % 2)[:, P * j:P * (j + 1)],
                                            a_p[:, CH * g + P * j:CH * g + P * (j + 1)], ident[:, :])
                    last.then_inc(a_t, 1)

            def a_mix(b):
                if b:
                    pe.wait_ge(a_o, b)
                for g in range(4):
                    pe.wait_ge(a_pto if g % 2 else a_pte, 2 * b + g // 2 + 1)
                    pe.wait_ge(acn_landed[g], 16 * (b + 1))
                    for j in range(4):
                        last = pe.matmul(bank(4), a_pt[:, 4 * g + j, :], a_cn[g][:, j, :],
                                         start=(g == 0 and j == 0), stop=(g == 3 and j == 3))
                    last.then_inc(a_pv, 1)

            a_scores(0)
            a_turn(0)
            for b in range(1, NB):
                a_scores(b)
                a_mix(b - 1)
                a_turn(b)
            a_mix(NB - 1)
            pe.wait_ge(a_o, NB)
            turn_out(a_ao, 0)
            pe.wait_ge(o_act, 2)
            pe.wait_ge(o_dve, 2)
            pe.wait_ge(aw_landed[2], 16)
            project_out(a_wa, KC)

            if stages >= 2:
                turn_tokens(1)
                wait_xt(1)
                for m in range(3):
                    pe.wait_ge(bw_landed[m], 16)
                    for t in range(NB):
                        n = 4 * m + t
                        if m == 1:
                            pe.wait_ge(x_added, t + 1)
                        if m == 2:
                            pe.wait_ge(b_zq, t + 1)
                        gemm(bank(n % 8), lambda i: XT[:, i, P * t:P * (t + 1)], lambda i: b_w[m][:, i, :], KC) \
                            .then_inc(b_p, 1)
                pe.wait_ge(b_o, NB)
                turn_out(b_ao, 1)
                pe.wait_ge(o_act, 4)
                pe.wait_ge(o_dve, 4)
                pe.wait_ge(bw_landed[3], 16)
                project_out(b_w[3], KC)

            if stages >= 3:
                turn_tokens(2)
                wait_xt(2)
                pe.wait_ge(cg_landed, 16)
                for t in range(NB):
                    last = gemm(bank(7)[:, NE * t:NE * (t + 1)], lambda i: XT[:, i, P * t:P * (t + 1)],
                                lambda i: c_wg[:, i, :], KC)
                last.then_inc(c_gate, 1)
                pe.wait_ge(c_xld, 1)

                def c_hidden(before, j):
                    s = j % 2
                    pe.wait_ge(c_lo12, before + (j + 1))
                    if j:
                        pe.wait_ge(c_gd, before + (j - 1) + AHEAD)
                    for m in range(2):
                        w = lambda x, i: x[s][:, m, P * i:P * (i + 1)]
                        last = three(bank(2 * s + m), KC, lambda i: w(c_wh, i), lambda i: w(c_wl, i),
                                     lambda i: c_xh[:, i, :], lambda i: c_xl[:, i, :])
                    last.then_inc(c_h, 1)

                def c_out(u, j):
                    s = j % 2
                    pe.wait_ge(c_gld, u + 1)
                    pe.wait_ge(c_lo3, u + 1)
                    for t in range(NB):
                        tk = slice(P * t, P * (t + 1))
                        pe.matmul(bank(4 + t), c_gh[s][:, tk], c_wh[s][:, 2, :], start=(j == 0), stop=False)
                        pe.matmul(bank(4 + t), c_gh[s][:, tk], c_wl[s][:, 2, :], start=False, stop=False)
                        last = pe.matmul(bank(4 + t), c_gl[s][:, tk], c_wh[s][:, 2, :], start=False, stop=(j == UE - 1))
                    last.then_inc(c_y, 1)

                def c_expert(e, final):
                    for j in range(UE):
                        if not (final and j == UE - 1):
                            c_hidden(e * UE, j + 1)
                        if j == 0:
                            pe.wait_ge(c_acc, e + AHEAD)
                        c_out(e * UE + j, j)

                c_hidden(0, 0)
                pe.wait_ge(c_e, 1)
                with pe.Fori(0, NE - 1) as e:
                    c_expert(e, False)
                c_expert(NE - 1, True)

            if stages >= 4:
                turn_tokens(3)
                wait_xt(3)
                pe.wait_ge(dw_landed[0], 16)
                for oc in range(KC):
                    gemm(bank(4 + oc), lambda i: d_wq[:, i, P * oc:P * (oc + 1)], lambda i: XT[:, i, :], KC) \
                        .then_inc(d_q, 1)
                pe.wait_ge(d_wld, 2)

                def d_project(b, first):
                    for c in range(NCH):
                        s = c % 2
                        pe.wait_ge(d_lo, b * NCH + (c + 1))
                        for j in range(4):
                            for m in range(2):
                                n = 8 * c + 2 * j + m
                                if n >= 4:
                                    pe.wait_ge(d_vev if m else d_kev, b * 16 + (n // 2 - 1))
                                elif n == 0:
                                    pe.wait_ge(d_exp, b * (4 * H0) + AHEAD)
                                dst = bank(n % 4)
                                if m == 0:
                                    w = lambda x, i: x[0][:, i, P * j:P * (j + 1)]
                                    last = three(dst, KC, lambda i: w(d_wh, i), lambda i: w(d_wl, i),
                                                 lambda i: d_ch[s][:, i, :], lambda i: d_cl[s][:, i, :])
                                else:
                                    k = slice(P * j, P * (j + 1))
                                    last = three(dst, KC, lambda i: d_ch[s][:, i, k], lambda i: d_cl[s][:, i, k],
                                                 lambda i: d_wh[1][:, i, :], lambda i: d_wl[1][:, i, :])
                                last.then_inc(d_pj, 1)

                def score(b, h, c):
                    if h:
                        pe.wait_ge(d_exp, b * (4 * H0) + (4 * (h - 1) + c + 1) + AHEAD)
                    pe.matmul(bank(c), d_qz[:, h, :], d_kt[:, h // 4, CH * c:CH * (c + 1)],
                              start=True, stop=True).then_inc(d_s, 1)

                def turn(b, h, g):
                    pe.wait_ge(d_exp, b * (4 * H0) + (4 * h + g + 1) + AHEAD)
                    if g == 3:
                        pe.wait_ge(d_pte, b * (2 * H0) + (2 * h + 1) + AHEAD)
                    else:
                        pe.wait_ge((d_pto, d_pto, d_pte)[g], b * (2 * H0) + 2 * h + AHEAD)
                    for j in range(4):
                        last = pe.transpose(bank(TB[g])[:, P * j:P * (j + 1)],
                                            d_p[h % 2][:, CH * g + P * j:CH * g + P * (j + 1)], ident[:, :])
                    last.then_inc(d_t, 1)

                def mix(b, h, g):
                    r, q = 32 * (h % 4), P * (h // 4)
                    pe.wait_ge(d_pto if g % 2 else d_pte, b * (2 * H0) + (2 * h + g // 2 + 1) + AHEAD)
                    for j in range(4):
                        last = pe.matmul(bank(6)[r:r + 32, q:q + P], d_v[:, 4 * g + j, DH0 * h:DH0 * (h + 1)],
                                         d_pt[:, 4 * g + j, :], start=(g == 0 and j == 0),
                                         stop=(g == 3 and j == 3))
                    if g == 3:
                        last.then_inc(d_pv, 1)

                def turn_and_mix(b, h):
                    turn(b, h, 0)
                    turn(b, h, 1)
                    turn(b, h, 2)
                    mix(b, h, 0)
                    turn(b, h, 3)
                    mix(b, h, 1)
                    mix(b, h, 2)

                with pe.Fori(0, NB) as b:
                    d_project(b, False)
                    pe.wait_ge(d_kev, b * 16 + 16)
                    pe.wait_ge(d_vev, b * 16 + 16)
                    pe.wait_ge(d_qzd, b * 4 + 4)
                    for h in range(H0):
                        for c in range(NCH):
                            score(b, h, c)
                            if c == 0 and h >= 2:
                                mix(b, h - 2, 3)
                        if h == 1:
                            pe.wait_ge(d_o, b + AHEAD)
                        if h:
                            turn_and_mix(b, h - 1)
                    mix(b, H0 - 2, 3)
                    turn_and_mix(b, H0 - 1)
                    mix(b, H0 - 1, 3)
                    pe.wait_ge(d_rxd, b + 1)
                    for g in range(KC):
                        last = pe.transpose(bank(7)[:, P * g:P * (g + 1)], d_rx[:, P * g:P * (g + 1)], ident[:, :])
                    last.then_inc(d_rt, 1)
                pe.wait_ge(d_o, NB + AHEAD)
                pe.wait_ge(dw_landed[3], 16)
                project_out(d_wo, KC, first=0)

            if stages >= 5:
                pe.wait_ge(x_added, 12)
                turn_tokens(4)
                wait_xt(4)
                for m in range(2):
                    pe.wait_ge(ew_landed[m], 16)
                    for oc in range(8):
                        n = 8 * m + oc
                        if m:
                            pe.wait_ge(e_evd if oc % 2 else e_eva, oc // 2 + 1)
                        gemm(bank((4 + n) % 8), lambda i: e_w[m][:, i, P * oc:P * (oc + 1)],
                             lambda i: XT[:, i, :], KC).then_inc(e_pj, 1)
                pe.wait_ge(ew_landed[2], 16)
                for t in range(NB):
                    for f in range(2):
                        n = 2 * t + f
                        pe.wait_ge(e_evd if n % 2 else e_eva, 4 + n // 2 + 1)
                        gemm(bank((4 + n) % 8), lambda i: XT[:, i, P * t:P * (t + 1)],
                             lambda i: e_w[2][:, i, D * f:D * (f + 1)], KC).then_inc(e_pj, 1)
                pe.wait_ge(e_eva, 8)
                pe.wait_ge(e_evd, 8)
                for g in range(16):
                    if g < 8:
                        pe.wait_ge(e_evd, 8 + g + 1)
                    else:
                        pe.wait_ge(e_m, g - 8 + 1)
                    for j in range(4):
                        b, h = g // 4, e_head(g % 4, j)
                        r = slice(64 * (h % 2), 64 * (h % 2) + 64)
                        tk = slice(P * b, P * (b + 1))
                        last = pe.matmul(bank((4 + g) % 8)[:, P * j:P * (j + 1)], e_kt[r, h // 2, tk],
                                         e_qt[r, h // 2, tk], start=True, stop=True)
                    last.then_inc(e_s, 1)
                pe.wait_ge(e_m, 16)
                for b in range(NB):
                    pe.wait_ge(e_vs, b + 1)
                    for h in range(H1):
                        r = 64 * (h % 2)
                        last = pe.matmul(bank(h // 2)[r:r + 64, P * b:P * (b + 1)], e_v[:, b, DH1 * h:DH1 * (h + 1)],
                                         e_e[:, H1 * b + e_place(h), :], start=True, stop=True)
                last.then_inc(e_z, 1)
                pe.wait_ge(e_zev, 4)
                pe.wait_ge(e_zevd, 4)
                pe.wait_ge(ew_landed[3], 16)
                project_out(e_wo, 8, src=e_zt, first=4)

            if stages >= 6:
                for i in range(2):
                    pe.wait_ge(f_abs, i + 1)
                    pe.matmul(bank(0)[:, i:i + 1], ones[:, :], sm[:, 200 + i:201 + i], start=True, stop=True) \
                        .then_inc(f_tot, 1)
                pe.wait_ge(f_ybd, 1)
                pe.wait_ge(f_wq, 1)
                yt_ps = [bank(4 + i).bitcast(BF16) for i in range(2)]
                for c in range(KC):
                    for t in range(NB):
                        last = pe.transpose(yt_ps[c // 2][:, 512 * (c % 2) + P * t:512 * (c % 2) + P * (t + 1)],
                                            f_yb[:, t, P * c:P * (c + 1)], identb[:, :])
                last.then_inc(f_yt_t, 1)
                pe.wait_ge(f_ytd, 1)

                def f_up(t):
                    if t >= 2:
                        pe.wait_ge(x_added, 16 + t - 1)
                    for f in range(4):
                        last = gemm(bank(4 * (t % 2) + f), lambda i: f_yt[:, i, P * t:P * (t + 1)],
                                    lambda i: f_w1b[:, i, 512 * f:512 * (f + 1)], KC)
                    last.then_inc(f_m1, 1)

                def f_down(t):
                    o = 4 * (t % 2)
                    pe.wait_ge(f_hbd, t + 1)
                    tp = [bank(o + i).bitcast(BF16) for i in range(2)]
                    for j in range(FC):
                        last = pe.transpose(tp[j // 8][:, P * (j % 8):P * (j % 8 + 1)],
                                            f_hb[t % 2][:, P * j:P * (j + 1)], identb[:, :])
                    last.then_inc(f_t, 1)
                    pe.wait_ge(f_htd, t + 1)
                    gemm(bank(o + 2), lambda i: f_ht[t % 2][:, i, :], lambda i: f_w2b[:, i, :], FC).then_inc(f_m2, 1)

                f_up(0)
                f_up(1)
                f_down(0)
                f_up(2)
                f_down(1)
                f_up(3)
                f_down(2)
                f_down(3)

        @block.scalar
        def _(act):
            for signal in (d_exp, d_pte):
                act.sem_inc(signal, AHEAD)
            def copy(dst, src):
                return act.activation(dst, src, ACT.Copy)

            roots = [0]

            def take_root(t=slice(0, NB)):
                roots[0] += 1
                act.wait_ge(root_asked, roots[0])
                act.activation(root[:, t], rstd[:, t], ACT.Sqrt).then_inc(root_done, 1)

            def xt_chunks(n):
                act.wait_ge(ln_turned, n + 1)
                for c in range(2):
                    copy(XT[:, c, :], bank(c)).then_inc(xt_act, 1)

            def out_chunks(n):
                act.wait_ge(o_turned, n + 1)
                for c in range(2):
                    copy(XT[:, c, :], bank(c)).then_inc(o_act, 1)

            take_root()
            xt_chunks(0)
            act.wait_ge(ab_landed, 16)
            for oc in range(KC):
                act.wait_ge(a_q, oc + 1)
                act.activation(a_qt[:, oc, :], bank(4 + oc), ACT.Identity, bias=b1c[:, oc:oc + 1]).then_inc(a_qev, 1)
            for oc in range(2):
                act.wait_ge(a_qpd, oc + 1)
                copy(a_qp[:, oc, :], bank(oc)).then_inc(a_qpe_act, 1)
            for b in range(NB):
                act.wait_ge(a_nb, b + 1)
                if b:
                    act.wait_ge(a_t, 4 * b)
                for f in range(2):
                    act.activation(a_p[:, 1024 * f:1024 * (f + 1)], bank(2 * f, 2), ACT.Exp, bias=sm[:, 8 + b:9 + b],
                                   scale=1.0 / 32, accum_out=sm[:, 16 + 2 * b + f:17 + 2 * b + f]).then_inc(a_exp, 1)
                for g in (0, 2):
                    act.wait_ge(a_t, 4 * b + g + 1)
                    copy(a_pt[:, 4 * g:4 * g + 4, :], v3(bank(5), 4)).then_inc(a_pte, 1)
            out_chunks(0)

            if stages >= 2:
                take_root()
                xt_chunks(1)
                act.wait_ge(bb_landed, 80)
                act.activation(sm[:, 80:96], sm[:, 64:80], ACT.Exp).then_inc(b_beta, 1)
                for m in range(2):
                    hf = slice(2048 * m, 2048 * (m + 1))
                    act.wait_ge(b_zs, m + 1)
                    act.activation(b_s1[:, hf], fa(32 + 8 * m, 8), ACT.Abs).then_inc(b_u, 1)
                    act.wait_ge(b_u, 2 * m + 1)
                    act.activation(b_s1[:, hf], b_s1[:, hf], ACT.Exp, scale=-1.0).then_inc(b_u, 1)
                for m in range(2):
                    hf = slice(2048 * m, 2048 * (m + 1))
                    act.wait_ge(b_w1p, m + 1)
                    act.activation(b_s3[:, hf], b_s2[:, hf], ACT.Ln).then_inc(b_ln, 1)
                out_chunks(1)

            if stages >= 3:
                take_root()
                xt_chunks(2)
                act.wait_ge(xt_act, 6)
                act.wait_ge(xt_dve, 6)
                copy(c_xh, XT[:, :, :]).then_inc(c_xhd, 1)
                act.wait_ge(c_diff, 1)
                act.activation(sm[:, 120:124], sm[:, 116:120], ACT.Exp).then_inc(c_e, 1)

                def c_split12(before, k):
                    act.wait_ge(c_landed[k % NST], before * (16 // NST) + (16 * (k // NST) + 16))
                    if k:
                        act.wait_ge(c_h, before + (k - 1) + AHEAD)
                    copy(c_wh[k % 2][:, 0:2, :], c_st[k % NST][:, 0:2, :]).then_inc(c_hi12, 1)

                def c_expert(e, final):
                    for j in range(UE):
                        if not (final and j == UE - 1):
                            c_split12(e * UE, j + 1)
                        act.wait_ge(c_y, e * UE + max(j - 1, 0) + AHEAD)
                        copy(c_wh[j % 2][:, 2, :], c_st[j % NST][:, 2, :]).then_inc(c_hi3, 1)
                        act.wait_ge(c_h, e * UE + (j + 1) + AHEAD)
                        act.wait_ge(c_t, e * UE + j + AHEAD)
                        act.activation(c_sg, bank(2 * (j % 2)), ACT.Sigmoid).then_inc(c_sig, 1)

                c_split12(0, 0)
                with act.Fori(0, NE - 1) as e:
                    c_expert(e, False)
                c_expert(NE - 1, True)

            if stages >= 4:
                for i in range(2):
                    act.wait_ge(dw_landed[1 + i], 16)
                    act.wait_ge(c_y, NE * UE + AHEAD)
                    copy(d_wh[i], d_ws[i]).then_inc(d_whd, 1)

                def d_split(b, c):
                    act.wait_ge(d_landed[c % 2], b * 32 + (16 * (c // 2) + 16))
                    if isinstance(b, int) and c < 2:
                        pass
                    else:
                        act.wait_ge(d_pj, b * 32 + (8 * (c - 1)))
                    copy(d_ch[c % 2], d_st[c % 2]).then_inc(d_hi, 1)

                d_split(0, 0)
                d_split(0, 1)
                take_root()
                xt_chunks(3)
                for oc in range(KC):
                    act.wait_ge(d_q, oc + 1)
                    copy(Y[:, oc, :], bank(4 + oc)).then_inc(d_qev, 1)

                def d_batch(b, final):
                    for c in range(NCH):
                        for j in range(4):
                            n = 8 * c + 2 * j
                            act.wait_ge(d_pj, b * 32 + (n + 1))
                            copy(d_kt[:, j, CH * c:CH * (c + 1)], bank(n % 4)).then_inc(d_kev, 1)
                        if c < 2:
                            act.wait_ge(d_landed[c], b * 32 + 32)
                            act.wait_ge(d_pj, b * 32 + (8 * (c + 1)))
                            copy(d_ch[c], d_st[c]).then_inc(d_hi, 1)
                    for h in range(H0):
                        if h:
                            evac(b, h - 1, 0)
                        act.wait_ge(d_nb, b * H0 + (h + 1))
                        if h >= 2:
                            act.wait_ge(d_t, b * (4 * H0) + 4 * (h - 1))
                        for c in range(NCH):
                            act.activation(d_p[h % 2][:, CH * c:CH * (c + 1)], bank(c), ACT.Exp,
                                           bias=sm[:, 128 + h % 2:129 + h % 2], scale=float(DH0) ** -0.5,
                                           accum_out=sm[:, 136 + 4 * h + c:137 + 4 * h + c]).then_inc(d_exp, 1)
                            if c == 0 and h:
                                evac(b, h - 1, 2)
                        if not final and h in (5, 10):
                            c = h // 5 - 1
                            act.wait_ge(d_landed[c], b * 32 + 48)
                            act.wait_ge(d_pj, b * 32 + 32)
                            copy(d_ch[c], d_st[c]).then_inc(d_hi, 1)
                    evac(b, H0 - 1, 0)
                    evac(b, H0 - 1, 2)

                def evac(b, h, g):
                    act.wait_ge(d_t, b * (4 * H0) + (4 * h + g + 1))
                    copy(d_pt[:, 4 * g:4 * g + 4, :], v3(bank(TB[g]), 4)).then_inc(d_pte, 1)

                with act.Fori(0, NB - 1) as b:
                    d_batch(b, False)
                d_batch(NB - 1, True)

            if stages >= 5:
                take_root()
                take_root()
                xt_chunks(4)
                for m in range(2):
                    for oc in range(0, 8, 2):
                        n = 8 * m + oc
                        act.wait_ge(e_pj, n + 1)
                        act.activation((e_qt, e_kt)[m][:, oc, :], bank((4 + n) % 8), ACT.Identity,
                                       bias=(bqc, bkc)[m][:, oc:oc + 1]).then_inc(e_eva, 1)
                for i in range(64):
                    act.wait_ge(e_mx, i // 4 + 1)
                    act.activation(e_e[:, i, :], e_e[:, i, :], ACT.Exp, bias=e_nm[:, i:i + 1],
                                   accum_out=e_rs[:, i:i + 1]).then_inc(e_exp, 1)
                act.wait_ge(e_z, 1)
                for i in range(0, 8, 2):
                    copy(e_zt[:, i, :], bank(i)).then_inc(e_zev, 1)

            if stages >= 6:
                take_root()
                take_root()
                for t in range(NB):
                    act.wait_ge(f_hd, t + 1)
                    act.activation(f_h[t % 2], f_h[t % 2], ACT.Gelu).then_inc(f_gel, 1)
                    act.wait_ge(f_gel, t + 1)
                    act.activation(f_sq, f_h[t % 2], ACT.Square, accum_out=sm[:, 216 + t:217 + t]).then_inc(f_hsq, 1)
                    take_root(slice(t, t + 1))

        @block.vector
        def _(v):
            for signal in (c_t, c_gd, c_acc, d_pto, d_o):
                v.sem_inc(signal, AHEAD)
            count = [0]

            def link(ins):
                count[0] += 1
                ins.then_inc(dve, 1)
                v.wait_ge(dve, count[0])

            roots = [0]

            def inverse_root(ins, t=slice(0, NB)):
                roots[0] += 1
                ins.then_inc(root_asked, 1)
                v.wait_ge(root_done, roots[0])
                x, y, z = rstd[:, t], root[:, t], rtmp[:, t]
                link(v.reciprocal(y, y))
                link(v.tensor_tensor(z, y, y, ALU.mult))
                link(v.tensor_tensor(z, z, x, ALU.mult))
                link(v.tensor_scalar(z, z, -0.5, 1.5, ALU.mult, ALU.add))
                link(v.tensor_tensor(x, y, z, ALU.mult))

            def layernorm(n, rms=None):
                for t in range(NB):
                    last = v.bn_stats(st[:, t, :], X[:, t, :])
                link(last)
                for t in range(NB):
                    last = v.bn_aggr(mv[:, t, :], st[:, t, :])
                link(last)
                inverse_root(v.tensor_scalar(rstd[:, :], mv[:, :, 1], 1e-5, None, ALU.add))
                for t in range(NB):
                    last = v.tensor_scalar(Y[:, t, :], X[:, t, :], mv[:, t, 0:1], rstd[:, t:t + 1],
                                           ALU.subtract, ALU.mult)
                    if rms is None:
                        last.then_inc(ln_done, 1)
                if rms is None:
                    return
                link(last)
                for t in range(NB):
                    last = v.bn_stats(st[:, t, :], Y[:, t, :])
                link(last)
                for t in range(NB):
                    last = v.bn_aggr(mv[:, t, :], st[:, t, :])
                link(last)
                link(v.tensor_tensor(rstd[:, :], mv[:, :, 0], mv[:, :, 0], ALU.mult))
                inverse_root(v.scalar_tensor_tensor(rstd[:, :], rstd[:, :], rms, mv[:, :, 1], ALU.add, ALU.add))
                for t in range(NB):
                    v.tensor_scalar(Y[:, t, :], Y[:, t, :], rstd[:, t:t + 1], None, ALU.mult).then_inc(ln_done, 1)

            def xt_chunks(n):
                v.wait_ge(ln_turned, n + 1)
                for c in range(2, 4):
                    v.tensor_copy(XT[:, c, :], bank(c)).then_inc(xt_dve, 1)

            def out_chunks(n):
                v.wait_ge(o_turned, n + 1)
                for c in range(2, 4):
                    v.tensor_copy(XT[:, c, :], bank(c)).then_inc(o_dve, 1)

            def add_projection(n, first=4):
                for t in range(NB):
                    v.wait_ge(proj_done, NB * n + t + 1)
                    v.tensor_tensor(X[:, t, :], X[:, t, :], bank(first + t), ALU.add).then_inc(x_added, 1)
                v.wait_ge(x_added, NB * (n + 1))

            v.wait_ge(x_landed, 16)
            layernorm(0)
            xt_chunks(0)
            for oc in range(2, 4):
                v.wait_ge(a_qpd, oc + 1)
                v.tensor_copy(a_qp[:, oc, :], bank(oc)).then_inc(a_qpe_dve, 1)
            v.wait_ge(a_qb, 1)
            v.tensor_copy(sm[:, 0:4], bank(4)[:, 0:4]).then_inc(a_qpe_dve, 1)
            v.wait_ge(a_qpe_dve, 3)

            def a_take(b):
                link(v.tensor_tensor(sm[:, 24 + b:25 + b], sm[:, 16 + 2 * b:17 + 2 * b],
                                     sm[:, 17 + 2 * b:18 + 2 * b], ALU.add))
                link(v.reciprocal(sm[:, 28 + b:29 + b], sm[:, 24 + b:25 + b]))
                v.wait_ge(a_pv, 4 * (b + 1))
                v.tensor_scalar(a_ao[:, b, :], bank(4), sm[:, 28 + b:29 + b], None, ALU.mult).then_inc(a_o, 1)

            for b in range(NB):
                for f in range(2):
                    v.wait_ge(a_s, 4 * b + 2 * f + 2)
                    last = v.tensor_reduce(sm[:, 32 + 2 * b + f:33 + 2 * b + f], bank(2 * f, 2), AX, ALU.max)
                link(last)
                link(v.tensor_scalar(sm[:, 40 + b:41 + b], sm[:, 32 + 2 * b:33 + 2 * b], sm[:, 33 + 2 * b:34 + 2 * b],
                                     sm[:, b:b + 1], ALU.max, ALU.add))
                v.tensor_scalar(sm[:, 8 + b:9 + b], sm[:, 40 + b:41 + b], sm[:, b:b + 1], -1.0 / 32,
                                ALU.subtract, ALU.mult).then_inc(a_nb, 1)
                if b:
                    a_take(b - 1)
                for g in (1, 3):
                    v.wait_ge(a_t, 4 * b + g + 1)
                    v.tensor_copy(a_pt[:, 4 * g:4 * g + 4, :], v3(bank(6), 4)).then_inc(a_pto, 1)
                v.wait_ge(a_exp, 2 * b + 2)
            a_take(NB - 1)
            out_chunks(0)
            add_projection(0)

            if stages >= 2:
                layernorm(1)
                xt_chunks(1)
                v.wait_ge(bb_landed, 80)
                v.wait_ge(b_beta, 1)
                link(v.tensor_scalar(sm[:, 96:112], sm[:, 80:96], float(DH0) ** 0.5, None, ALU.mult))
                link(v.reciprocal(sm[:, 80:96], sm[:, 96:112]))
                for t in range(NB):
                    last = v.tensor_tensor(X[:, t, :], X[:, t, :], BI[:, 3 * D:4 * D], ALU.add)
                link(last)
                for m in range(2):
                    for t in range(NB):
                        n = 4 * m + t
                        v.wait_ge(b_p, n + 1)
                        v.tensor_tensor(b_z[:, n, :], bank(n), BI[:, D * m:D * (m + 1)], ALU.add).then_inc(b_zq, 1)
                    v.wait_ge(b_zq, 4 * (m + 1))
                    z4 = b_z[:, 4 * m:4 * m + 4, :].rearrange("p a (h d) -> p a h d", h=H0)
                    sc = sm[:, 80:96].unsqueeze(1).unsqueeze(3).broadcast_to([P, 4, H0, DH0])
                    v.tensor_tensor(z4, z4, sc, ALU.mult).then_inc(b_zs, 1)
                for t in range(NB):
                    v.wait_ge(b_p, 8 + t + 1)
                    v.tensor_tensor(b_v[:, t, :], bank(t), BI[:, 2 * D:3 * D], ALU.add).then_inc(b_zq, 1)
                for m in range(2):
                    hf = slice(2048 * m, 2048 * (m + 1))
                    v.wait_ge(b_u, 2 * m + 2)
                    v.tensor_scalar(b_s2[:, hf], b_s1[:, hf], 1.0, None, ALU.add).then_inc(b_w1p, 1)
                for m in range(2):
                    hf = slice(2048 * m, 2048 * (m + 1))
                    v.wait_ge(b_ln, m + 1)
                    link(v.scalar_tensor_tensor(b_s2[:, hf], b_s2[:, hf], -1.0, b_s1[:, hf], ALU.add, ALU.subtract))
                    link(v.tensor_tensor(b_s3[:, hf], b_s3[:, hf], b_s2[:, hf], ALU.subtract))
                    zf = fa(32 + 8 * m, 8)
                    link(v.scalar_tensor_tensor(zf, zf, 0.0, b_s3[:, hf], ALU.max, ALU.add))
                v.wait_ge(b_zq, 12)
                pr = v3(b_s1[:, 0:2048], 4)
                att = b_s2[:, 0:256].rearrange("p (s t h) -> p s t h", s=4, t=4)
                den = b_s2[:, 256:320].rearrange("p (s h) -> p s h", s=4)
                rden = b_s2[:, 320:384].rearrange("p (s h) -> p s h", s=4)
                for s in range(NB):
                    n = s + 1
                    link(v.tensor_tensor(pr[:, 0:n, :], b_z[:, s:s + 1, :].broadcast_to([P, n, D]), b_z[:, 4:4 + n, :],
                                         ALU.mult))
                    link(v.tensor_reduce(att[:, s, 0:n, :], pr[:, 0:n, :].rearrange("p a (h d) -> p a h d", h=H0),
                                         AX, ALU.add))
                    link(v.tensor_reduce(den[:, s, :], att[:, s, 0:n, :].rearrange("p t h -> p h t"), AX, ALU.add))
                    link(v.reciprocal(rden[:, s, :], den[:, s, :]))
                    link(v.tensor_tensor(pr[:, 0:n, :].rearrange("p a (h d) -> p a h d", h=H0),
                                         att[:, s, 0:n, :].unsqueeze(3).broadcast_to([P, n, H0, DH0]),
                                         b_v[:, 0:n, :].rearrange("p a (h d) -> p a h d", h=H0), ALU.mult))
                    link(v.tensor_reduce(b_ao[:, s, :], pr[:, 0:n, :].rearrange("p t n -> p n t"), AX, ALU.add))
                    o3 = b_ao[:, s, :].rearrange("p (h d) -> p h d", h=H0)
                    v.tensor_tensor(o3, o3, rden[:, s, :].unsqueeze(2).broadcast_to([P, H0, DH0]), ALU.mult) \
                        .then_inc(b_o, 1)
                out_chunks(1)
                add_projection(1)

            if stages >= 3:
                layernorm(2)
                xt_chunks(2)
                v.wait_ge(xt_dve, 6)
                v.wait_ge(xt_act, 6)
                v.wait_ge(c_xhd, 1)
                v.tensor_tensor(c_xl, XT[:, :, :], c_xh.bitcast(F32), ALU.subtract).then_inc(c_xld, 1)
                v.wait_ge(c_gate, 1)
                v.wait_ge(const_ready, N_CONST)
                gt = g_[:, 0:32].rearrange("p (t e) -> p t e", t=NB)
                oh = [g_[:, 32 * (i + 1):32 * (i + 2)].rearrange("p (t e) -> p t e", t=NB) for i in range(2)]
                g2 = g_[:, 96:128].rearrange("p (t e) -> p t e", t=NB)
                wt = g_[:, 128:160].rearrange("p (t e) -> p t e", t=NB)
                m12 = [sm[:, 100:104], sm[:, 104:108]]
                mxi = sm[:, 108:112]

                def over_e(ap):
                    return ap.unsqueeze(2).broadcast_to([P, NB, NE])

                rv = rev8[:, :].unsqueeze(1).broadcast_to([P, NB, NE])
                link(v.tensor_copy(gt, bank(7)[:, 0:NB * NE].rearrange("p (t e) -> p t e", t=NB)))
                src = gt
                for i in range(2):
                    link(v.tensor_reduce(m12[i], src, AX, ALU.max))
                    link(v.tensor_tensor(oh[i], src, over_e(m12[i]), ALU.is_equal))
                    link(v.tensor_tensor(oh[i], oh[i], rv, ALU.mult))
                    link(v.tensor_reduce(mxi, oh[i], AX, ALU.max))
                    link(v.tensor_tensor(oh[i], oh[i], over_e(mxi), ALU.is_equal))
                    if i == 0:
                        link(v.scalar_tensor_tensor(g2, oh[0], NEG, gt, ALU.mult, ALU.add))
                        src = g2
                v.tensor_tensor(sm[:, 116:120], m12[1], m12[0], ALU.subtract).then_inc(c_diff, 1)
                v.wait_ge(c_e, 1)
                link(v.tensor_scalar(sm[:, 112:116], sm[:, 120:124], 1.0, None, ALU.add))
                link(v.reciprocal(sm[:, 100:104], sm[:, 112:116]))
                link(v.tensor_tensor(sm[:, 104:108], sm[:, 100:104], sm[:, 120:124], ALU.mult))
                for i in range(2):
                    link(v.tensor_tensor(oh[i], oh[i], over_e(m12[i]), ALU.mult))
                link(v.tensor_tensor(wt, oh[0], oh[1], ALU.add))

                def c_low12(u, k):
                    v.wait_ge(c_hi12, u + 1)
                    v.tensor_tensor(c_wl[k % 2][:, 0:2, :], c_st[k % NST][:, 0:2, :],
                                    c_wh[k % 2][:, 0:2, :].bitcast(F32), ALU.subtract).then_inc(c_lo12, 1)

                def c_low3(u, k):
                    v.wait_ge(c_hi3, u + 1)
                    v.tensor_tensor(c_wl[k % 2][:, 2, :], c_st[k % NST][:, 2, :],
                                    c_wh[k % 2][:, 2, :].bitcast(F32), ALU.subtract).then_inc(c_lo3, 1)

                def c_expert(e, final):
                    for j in range(UE):
                        u = e * UE + j
                        s = j % 2
                        if not (final and j == UE - 1):
                            c_low12(e * UE + (j + 1), j + 1)
                        c_low3(u, j)
                        v.wait_ge(c_sig, u + 1)
                        v.tensor_tensor(c_tt, c_sg, bank(2 * s), ALU.mult).then_inc(c_t, 1)
                        v.wait_ge(c_t, u + 1 + AHEAD)
                        v.tensor_tensor(c_g, c_tt, bank(2 * s + 1), ALU.mult).then_inc(c_gd, 1)
                        v.wait_ge(c_gd, u + 1 + AHEAD)
                        v.tensor_copy(c_gh[s], c_g).then_inc(c_ghd, 1)
                        v.wait_ge(c_ghd, u + 1)
                        v.tensor_tensor(c_gl[s], c_g, c_gh[s].bitcast(F32), ALU.subtract).then_inc(c_gld, 1)
                    v.wait_ge(c_y, e * UE + UE + AHEAD)
                    for t in range(NB):
                        last = v.scalar_tensor_tensor(X[:, t, :], bank(4 + t), wt[:, t, bass.ds(e, 1)], X[:, t, :],
                                                      ALU.mult, ALU.add)
                    last.then_inc(c_acc, 1)
                    v.wait_ge(c_acc, e + 1 + AHEAD)

                c_low12(0, 0)
                with v.Fori(0, NE - 1) as e:
                    c_expert(e, False)
                c_expert(NE - 1, True)

            if stages >= 4:
                for i in range(2):
                    v.wait_ge(d_whd, i + 1)
                    v.tensor_tensor(d_wl[i], d_ws[i], d_wh[i].bitcast(F32), ALU.subtract).then_inc(d_wld, 1)

                def d_low(n, s):
                    v.wait_ge(d_hi, n + 1)
                    v.tensor_tensor(d_cl[s], d_st[s], d_ch[s].bitcast(F32), ALU.subtract).then_inc(d_lo, 1)

                d_low(0, 0)
                d_low(1, 1)
                layernorm(3)
                xt_chunks(3)

                def evac(b, h, g):
                    v.wait_ge(d_t, b * (4 * H0) + (4 * h + g + 1))
                    v.tensor_copy(d_pt[:, 4 * g:4 * g + 4, :], v3(bank(TB[g]), 4)).then_inc(d_pto, 1)

                def d_batch(b, final):
                    for c in range(NCH):
                        for j in range(4):
                            n = 8 * c + 2 * j + 1
                            v.wait_ge(d_pj, b * 32 + (n + 1))
                            v.tensor_copy(d_v[:, 4 * c + j, :], bank(n % 4)).then_inc(d_vev, 1)
                        if c < 2:
                            d_low(b * NCH + (c + 2), c)
                    for h in range(H0):
                        for c in range(NCH):
                            v.wait_ge(d_s, b * (4 * H0) + (4 * h + c + 1) + AHEAD)
                            v.tensor_reduce(sm[:, 130 + c:131 + c], bank(c), AX, ALU.max).then_inc(d_mx, 1)
                        v.wait_ge(d_mx, b * (5 * H0) + (5 * h + 4))
                        v.tensor_reduce(sm[:, 134:135], sm[:, 130:134], AX, ALU.max).then_inc(d_mx, 1)
                        v.wait_ge(d_mx, b * (5 * H0) + (5 * h + 5))
                        v.tensor_scalar(sm[:, 128 + h % 2:129 + h % 2], sm[:, 134:135],
                                        -float(DH0) ** -0.5, None, ALU.mult).then_inc(d_nb, 1)
                        if h:
                            evac(b, h - 1, 1)
                            evac(b, h - 1, 3)
                        if not final and h in (5, 10):
                            d_low(b * NCH + (NCH + h // 5 - 1), h // 5 - 1)
                    evac(b, H0 - 1, 1)
                    evac(b, H0 - 1, 3)
                    v.wait_ge(d_exp, b * (4 * H0) + 4 * H0 + AHEAD)
                    rs = sm[:, 136:200].rearrange("p (h c) -> p h c", c=NCH)
                    v.tensor_reduce(sm[:, 64:80], rs, AX, ALU.add).then_inc(d_sum, 1)
                    v.wait_ge(d_sum, b * 3 + 1)
                    v.reciprocal(sm[:, 80:96], sm[:, 64:80]).then_inc(d_sum, 1)
                    v.wait_ge(d_sum, b * 3 + 2)
                    v.tensor_copy(d_rx[:, :].rearrange("p (h d) -> p h d", h=H0),
                                  sm[:, 80:96].unsqueeze(2).broadcast_to([P, H0, DH0])).then_inc(d_rxd, 1)
                    v.wait_ge(d_rt, b + 1)
                    v.tensor_copy(d_rx[:, :], bank(7)).then_inc(d_sum, 1)
                    v.wait_ge(d_sum, b * 3 + 3)
                    v.wait_ge(d_pv, b * H0 + H0)
                    v.tensor_tensor(XT[:, :, bass.ds(b * P, P)], v3(bank(6), KC), v3(d_rx[:, :], KC), ALU.mult) \
                        .then_inc(d_o, 1)

                with v.Fori(0, NB - 1) as b:
                    d_batch(b, False)
                d_batch(NB - 1, True)
                add_projection(2, first=0)

            if stages >= 5:
                layernorm(4, rms=1.1920929e-07)
                xt_chunks(4)
                v.wait_ge(eb_landed, 32)
                for t in range(NB):
                    last = v.tensor_tensor(X[:, t, :], X[:, t, :], BI[:, DQ:DQ + D], ALU.add)
                link(last)
                for m in range(2):
                    for oc in range(1, 8, 2):
                        n = 8 * m + oc
                        v.wait_ge(e_pj, n + 1)
                        v.tensor_scalar((e_qt, e_kt)[m][:, oc, :], bank((4 + n) % 8),
                                        (bqc, bkc)[m][:, oc:oc + 1], None, ALU.add).then_inc(e_evd, 1)
                for n in range(8):
                    v.wait_ge(e_pj, 16 + n + 1)
                    f = n % 2
                    v.tensor_tensor(e_v[:, n // 2, D * f:D * (f + 1)], bank((4 + n) % 8), BI[:, D * f:D * (f + 1)],
                                    ALU.add).then_inc(e_evd, 1)

                def e_scale(b):
                    v.wait_ge(e_exp, 16 * (b + 1))
                    link(v.reciprocal(e_ri[:, 16 * b:16 * (b + 1)], e_rs[:, 16 * b:16 * (b + 1)]))
                    for f in range(2):
                        v4 = e_v[:, b, D * f:D * (f + 1)].rearrange("p (j q d) -> p j q d", j=4, q=2)
                        ri = e_ri[:, 16 * b + 8 * f:16 * b + 8 * f + 8].rearrange("p (q j) -> p j q", q=2)
                        last = v.tensor_tensor(v4, v4, ri.unsqueeze(3).broadcast_to([P, 4, 2, DH1]), ALU.mult)
                    last.then_inc(e_vs, 1)

                for g in range(16):
                    v.wait_ge(e_s, g + 1)
                    eg = e_e[:, 4 * g:4 * g + 4, :]
                    v.tensor_tensor(eg, v3(bank((4 + g) % 8), 4), caus[:, :].unsqueeze(1).broadcast_to([P, 4, P]),
                                    ALU.add).then_inc(e_m, 1)
                    v.wait_ge(e_m, g + 1)
                    v.tensor_reduce(e_nm[:, 4 * g:4 * g + 4], eg, AX, ALU.max, negate=True).then_inc(e_mx, 1)
                    if g % 4 == 1 and g > 4:
                        e_scale(g // 4 - 1)
                e_scale(3)
                v.wait_ge(e_z, 1)
                for i in range(1, 8, 2):
                    v.tensor_copy(e_zt[:, i, :], bank(i)).then_inc(e_zevd, 1)
                add_projection(3)

            if stages >= 6:
                n1 = float(D * FF)
                for i in range(2):
                    v.wait_ge(fw_landed[i], 16)
                    v.tensor_reduce(sm[:, 200 + i:201 + i], fa(32 * i, 32), AX, ALU.add,
                                    apply_absolute_value=True).then_inc(f_abs, 1)
                v.wait_ge(f_tot, 2)
                link(v.tensor_scalar(sm[:, 240:242], bank(0)[:, 0:2], 1.0 / n1, 1e-5, ALU.mult, ALU.max))
                link(v.reciprocal(sm[:, 242:244], sm[:, 240:242]))
                for i in range(2):
                    w, wb = fa(32 * i, 32), fa(64 + 16 * i, 16).bitcast(BF16)
                    link(v.tensor_scalar(w, w, sm[:, 242 + i:243 + i], MAGIC, ALU.mult, ALU.add))
                    link(v.tensor_scalar(w, w, MAGIC, 1.0, ALU.subtract, ALU.min))
                    last = v.tensor_scalar(wb, w, -1.0, None, ALU.max)
                    if i == 0:
                        link(last)
                last.then_inc(f_wq, 1)
                layernorm(5, rms=1e-5)
                v.wait_ge(ln_done, 24)
                link(v.tensor_reduce(sm[:, 212:216], Y[:, :, :], AX, ALU.max, apply_absolute_value=True))

                def quant(m, dq, dqs, y, dst, r, n):
                    link(v.tensor_scalar(m, m, 1e-5, None, ALU.max))
                    link(v.reciprocal(dq, m))
                    link(v.tensor_scalar(dq, dq, 127.0, None, ALU.mult))
                    for t in range(len(y)):
                        if r is None:
                            link(v.tensor_scalar(y[t], y[t], dq[:, t:t + 1], None, ALU.mult))
                        else:
                            link(v.tensor_scalar(y[t], y[t], r, dq[:, t:t + 1], ALU.mult, ALU.mult))
                        link(v.tensor_scalar(y[t], y[t], 127.0, -128.0, ALU.min, ALU.max))
                        link(v.tensor_scalar(dst[t], y[t], MAGIC, MAGIC, ALU.add, ALU.subtract))
                    link(v.tensor_scalar(dqs, m, 1.0 / 127.0, sm[:, 240 + n:241 + n], ALU.mult, ALU.mult))

                quant(sm[:, 212:216], sm[:, 220:224], sm[:, 224:228], [Y[:, t, :] for t in range(NB)],
                      [f_yb[:, t, :] for t in range(NB)], None, 0)
                v.wait_ge(fb_landed, 32)
                v.tensor_copy(sm[:, 228:229], sm[:, 224:225]).then_inc(f_ybd, 1)
                v.wait_ge(f_yt_t, 1)
                for i in range(2):
                    last = v.tensor_copy(f_yt[:, 2 * i:2 * i + 2, :], v3(bank(4 + i).bitcast(BF16), 2))
                last.then_inc(f_ytd, 1)
                for t in range(NB):
                    last = v.tensor_tensor(X[:, t, :], X[:, t, :], d_rx[:, :], ALU.add)
                link(last)

                def f_take(t):
                    v.wait_ge(f_m1, t + 1)
                    if t >= 2:
                        v.wait_ge(f_hbd, t - 1)
                    v.scalar_tensor_tensor(f_h[t % 2], bank(4 * (t % 2), 4), sm[:, 224 + t:225 + t], BI[:, :],
                                           ALU.mult, ALU.add).then_inc(f_hd, 1)

                def f_quant(t):
                    hm, r = sm[:, 232 + t:233 + t], rstd[:, t:t + 1]
                    v.wait_ge(f_gel, t + 1)
                    link(v.tensor_reduce(hm, f_h[t % 2], AX, ALU.max, apply_absolute_value=True))
                    v.wait_ge(f_hsq, t + 1)
                    inverse_root(v.tensor_scalar(r, sm[:, 216 + t:217 + t], 1.0 / FF, 1e-5, ALU.mult, ALU.add), slice(t, t + 1))
                    link(v.tensor_tensor(hm, hm, r, ALU.mult))
                    quant(hm, sm[:, 244 + t:245 + t], sm[:, 248 + t:249 + t], [f_h[t % 2]], [f_hb[t % 2]], r, 1)
                    v.tensor_copy(sm[:, 252 + t:253 + t], sm[:, 248 + t:249 + t]).then_inc(f_hbd, 1)

                def f_turn(t):
                    v.wait_ge(f_t, t + 1)
                    o = 4 * (t % 2)
                    for i in range(2):
                        last = v.tensor_copy(f_ht[t % 2][:, 8 * i:8 * i + 8, :], v3(bank(o + i).bitcast(BF16), 8))
                    last.then_inc(f_htd, 1)

                def f_add(t):
                    v.wait_ge(f_m2, t + 1)
                    v.scalar_tensor_tensor(X[:, t, :], bank(4 * (t % 2) + 2), sm[:, 248 + t:249 + t], X[:, t, :],
                                           ALU.mult, ALU.add).then_inc(x_added, 1)

                f_take(0)
                f_take(1)
                for t in range(NB):
                    f_quant(t)
                    f_turn(t)
                    f_add(t)
                    if t + 2 < NB:
                        f_take(t + 2)


def kernel(**inputs):
    import numpy as np
    import concourse.bacc as bacc
    from concourse.bass_utils import run_bass_kernel_spmd

    a = {k: np.asarray(v) for k, v in inputs.items()}

    def rows(w):
        return np.ascontiguousarray(w.reshape(-1, P, w.shape[1]).transpose(1, 0, 2))

    def columns(v):
        return v.reshape(-1, P).T

    c = a["ctx_1024"].reshape(NB * NCH, CH, D)
    qkv = a["L1_attn_W_qkv"].reshape(DQ, 3, D)
    bqkv = a["L1_attn_b_qkv"].reshape(DQ, 3)
    ins = {
        "x": a["x"],
        "ctx_n": c.reshape(NB * NCH, 4, P, D).transpose(0, 2, 1, 3),
        "ctx_t": c.transpose(0, 2, 1).reshape(NB * NCH, KC, P, CH).transpose(0, 2, 1, 3),
        "w1t": rows(a["L0_xattn_W1"].T), "w2n": rows(a["L0_xattn_W2"]), "w3t": rows(a["L0_xattn_W3"].T),
        "bcols": np.concatenate([columns(a["L0_xattn_b1"]), columns(a["L0_xattn_b2"]), columns(bqkv[:, 0]),
                                 columns(bqkv[:, 1]), np.zeros((P, 8), np.float32)], axis=1),
        "beta": a["L0_attn_beta"],
        "l0a_w": np.stack([rows(a[f"L0_attn_W{n}"].T) for n in "qkvo"]),
        "l0a_bq": a["L0_attn_bq"], "l0a_bk": a["L0_attn_bk"], "l0a_bv": a["L0_attn_bv"], "l0a_bo": a["L0_attn_bo"],
        "wgt": rows(a["L0_ffn_Wg"].T),
        "moe_w": np.stack([
            a["L0_ffn_W1"].reshape(NE * UE, P, KC, P).transpose(0, 3, 2, 1).reshape(NE * UE, P, D),
            a["L0_ffn_W2"].reshape(NE * UE, P, KC, P).transpose(0, 3, 2, 1).reshape(NE * UE, P, D),
            a["L0_ffn_W3"].reshape(NE, D, UE, P).transpose(0, 2, 3, 1).reshape(NE * UE, P, D)], axis=2),
        "l1x_w": np.stack([rows(a[f"L1_xattn_W{n}"].T) for n in "qkvo"]),
        "l1a_w": np.stack([rows(qkv[:, i].T) for i in range(3)]),
        "l1a_bv": bqkv[:, 2], "l1a_bo": a["L1_attn_b_o"], "l1a_wo": rows(a["L1_attn_W_o"].T),
        "w1t_f": rows(a["L1_ffn_w1"].T), "w2t_f": rows(a["L1_ffn_w2"].T),
        "l1f_b1": a["L1_ffn_b1"], "l1f_b2": a["L1_ffn_b2"],
    }
    nc = bacc.Bacc("TRN2", target_bir_lowering=False, num_devices=1)
    arrays, aps = {}, {}
    for name, v in ins.items():
        v = np.ascontiguousarray(v)
        arrays[f"in_{name}"] = v
        aps[name] = nc.dram_tensor(f"in_{name}", v.shape, mybir.dt.from_np(v.dtype), kind="ExternalInput").ap()
    out = nc.dram_tensor("out_x", (NB, P, D), F32, kind="ExternalOutput").ap()
    build(nc, aps, out)
    r = run_bass_kernel_spmd(nc, [arrays], core_ids=[0])
    return r.results[0]["out_x"]
```

```python
from contextlib import ExitStack

import concourse.bass as bass
from concourse import mybir
from concourse.alu_op_type import AluOpType as ALU

ACT = mybir.ActivationFunctionType
AX = mybir.AxisListType.X
F32 = mybir.dt.float32
F32R = mybir.dt.float32r
BF16 = mybir.dt.bfloat16

P = 128
D = 512
KC = D // P
NB = 4
T = NB * P
SK = 2048
CH = 512
NCH = SK // CH
NE = 8
HE = 1024
UE = HE // P
H0, DH0 = 16, 32
H1, DH1 = 16, 64
DQ = H1 * DH1
FF = 2048
FC = FF // P
KB = 256
MAGIC = 1.5 * 2.0 ** 23
NEG = -3.0e38
AHEAD = 2
LAST = 6


def build(nc, a, out, stages=LAST):
    ctx = ExitStack()
    with ctx:
        def sb(name, shape, dt=F32):
            return ctx.enter_context(nc.sbuf_tensor(name, shape, dt))

        def sem(name):
            return ctx.enter_context(nc.semaphore(name))

        X = sb("X", [P, NB, D])
        Y = sb("Y", [P, NB, D])
        XT = sb("XT", [P, KC, T])
        BI = sb("BI", [P, 8 * KB])
        FA = sb("FA", [P, 104 * KB])
        RA = sb("RA", [P, 64 * KB], F32R)
        ident = sb("ident", [P, P])
        identb = sb("identb", [P, P], BF16)
        caus = sb("caus", [P, P])
        ones = sb("ones", [P, P])
        rev8 = sb("rev8", [P, NE])
        st = sb("st", [P, NB, 6])
        mv = sb("mv", [P, NB, 2])
        rstd = sb("rstd", [P, NB])
        root = sb("root", [P, NB])
        rtmp = sb("rtmp", [P, NB])
        sm = sb("sm", [P, 256])
        bcol = sb("bcol", [P, 32])
        PS = ctx.enter_context(nc.psum_tensor("PS", [P, 8 * 512], F32))

        TB = (4, 5, 7, 4)

        def bank(i, n=1):
            return PS[:, 512 * i:512 * (i + n)]

        def fa(kb, n):
            return FA[:, kb * KB:(kb + n) * KB]

        def ra(kb, n):
            return RA[:, kb * KB:(kb + n) * KB]

        def v3(ap, n):
            return ap.rearrange("p (a n) -> p a n", a=n)

        b1c, b2c = bcol[:, 0:4], bcol[:, 4:8]
        bqc, bkc = bcol[:, 8:16], bcol[:, 16:24]

        a_ct = [v3(fa(8 * i, 8), KC) for i in range(4)]
        a_cn = [v3(fa(32 + 8 * i, 8), 4) for i in range(4)]
        a_p = fa(64, 8)
        a_pt = v3(fa(72, 8), 16)
        a_qt = v3(fa(80, 8), KC)
        a_ao = v3(fa(80, 8), NB)
        a_wa = v3(fa(88, 8), KC)
        a_wb = v3(fa(96, 8), KC)
        a_qp = v3(BI[:, :], KC)
        b_w = [v3(fa(8 * i, 8), KC) for i in range(4)]
        b_z = v3(fa(32, 16), 8)
        b_v = v3(fa(48, 8), NB)
        b_s1, b_s2, b_s3 = fa(56, 16), fa(72, 16), fa(88, 16)
        b_ao = v3(fa(88, 8), NB)
        NST = 4
        c_st = [v3(fa(6 * i, 6), 3) for i in range(NST)]
        c_sg, c_tt, c_g = fa(24, 2), fa(26, 2), fa(28, 2)
        c_wg = fa(30, 1)[:, 0:KC * NE].rearrange("p (k e) -> p k e", k=KC)
        c_xh, c_xl = v3(ra(0, 8), KC), v3(ra(8, 8), KC)
        c_wh = [v3(ra(16 + 12 * i, 6), 3) for i in range(2)]
        c_wl = [v3(ra(22 + 12 * i, 6), 3) for i in range(2)]
        c_gh = [ra(40 + 4 * i, 2) for i in range(2)]
        c_gl = [ra(42 + 4 * i, 2) for i in range(2)]
        d_st = [v3(fa(8 * i, 8), KC) for i in range(2)]
        d_kt = v3(fa(16, 32), KC)
        d_v = v3(fa(48, 32), 16)
        d_p = [fa(80 + 8 * i, 8) for i in range(2)]
        d_wq = v3(fa(80, 8), KC)
        d_ws = [v3(fa(48 + 8 * i, 8), KC) for i in range(2)]
        d_pt = v3(BI[:, :], 16)
        d_qz = v3(fa(96, 8), 16)
        d_wo = v3(fa(16, 8), KC)
        d_wh = [v3(ra(48 * i, 8), KC) for i in range(2)]
        d_wl = [v3(ra(8 + 48 * i, 8), KC) for i in range(2)]
        d_ch = [v3(ra(16 + 16 * i, 8), KC) for i in range(2)]
        d_cl = [v3(ra(24 + 16 * i, 8), KC) for i in range(2)]
        d_rx = sb("d_rx", [P, D])
        g_ = sb("per_token", [P, 192])
        e_w = [v3(fa(16 * i, 16), KC) for i in range(3)]
        e_qt, e_kt = v3(fa(48, 16), 8), v3(fa(64, 16), 8)
        e_v = v3(fa(80, 16), NB)
        e_wo = v3(fa(0, 16), 8)
        e_e = v3(fa(16, 32), 64)
        e_zt = v3(fa(48, 16), 8)

        def e_head(g, j):
            return 8 * (g // 2) + 2 * j + g % 2

        def e_place(h):
            return 8 * (h // 8) + 4 * (h % 2) + h % 8 // 2

        e_nm, e_rs, e_ri = g_[:, 0:64], g_[:, 64:128], g_[:, 128:192]
        QC = 2048
        NQ = D * FF // P // QC
        q_w = [fa(31 + 32 * i, 32) for i in range(2)]
        q_abs, q_acc = fa(95, 4), fa(99, 4)
        q_all = v3(fa(95, 1), P)
        q_st = [fa(95 + 4 * i, 4).bitcast(BF16) for i in range(2)]
        wq = nc.dram_tensor("ternary_weights", (2, P, NQ * QC), BF16, kind="Internal").ap()
        wsum = nc.dram_tensor("weight_sums", (P, 2), F32, kind="Internal").ap()
        f_wb = [ra(16 * i, 16).bitcast(BF16) for i in range(2)]
        f_w1b, f_w2b = v3(f_wb[0], KC), v3(f_wb[1], FC)
        f_h = [fa(8 * i, 8) for i in range(NB)]
        f_sq = fa(32, 8)
        f_hb = [fa(40 + 4 * i, 4).bitcast(BF16) for i in range(2)]
        f_ht = [v3(fa(48 + 4 * i, 4).bitcast(BF16), FC) for i in range(2)]
        f_yb = v3(fa(56, 4).bitcast(BF16), NB)
        f_yt = v3(fa(60, 4).bitcast(BF16), KC)
        f_b1 = fa(96, 8)
        wmean = sm[:, 240:242]

        const_ready = sem("const_ready")
        const_step = sem("const_step")
        x_landed = sem("x_landed")
        out_stored = sem("out_stored")
        dve = sem("dve_chain")
        root_asked = sem("root_asked")
        root_done = sem("root_done")
        ln_done = sem("ln_done")
        ln_turned = sem("ln_turned")
        xt_act = sem("xt_act")
        xt_dve = sem("xt_dve")

        aw_landed = [sem(f"a_w{i}_landed") for i in range(3)]
        ab_landed = sem("a_b_landed")
        act_landed = [sem(f"a_ct{i}_landed") for i in range(4)]
        acn_landed = [sem(f"a_cn{i}_landed") for i in range(4)]
        a_q = sem("a_q")
        a_qev = sem("a_qev")
        a_qpd = sem("a_qpd")
        a_qb = sem("a_qb")
        a_qpe_act = sem("a_qpe_act")
        a_qpe_dve = sem("a_qpe_dve")
        a_s = sem("a_s")
        a_nb = sem("a_nb")
        a_exp = sem("a_exp")
        a_t = sem("a_t")
        a_pte = sem("a_pte")
        a_pto = sem("a_pto")
        a_pv = sem("a_pv")
        a_o = sem("a_o")
        o_turned = sem("o_turned")
        o_act = sem("o_act")
        o_dve = sem("o_dve")
        proj_done = sem("proj_done")
        x_added = sem("x_added")

        bw_landed = [sem(f"b_w{i}_landed") for i in range(4)]
        bb_landed = sem("b_b_landed")
        b_p = sem("b_p")
        b_zq = sem("b_zq")
        b_beta = sem("b_beta")
        b_zs = sem("b_zs")
        b_u = sem("b_u")
        b_w1p = sem("b_w1p")
        b_ln = sem("b_ln")
        b_o = sem("b_o")

        cg_landed = sem("c_wg_landed")
        c_landed = [sem(f"c_w{i}_landed") for i in range(NST)]
        c_gate = sem("c_gate")
        c_diff = sem("c_diff")
        c_e = sem("c_e")
        c_xhd = sem("c_xh_done")
        c_xld = sem("c_xl_done")
        c_hi12 = sem("c_hi12")
        c_lo12 = sem("c_lo12")
        c_hi3 = sem("c_hi3")
        c_lo3 = sem("c_lo3")
        c_h = sem("c_h")
        c_sig = sem("c_sig")
        c_t = sem("c_t")
        c_gd = sem("c_gd")
        c_ghd = sem("c_ghd")
        c_gld = sem("c_gld")
        c_y = sem("c_y")
        c_acc = sem("c_acc")

        dw_landed = [sem(f"d_w{i}_landed") for i in range(4)]
        d_landed = [sem(f"d_ct{i}_landed") for i in range(2)]
        d_whd = sem("d_whd")
        d_wld = sem("d_wld")
        d_hi = sem("d_hi")
        d_lo = sem("d_lo")
        d_q = sem("d_q")
        d_qev = sem("d_qev")
        d_zero = sem("d_zero")
        d_qzd = sem("d_qzd")
        d_pj = sem("d_pj")
        d_kev = sem("d_kev")
        d_vev = sem("d_vev")
        d_s = sem("d_s")
        d_mx = sem("d_mx")
        d_nb = sem("d_nb")
        d_exp = sem("d_exp")
        d_t = sem("d_t")
        d_pte = sem("d_pte")
        d_pto = sem("d_pto")
        d_pv = sem("d_pv")
        d_sum = sem("d_sum")
        d_rxd = sem("d_rxd")
        d_rt = sem("d_rt")
        d_o = sem("d_o")

        ew_landed = [sem(f"e_w{i}_landed") for i in range(4)]
        eb_landed = sem("e_b_landed")
        e_pj = sem("e_pj")
        e_eva = sem("e_eva")
        e_evd = sem("e_evd")
        e_s = sem("e_s")
        e_m = sem("e_m")
        e_mx = sem("e_mx")
        e_exp = sem("e_exp")
        e_vs = sem("e_vs")
        e_z = sem("e_z")
        e_zev = sem("e_zev")
        e_zevd = sem("e_zevd")

        fw_landed = [sem(f"f_w{i}_landed") for i in range(2)]
        fb_landed = sem("f_b_landed")
        q_landed = [sem(f"q_w{i}_landed") for i in range(3)]
        q_step = sem("q_step")
        q_sums = sem("q_sums")
        q_stored = [sem(f"q_stored{i}") for i in range(2)]
        q_done = sem("q_done")
        f_ybd = sem("f_ybd")
        f_yt_t = sem("f_yt_t")
        f_ytd = sem("f_ytd")
        f_m1 = sem("f_m1")
        f_hd = sem("f_hd")
        f_gel = sem("f_gel")
        f_hsq = sem("f_hsq")
        f_ready = sem("f_ready")
        f_hr = sem("f_hr")
        f_hc = sem("f_hc")
        f_hbd = sem("f_hbd")
        f_t = sem("f_t")
        f_hta = sem("f_hta")
        f_htd = sem("f_htd")
        f_m2 = sem("f_m2")

        block = ctx.enter_context(nc.Block())

        @block.sync
        def _(sp):
            sp.dma_start(X[:, :, :], a["x"].rearrange("b p d -> p b d")).then_inc(x_landed, 16)
            sp.dma_start(a_wa, a["w1t"]).then_inc(aw_landed[0], 16)
            sp.dma_start(bcol[:, :], a["bcols"]).then_inc(ab_landed, 16)
            sp.dma_start(a_wb, a["w2n"]).then_inc(aw_landed[1], 16)
            for b in range(NB):
                for c in range(NCH):
                    if b:
                        sp.wait_ge(a_s, 4 * (b - 1) + c + 1)
                    sp.dma_start(a_ct[c], a["ctx_t"][NCH * b + c]).then_inc(act_landed[c], 16)
                if b == 0:
                    sp.wait_ge(a_q, 4)
                    sp.dma_start(a_wa, a["w3t"]).then_inc(aw_landed[2], 16)
                for c in range(NCH):
                    if b:
                        sp.wait_ge(a_pv, 4 * (b - 1) + c + 1)
                    sp.dma_start(a_cn[c], a["ctx_n"][NCH * b + c]).then_inc(acn_landed[c], 16)
            if stages >= 2:
                for i in range(4):
                    sp.wait_ge(a_s, 4 * (NB - 1) + i + 1)
                    sp.dma_start(b_w[i], a["l0a_w"][i]).then_inc(bw_landed[i], 16)
                sp.wait_ge(a_s, 16)
                for i, name in enumerate(("l0a_bq", "l0a_bk", "l0a_bv", "l0a_bo")):
                    sp.dma_start(BI[:, D * i:D * (i + 1)], a[name].partition_broadcast(P)).then_inc(bb_landed, 16)
                sp.dma_start(sm[:, 64:80], a["beta"].partition_broadcast(P)).then_inc(bb_landed, 16)
            if stages >= 3:
                sp.wait_ge(b_p, 12)
                for u in range(NST):
                    sp.dma_start(c_st[u], a["moe_w"][u]).then_inc(c_landed[u], 16)
                sp.wait_ge(proj_done, 8)
                sp.dma_start(c_wg, a["wgt"]).then_inc(cg_landed, 16)
                with sp.Fori(1, NE * UE // NST) as q:
                    for j in range(NST):
                        sp.wait_ge(c_lo3, q * NST + (j - NST + 1))
                        sp.dma_start(c_st[j].unsqueeze(1), a["moe_w"][bass.ds(q * NST + j, 1)].rearrange(
                            "u p a n -> p u a n")).then_inc(c_landed[j], 16)
            if stages >= 4:
                sp.wait_ge(c_lo3, NE * UE)
                for j in range(2):
                    sp.dma_start(d_st[j], a["ctx_t"][j]).then_inc(d_landed[j], 16)
                with sp.Fori(1, NB * NCH // 2) as q:
                    for j in range(2):
                        sp.wait_ge(d_lo, q * 2 + (j - 1))
                        sp.dma_start(d_st[j].unsqueeze(1), a["ctx_t"][bass.ds(q * 2 + j, 1)].rearrange(
                            "u p a n -> p u a n")).then_inc(d_landed[j], 16)
                sp.wait_ge(d_s, 4 * H0 * NB + AHEAD)
                sp.dma_start(d_wo, a["l1x_w"][3]).then_inc(dw_landed[3], 16)
            if stages >= 5:
                sp.wait_ge(d_lo, NB * NCH)
                sp.dma_start(e_w[0], a["l1a_w"][0]).then_inc(ew_landed[0], 16)
                sp.wait_ge(proj_done, 12)
                for i in range(1, 3):
                    sp.dma_start(e_w[i], a["l1a_w"][i]).then_inc(ew_landed[i], 16)
                sp.dma_start(BI[:, 0:DQ], a["l1a_bv"].partition_broadcast(P)).then_inc(eb_landed, 16)
                sp.dma_start(BI[:, DQ:DQ + D], a["l1a_bo"].partition_broadcast(P)).then_inc(eb_landed, 16)
                sp.wait_ge(e_pj, 8)
                sp.dma_start(e_wo, a["l1a_wo"]).then_inc(ew_landed[3], 16)
            if stages >= 6:
                sp.dma_start(f_b1, a["l1f_b1"].partition_broadcast(P)).then_inc(fb_landed, 16)
                sp.dma_start(d_rx[:, :], a["l1f_b2"].partition_broadcast(P)).then_inc(fb_landed, 16)
                sp.wait_ge(d_pj, 8 * NCH * NB)
                for i in range(2):
                    sp.dma_start(f_wb[i], wq[i]).then_inc(fw_landed[i], 16)
                for t in range(NB):
                    sp.wait_ge(x_added, 16 + t + 1)
                    sp.dma_start(out[t], X[:, t, :]).then_inc(out_stored, 16)
                sp.wait_ge(out_stored, 16 * NB)
                return
            sp.wait_ge(x_added, 4 * stages if stages < 3 else 4 * (stages - 1))
            if stages == 3:
                sp.wait_ge(c_acc, NE + AHEAD)
            sp.dma_start(out.rearrange("b p d -> p b d"), X[:, :, :]).then_inc(out_stored, 16)
            sp.wait_ge(out_stored, 16)

        @block.gpsimd
        def _(pool):
            pool.memset(ident[:, :], 0.0).then_inc(const_step, 1)
            pool.memset(caus[:, :], 0.0).then_inc(const_step, 1)
            pool.memset(ones[:, :], 1.0).then_inc(const_ready, 1)
            for e in range(NE):
                pool.memset(rev8[:, e:e + 1], float(NE - e)).then_inc(const_ready, 1)
            pool.wait_ge(const_step, 2)
            pool.affine_select(out=ident[:, :], in_=ident[:, :], compare_op=ALU.not_equal, fill=1.0, base=0,
                               pattern=[[-1, P]], channel_multiplier=1).then_inc(const_step, 1)
            pool.affine_select(out=caus[:, :], in_=caus[:, :], compare_op=ALU.is_ge, fill=NEG, base=0,
                               pattern=[[1, P]], channel_multiplier=-1).then_inc(const_ready, 1)
            pool.wait_ge(const_step, 3)
            pool.tensor_copy(identb[:, :], ident[:, :]).then_inc(const_ready, 1)
            if stages >= 4:
                pool.wait_ge(proj_done, 8)
            if stages >= 6:
                steps = [0]

                def q_link(ins):
                    steps[0] += 1
                    ins.then_inc(q_step, 1)
                    pool.wait_ge(q_step, steps[0])

                def q_load(k):
                    i, part = k // NQ, slice(QC * (k % NQ), QC * (k % NQ + 1))
                    src = a[("w1t_f", "w2t_f")[i]].rearrange("p a n -> p (a n)")
                    pool.dma_start(q_w[i][:, part], src[:, part]).then_inc(q_landed[k % 3], 16)

                half = QC // 2
                for k in range(3):
                    q_load(k)
                for k in range(2 * NQ):
                    pool.wait_ge(q_landed[k % 3], 16 * (k // 3 + 1))
                    for f in range(2):
                        o = QC * (k % NQ) + half * f
                        w = q_w[k // NQ][:, o:o + half]
                        first = k % NQ == 0 and f == 0
                        q_link(pool.tensor_scalar(q_abs, w, 0.0, 2.0, ALU.max, ALU.mult))
                        q_link(pool.tensor_tensor(q_acc if first else q_abs, q_abs, w, ALU.subtract))
                        if not first:
                            q_link(pool.tensor_tensor(q_acc, q_acc, q_abs, ALU.add))
                    if k + 3 < 2 * NQ:
                        q_load(k + 3)
                    if k % NQ == NQ - 1:
                        n, i = half // 2, k // NQ
                        while n:
                            dst = q_acc[:, 0:n] if n > 1 else sm[:, 200 + i:201 + i]
                            q_link(pool.tensor_tensor(dst, q_acc[:, 0:n], q_acc[:, n:2 * n], ALU.add))
                            n //= 2
                pool.dma_start(wsum, sm[:, 200:202]).then_inc(q_sums, 16)
                pool.wait_ge(q_sums, 16)
                pool.dma_start(fa(95, 1), wsum.rearrange("p i -> (p i)").partition_broadcast(P)).then_inc(q_sums, 16)
                pool.wait_ge(q_sums, 32)
                n = P // 2
                while n:
                    q_link(pool.tensor_tensor(q_all[:, 0:n, :], q_all[:, 0:n, :], q_all[:, n:2 * n, :], ALU.add))
                    n //= 2
                q_link(pool.tensor_scalar(wmean, q_all[:, 0, :], 1.0 / (D * FF), 1e-5, ALU.mult, ALU.max))
                pool.tensor_scalar(sm[:, 204:206], wmean, 0.5, None, ALU.mult)
                q_link(pool.tensor_scalar(sm[:, 206:208], wmean, -0.5, None, ALU.mult))
                for k in range(2 * NQ):
                    i, part = k // NQ, slice(QC * (k % NQ), QC * (k % NQ + 1))
                    if k >= 2:
                        pool.wait_ge(q_stored[k % 2], 16 * (k // 2))
                    w = q_w[i][:, part]
                    q_link(pool.tensor_scalar(q_st[k % 2], w, sm[:, 204 + i:205 + i], 1.0, ALU.is_gt, ALU.subtract))
                    q_link(pool.tensor_scalar(w, w, sm[:, 206 + i:207 + i], None, ALU.is_ge))
                    q_link(pool.tensor_tensor(q_st[k % 2], q_st[k % 2], w, ALU.add))
                    pool.dma_start(wq[i][:, part], q_st[k % 2]).then_inc(q_stored[k % 2], 16)
                for i in range(2):
                    pool.wait_ge(q_stored[i], 16 * NQ)
                pool.sem_inc(q_done, 1)
            if stages >= 4:
                for i in range(2):
                    pool.dma_start(d_ws[i], a["l1x_w"][1 + i]).then_inc(dw_landed[1 + i], 16)
                pool.dma_start(d_wq, a["l1x_w"][0]).then_inc(dw_landed[0], 16)
                pool.memset(fa(96, 8), 0.0).then_inc(d_zero, 1)
                pool.wait_ge(d_zero, 1)
                pool.wait_ge(d_qev, 4)
                with pool.Fori(0, NB) as b:
                    pool.wait_ge(d_s, b * (4 * H0) + AHEAD)
                    for j in range(4):
                        dst = d_qz.rearrange("p (g j) n -> p g j n", j=4)[32 * j:32 * j + 32, :, j, :]
                        pool.tensor_copy(dst, Y[32 * j:32 * j + 32, :, bass.ds(b * P, P)]).then_inc(d_qzd, 1)

        N_CONST = 1 + NE + 2

        @block.tensor
        def _(pe):
            for signal in (c_h, c_y, d_s):
                pe.sem_inc(signal, AHEAD)
            def turn_tokens(n):
                for t in range(NB):
                    pe.wait_ge(ln_done, NB * n + t + 1)
                    for c in range(KC):
                        last = pe.transpose(bank(c)[:, P * t:P * (t + 1)], Y[:, t, P * c:P * (c + 1)], ident[:, :])
                last.then_inc(ln_turned, 1)

            def wait_xt(n):
                pe.wait_ge(xt_act, 2 * n + 2)
                pe.wait_ge(xt_dve, 2 * n + 2)

            def gemm(dst, lhs, rhs, k):
                for i in range(k):
                    last = pe.matmul(dst, lhs(i), rhs(i), start=(i == 0), stop=(i == k - 1))
                return last

            def three(dst, k, lh, ll, rh, rl):
                for i in range(k):
                    pe.matmul(dst, lh(i), rh(i), start=(i == 0), stop=False)
                    pe.matmul(dst, lh(i), rl(i), start=False, stop=False)
                    last = pe.matmul(dst, ll(i), rh(i), start=False, stop=(i == k - 1))
                return last

            def turn_out(src, n):
                for t in range(NB):
                    for c in range(KC):
                        last = pe.transpose(bank(c)[:, P * t:P * (t + 1)], src[:, t, P * c:P * (c + 1)], ident[:, :])
                last.then_inc(o_turned, 1)

            def project_out(w, k, src=XT, first=4):
                for t in range(NB):
                    gemm(bank(first + t), lambda i: src[:, i, P * t:P * (t + 1)], lambda i: w[:, i, :], k) \
                        .then_inc(proj_done, 1)

            pe.wait_ge(const_ready, N_CONST)
            turn_tokens(0)
            pe.wait_ge(aw_landed[0], 16)
            wait_xt(0)
            for oc in range(KC):
                gemm(bank(4 + oc), lambda i: a_wa[:, i, P * oc:P * (oc + 1)], lambda i: XT[:, i, :], KC).then_inc(a_q, 1)
            pe.wait_ge(a_qev, 4)
            pe.wait_ge(aw_landed[1], 16)
            for oc in range(KC):
                gemm(bank(oc), lambda i: a_wb[:, i, P * oc:P * (oc + 1)], lambda i: a_qt[:, i, :], KC).then_inc(a_qpd, 1)
            for t in range(NB):
                last = gemm(bank(4)[:, t:t + 1], lambda i: a_qt[:, i, P * t:P * (t + 1)],
                            lambda i: b2c[:, i:i + 1], KC)
            last.then_inc(a_qb, 1)
            pe.wait_ge(a_qpe_act, 2)
            pe.wait_ge(a_qpe_dve, 3)

            def a_scores(b):
                for c in range(NCH):
                    pe.wait_ge(act_landed[c], 16 * (b + 1))
                    if b:
                        pe.wait_ge(a_exp, 2 * (b - 1) + 1 + c // 2)
                    gemm(bank(c), lambda i: a_qp[:, i, P * b:P * (b + 1)], lambda i: a_ct[c][:, i, :], KC).then_inc(a_s, 1)

            def a_turn(b):
                for g in range(4):
                    pe.wait_ge(a_exp, 2 * b + 1 + g // 2)
                    if 2 * b + g // 2 > 0:
                        pe.wait_ge(a_pto if g % 2 else a_pte, 2 * b + g // 2)
                    for j in range(4):
                        last = pe.transpose(bank(5 + g % 2)[:, P * j:P * (j + 1)],
                                            a_p[:, CH * g + P * j:CH * g + P * (j + 1)], ident[:, :])
                    last.then_inc(a_t, 1)

            def a_mix(b):
                if b:
                    pe.wait_ge(a_o, b)
                for g in range(4):
                    pe.wait_ge(a_pto if g % 2 else a_pte, 2 * b + g // 2 + 1)
                    pe.wait_ge(acn_landed[g], 16 * (b + 1))
                    for j in range(4):
                        last = pe.matmul(bank(4), a_pt[:, 4 * g + j, :], a_cn[g][:, j, :],
                                         start=(g == 0 and j == 0), stop=(g == 3 and j == 3))
                    last.then_inc(a_pv, 1)

            a_scores(0)
            a_turn(0)
            for b in range(1, NB):
                a_scores(b)
                a_mix(b - 1)
                a_turn(b)
            a_mix(NB - 1)
            pe.wait_ge(a_o, NB)
            turn_out(a_ao, 0)
            pe.wait_ge(o_act, 2)
            pe.wait_ge(o_dve, 2)
            pe.wait_ge(aw_landed[2], 16)
            project_out(a_wa, KC)

            if stages >= 2:
                turn_tokens(1)
                wait_xt(1)
                for m in range(3):
                    pe.wait_ge(bw_landed[m], 16)
                    for t in range(NB):
                        n = 4 * m + t
                        if m == 1:
                            pe.wait_ge(x_added, t + 1)
                        if m == 2:
                            pe.wait_ge(b_zq, t + 1)
                        gemm(bank(n % 8), lambda i: XT[:, i, P * t:P * (t + 1)], lambda i: b_w[m][:, i, :], KC) \
                            .then_inc(b_p, 1)
                pe.wait_ge(b_o, NB)
                turn_out(b_ao, 1)
                pe.wait_ge(o_act, 4)
                pe.wait_ge(o_dve, 4)
                pe.wait_ge(bw_landed[3], 16)
                project_out(b_w[3], KC)

            if stages >= 3:
                turn_tokens(2)
                wait_xt(2)
                pe.wait_ge(cg_landed, 16)
                for t in range(NB):
                    last = gemm(bank(7)[:, NE * t:NE * (t + 1)], lambda i: XT[:, i, P * t:P * (t + 1)],
                                lambda i: c_wg[:, i, :], KC)
                last.then_inc(c_gate, 1)
                pe.wait_ge(c_xld, 1)

                def c_hidden(before, j):
                    s = j % 2
                    pe.wait_ge(c_lo12, before + (j + 1))
                    if j:
                        pe.wait_ge(c_gd, before + (j - 1) + AHEAD)
                    for m in range(2):
                        w = lambda x, i: x[s][:, m, P * i:P * (i + 1)]
                        last = three(bank(2 * s + m), KC, lambda i: w(c_wh, i), lambda i: w(c_wl, i),
                                     lambda i: c_xh[:, i, :], lambda i: c_xl[:, i, :])
                    last.then_inc(c_h, 1)

                def c_out(u, j):
                    s = j % 2
                    pe.wait_ge(c_gld, u + 1)
                    pe.wait_ge(c_lo3, u + 1)
                    for t in range(NB):
                        tk = slice(P * t, P * (t + 1))
                        pe.matmul(bank(4 + t), c_gh[s][:, tk], c_wh[s][:, 2, :], start=(j == 0), stop=False)
                        pe.matmul(bank(4 + t), c_gh[s][:, tk], c_wl[s][:, 2, :], start=False, stop=False)
                        last = pe.matmul(bank(4 + t), c_gl[s][:, tk], c_wh[s][:, 2, :], start=False, stop=(j == UE - 1))
                    last.then_inc(c_y, 1)

                def c_expert(e, final):
                    for j in range(UE):
                        if not (final and j == UE - 1):
                            c_hidden(e * UE, j + 1)
                        if j == 0:
                            pe.wait_ge(c_acc, e + AHEAD)
                        c_out(e * UE + j, j)

                c_hidden(0, 0)
                pe.wait_ge(c_e, 1)
                with pe.Fori(0, NE - 1) as e:
                    c_expert(e, False)
                c_expert(NE - 1, True)

            if stages >= 4:
                turn_tokens(3)
                wait_xt(3)
                pe.wait_ge(dw_landed[0], 16)
                for oc in range(KC):
                    gemm(bank(4 + oc), lambda i: d_wq[:, i, P * oc:P * (oc + 1)], lambda i: XT[:, i, :], KC) \
                        .then_inc(d_q, 1)
                pe.wait_ge(d_wld, 2)

                def d_project(b, first):
                    for c in range(NCH):
                        s = c % 2
                        pe.wait_ge(d_lo, b * NCH + (c + 1))
                        for j in range(4):
                            for m in range(2):
                                n = 8 * c + 2 * j + m
                                if n >= 4:
                                    pe.wait_ge(d_vev if m else d_kev, b * 16 + (n // 2 - 1))
                                elif n == 0:
                                    pe.wait_ge(d_exp, b * (4 * H0) + AHEAD)
                                dst = bank(n % 4)
                                if m == 0:
                                    w = lambda x, i: x[0][:, i, P * j:P * (j + 1)]
                                    last = three(dst, KC, lambda i: w(d_wh, i), lambda i: w(d_wl, i),
                                                 lambda i: d_ch[s][:, i, :], lambda i: d_cl[s][:, i, :])
                                else:
                                    k = slice(P * j, P * (j + 1))
                                    last = three(dst, KC, lambda i: d_ch[s][:, i, k], lambda i: d_cl[s][:, i, k],
                                                 lambda i: d_wh[1][:, i, :], lambda i: d_wl[1][:, i, :])
                                last.then_inc(d_pj, 1)

                def score(b, h, c):
                    if h:
                        pe.wait_ge(d_exp, b * (4 * H0) + (4 * (h - 1) + c + 1) + AHEAD)
                    pe.matmul(bank(c), d_qz[:, h, :], d_kt[:, h // 4, CH * c:CH * (c + 1)],
                              start=True, stop=True).then_inc(d_s, 1)

                def turn(b, h, g):
                    pe.wait_ge(d_exp, b * (4 * H0) + (4 * h + g + 1) + AHEAD)
                    if g == 3:
                        pe.wait_ge(d_pte, b * (2 * H0) + (2 * h + 1) + AHEAD)
                    else:
                        pe.wait_ge((d_pto, d_pto, d_pte)[g], b * (2 * H0) + 2 * h + AHEAD)
                    for j in range(4):
                        last = pe.transpose(bank(TB[g])[:, P * j:P * (j + 1)],
                                            d_p[h % 2][:, CH * g + P * j:CH * g + P * (j + 1)], ident[:, :])
                    last.then_inc(d_t, 1)

                def mix(b, h, g):
                    r, q = 32 * (h % 4), P * (h // 4)
                    pe.wait_ge(d_pto if g % 2 else d_pte, b * (2 * H0) + (2 * h + g // 2 + 1) + AHEAD)
                    for j in range(4):
                        last = pe.matmul(bank(6)[r:r + 32, q:q + P], d_v[:, 4 * g + j, DH0 * h:DH0 * (h + 1)],
                                         d_pt[:, 4 * g + j, :], start=(g == 0 and j == 0),
                                         stop=(g == 3 and j == 3))
                    if g == 3:
                        last.then_inc(d_pv, 1)

                def turn_and_mix(b, h):
                    turn(b, h, 0)
                    turn(b, h, 1)
                    turn(b, h, 2)
                    mix(b, h, 0)
                    turn(b, h, 3)
                    mix(b, h, 1)
                    mix(b, h, 2)

                with pe.Fori(0, NB) as b:
                    d_project(b, False)
                    pe.wait_ge(d_kev, b * 16 + 16)
                    pe.wait_ge(d_vev, b * 16 + 16)
                    pe.wait_ge(d_qzd, b * 4 + 4)
                    for h in range(H0):
                        for c in range(NCH):
                            score(b, h, c)
                            if c == 0 and h >= 2:
                                mix(b, h - 2, 3)
                        if h == 1:
                            pe.wait_ge(d_o, b + AHEAD)
                        if h:
                            turn_and_mix(b, h - 1)
                    mix(b, H0 - 2, 3)
                    turn_and_mix(b, H0 - 1)
                    mix(b, H0 - 1, 3)
                    pe.wait_ge(d_rxd, b + 1)
                    for g in range(KC):
                        last = pe.transpose(bank(7)[:, P * g:P * (g + 1)], d_rx[:, P * g:P * (g + 1)], ident[:, :])
                    last.then_inc(d_rt, 1)
                pe.wait_ge(d_o, NB + AHEAD)
                pe.wait_ge(dw_landed[3], 16)
                project_out(d_wo, KC, first=0)

            if stages >= 5:
                pe.wait_ge(x_added, 12)
                turn_tokens(4)
                wait_xt(4)
                for m in range(2):
                    pe.wait_ge(ew_landed[m], 16)
                    for oc in range(8):
                        n = 8 * m + oc
                        if m:
                            pe.wait_ge(e_evd if oc % 2 else e_eva, oc // 2 + 1)
                        gemm(bank((4 + n) % 8), lambda i: e_w[m][:, i, P * oc:P * (oc + 1)],
                             lambda i: XT[:, i, :], KC).then_inc(e_pj, 1)
                pe.wait_ge(ew_landed[2], 16)
                for t in range(NB):
                    for f in range(2):
                        n = 2 * t + f
                        pe.wait_ge(e_evd if n % 2 else e_eva, 4 + n // 2 + 1)
                        gemm(bank((4 + n) % 8), lambda i: XT[:, i, P * t:P * (t + 1)],
                             lambda i: e_w[2][:, i, D * f:D * (f + 1)], KC).then_inc(e_pj, 1)
                pe.wait_ge(e_eva, 8)
                pe.wait_ge(e_evd, 8)
                for g in range(16):
                    if g < 8:
                        pe.wait_ge(e_evd, 8 + g + 1)
                    else:
                        pe.wait_ge(e_m, g - 8 + 1)
                    for j in range(4):
                        b, h = g // 4, e_head(g % 4, j)
                        r = slice(64 * (h % 2), 64 * (h % 2) + 64)
                        tk = slice(P * b, P * (b + 1))
                        last = pe.matmul(bank((4 + g) % 8)[:, P * j:P * (j + 1)], e_kt[r, h // 2, tk],
                                         e_qt[r, h // 2, tk], start=True, stop=True)
                    last.then_inc(e_s, 1)
                pe.wait_ge(e_m, 16)
                for b in range(NB):
                    pe.wait_ge(e_vs, b + 1)
                    for h in range(H1):
                        r = 64 * (h % 2)
                        last = pe.matmul(bank(h // 2)[r:r + 64, P * b:P * (b + 1)], e_v[:, b, DH1 * h:DH1 * (h + 1)],
                                         e_e[:, H1 * b + e_place(h), :], start=True, stop=True)
                last.then_inc(e_z, 1)
                pe.wait_ge(e_zev, 4)
                pe.wait_ge(e_zevd, 4)
                pe.wait_ge(ew_landed[3], 16)
                project_out(e_wo, 8, src=e_zt, first=4)

            if stages >= 6:
                pe.wait_ge(f_ybd, 1)
                yt_ps = [bank(4 + i).bitcast(BF16) for i in range(2)]
                for c in range(KC):
                    for t in range(NB):
                        last = pe.transpose(yt_ps[c // 2][:, 512 * (c % 2) + P * t:512 * (c % 2) + P * (t + 1)],
                                            f_yb[:, t, P * c:P * (c + 1)], identb[:, :])
                last.then_inc(f_yt_t, 1)
                pe.wait_ge(f_ytd, 1)

                pe.wait_ge(fw_landed[0], 16)
                for t in range(NB):
                    if t >= 2:
                        pe.wait_ge(f_hd, t - 1)
                    for f in range(4):
                        last = gemm(bank(4 * (t % 2) + f), lambda i: f_yt[:, i, P * t:P * (t + 1)],
                                    lambda i: f_w1b[:, i, 512 * f:512 * (f + 1)], KC)
                    last.then_inc(f_m1, 1)
                pe.wait_ge(fw_landed[1], 16)
                pe.wait_ge(f_hd, NB)

                def f_turn(t):
                    pe.wait_ge(f_hbd, t + 1)
                    tp = [bank(4 * (t % 2) + i).bitcast(BF16) for i in range(2)]
                    for j in range(FC):
                        last = pe.transpose(tp[j // 8][:, P * (j % 8):P * (j % 8 + 1)],
                                            f_hb[t % 2][:, P * j:P * (j + 1)], identb[:, :])
                    last.then_inc(f_t, 1)

                def f_down(t):
                    pe.wait_ge(f_hta, t + 1)
                    pe.wait_ge(f_htd, t + 1)
                    if t >= 2:
                        pe.wait_ge(x_added, 16 + t - 1)
                    gemm(bank(4 * (t % 2) + 2), lambda i: f_ht[t % 2][:, i, :], lambda i: f_w2b[:, i, :], FC) \
                        .then_inc(f_m2, 1)

                f_turn(0)
                for t in range(NB):
                    if t + 1 < NB:
                        f_turn(t + 1)
                    f_down(t)

        @block.scalar
        def _(act):
            for signal in (d_exp, d_pte):
                act.sem_inc(signal, AHEAD)
            def copy(dst, src):
                return act.activation(dst, src, ACT.Copy)

            roots = [0]

            def take_root(t=slice(0, NB)):
                roots[0] += 1
                act.wait_ge(root_asked, roots[0])
                act.activation(root[:, t], rstd[:, t], ACT.Sqrt).then_inc(root_done, 1)

            def xt_chunks(n):
                act.wait_ge(ln_turned, n + 1)
                for c in range(2):
                    copy(XT[:, c, :], bank(c)).then_inc(xt_act, 1)

            def out_chunks(n):
                act.wait_ge(o_turned, n + 1)
                for c in range(2):
                    copy(XT[:, c, :], bank(c)).then_inc(o_act, 1)

            take_root()
            xt_chunks(0)
            act.wait_ge(ab_landed, 16)
            for oc in range(KC):
                act.wait_ge(a_q, oc + 1)
                act.activation(a_qt[:, oc, :], bank(4 + oc), ACT.Identity, bias=b1c[:, oc:oc + 1]).then_inc(a_qev, 1)
            for oc in range(2):
                act.wait_ge(a_qpd, oc + 1)
                copy(a_qp[:, oc, :], bank(oc)).then_inc(a_qpe_act, 1)
            for b in range(NB):
                act.wait_ge(a_nb, b + 1)
                if b:
                    act.wait_ge(a_t, 4 * b)
                for f in range(2):
                    act.activation(a_p[:, 1024 * f:1024 * (f + 1)], bank(2 * f, 2), ACT.Exp, bias=sm[:, 8 + b:9 + b],
                                   scale=1.0 / 32, accum_out=sm[:, 16 + 2 * b + f:17 + 2 * b + f]).then_inc(a_exp, 1)
                for g in (0, 2):
                    act.wait_ge(a_t, 4 * b + g + 1)
                    copy(a_pt[:, 4 * g:4 * g + 4, :], v3(bank(5), 4)).then_inc(a_pte, 1)
            out_chunks(0)

            if stages >= 2:
                take_root()
                xt_chunks(1)
                act.wait_ge(bb_landed, 80)
                act.activation(sm[:, 80:96], sm[:, 64:80], ACT.Exp).then_inc(b_beta, 1)
                for m in range(2):
                    hf = slice(2048 * m, 2048 * (m + 1))
                    act.wait_ge(b_zs, m + 1)
                    act.activation(b_s1[:, hf], fa(32 + 8 * m, 8), ACT.Abs).then_inc(b_u, 1)
                    act.wait_ge(b_u, 2 * m + 1)
                    act.activation(b_s1[:, hf], b_s1[:, hf], ACT.Exp, scale=-1.0).then_inc(b_u, 1)
                for m in range(2):
                    hf = slice(2048 * m, 2048 * (m + 1))
                    act.wait_ge(b_w1p, m + 1)
                    act.activation(b_s3[:, hf], b_s2[:, hf], ACT.Ln).then_inc(b_ln, 1)
                out_chunks(1)

            if stages >= 3:
                take_root()
                xt_chunks(2)
                act.wait_ge(xt_act, 6)
                act.wait_ge(xt_dve, 6)
                copy(c_xh, XT[:, :, :]).then_inc(c_xhd, 1)
                act.wait_ge(c_diff, 1)
                act.activation(sm[:, 120:124], sm[:, 116:120], ACT.Exp).then_inc(c_e, 1)

                def c_split12(before, k):
                    act.wait_ge(c_landed[k % NST], before * (16 // NST) + (16 * (k // NST) + 16))
                    if k:
                        act.wait_ge(c_h, before + (k - 1) + AHEAD)
                    copy(c_wh[k % 2][:, 0:2, :], c_st[k % NST][:, 0:2, :]).then_inc(c_hi12, 1)

                def c_expert(e, final):
                    for j in range(UE):
                        if not (final and j == UE - 1):
                            c_split12(e * UE, j + 1)
                        act.wait_ge(c_y, e * UE + (j - 1 + AHEAD))
                        copy(c_wh[j % 2][:, 2, :], c_st[j % NST][:, 2, :]).then_inc(c_hi3, 1)
                        act.wait_ge(c_h, e * UE + (j + 1) + AHEAD)
                        act.wait_ge(c_t, e * UE + j + AHEAD)
                        act.activation(c_sg, bank(2 * (j % 2)), ACT.Sigmoid).then_inc(c_sig, 1)

                def d_split_weights(i):
                    act.wait_ge(dw_landed[1 + i], 16)
                    copy(d_wh[i], d_ws[i]).then_inc(d_whd, 1)

                c_split12(0, 0)
                with act.Fori(0, NE - 1) as e:
                    c_expert(e, False)
                if stages >= 4:
                    d_split_weights(1)
                c_expert(NE - 1, True)

            if stages >= 4:
                act.wait_ge(c_h, NE * UE + AHEAD)
                d_split_weights(0)

                def d_split(b, c):
                    act.wait_ge(d_landed[c % 2], b * 32 + (16 * (c // 2) + 16))
                    if isinstance(b, int) and c < 2:
                        pass
                    else:
                        act.wait_ge(d_pj, b * 32 + (8 * (c - 1)))
                    copy(d_ch[c % 2], d_st[c % 2]).then_inc(d_hi, 1)

                act.wait_ge(c_y, NE * UE + AHEAD)
                take_root()
                d_split(0, 0)
                xt_chunks(3)
                d_split(0, 1)
                for oc in range(KC):
                    act.wait_ge(d_q, oc + 1)
                    copy(Y[:, oc, :], bank(4 + oc)).then_inc(d_qev, 1)

                def d_batch(b, final):
                    for c in range(NCH):
                        for j in range(4):
                            n = 8 * c + 2 * j
                            act.wait_ge(d_pj, b * 32 + (n + 1))
                            copy(d_kt[:, j, CH * c:CH * (c + 1)], bank(n % 4)).then_inc(d_kev, 1)
                        if c < 2:
                            act.wait_ge(d_landed[c], b * 32 + 32)
                            act.wait_ge(d_pj, b * 32 + (8 * (c + 1)))
                            copy(d_ch[c], d_st[c]).then_inc(d_hi, 1)
                    for h in range(H0):
                        if h:
                            evac(b, h - 1, 0)
                        act.wait_ge(d_nb, b * H0 + (h + 1))
                        if h >= 2:
                            act.wait_ge(d_t, b * (4 * H0) + 4 * (h - 1))
                        for c in range(NCH):
                            act.activation(d_p[h % 2][:, CH * c:CH * (c + 1)], bank(c), ACT.Exp,
                                           bias=sm[:, 128 + h % 2:129 + h % 2], scale=float(DH0) ** -0.5,
                                           accum_out=sm[:, 136 + 4 * h + c:137 + 4 * h + c]).then_inc(d_exp, 1)
                            if c == 0 and h:
                                evac(b, h - 1, 2)
                        if not final and h in (5, 10):
                            c = h // 5 - 1
                            act.wait_ge(d_landed[c], b * 32 + 48)
                            act.wait_ge(d_pj, b * 32 + 32)
                            copy(d_ch[c], d_st[c]).then_inc(d_hi, 1)
                    evac(b, H0 - 1, 0)
                    evac(b, H0 - 1, 2)

                def evac(b, h, g):
                    act.wait_ge(d_t, b * (4 * H0) + (4 * h + g + 1))
                    copy(d_pt[:, 4 * g:4 * g + 4, :], v3(bank(TB[g]), 4)).then_inc(d_pte, 1)

                with act.Fori(0, NB - 1) as b:
                    d_batch(b, False)
                d_batch(NB - 1, True)

            if stages >= 5:
                take_root()
                take_root()
                xt_chunks(4)
                for m in range(2):
                    for oc in range(0, 8, 2):
                        n = 8 * m + oc
                        act.wait_ge(e_pj, n + 1)
                        act.activation((e_qt, e_kt)[m][:, oc, :], bank((4 + n) % 8), ACT.Identity,
                                       bias=(bqc, bkc)[m][:, oc:oc + 1]).then_inc(e_eva, 1)
                for i in range(64):
                    act.wait_ge(e_mx, i // 4 + 1)
                    act.activation(e_e[:, i, :], e_e[:, i, :], ACT.Exp, bias=e_nm[:, i:i + 1],
                                   accum_out=e_rs[:, i:i + 1]).then_inc(e_exp, 1)
                act.wait_ge(e_z, 1)
                for i in range(0, 8, 2):
                    copy(e_zt[:, i, :], bank(i)).then_inc(e_zev, 1)

            if stages >= 6:
                take_root()
                take_root()
                for t in range(NB):
                    act.wait_ge(f_hd, t + 1)
                    act.activation(f_h[t], f_h[t], ACT.Gelu).then_inc(f_gel, 1)
                    act.wait_ge(f_gel, t + 1)
                    act.activation(f_sq, f_h[t], ACT.Square, accum_out=sm[:, 216 + t:217 + t]).then_inc(f_hsq, 1)
                    act.wait_ge(f_hsq, t + 1)
                take_root()

                def f_scale(t):
                    act.activation(f_h[t], f_h[t], ACT.Copy, scale=rstd[:, t:t + 1]).then_inc(f_hr, 1)

                def f_integer(t):
                    act.wait_ge(f_hc, t + 1)
                    if t >= 2:
                        act.wait_ge(f_t, t - 1)
                    act.activation(f_hb[t % 2], f_h[t], ACT.Copy, bias=-MAGIC).then_inc(f_hbd, 1)

                def f_copy(t):
                    act.wait_ge(f_t, t + 1)
                    if t >= 2:
                        act.wait_ge(f_m2, t - 1)
                    copy(f_ht[t % 2][:, 0:8, :], v3(bank(4 * (t % 2)).bitcast(BF16), 8)).then_inc(f_hta, 1)

                act.wait_ge(f_ready, 1)
                f_scale(0)
                for t in range(NB):
                    if t + 1 < NB:
                        f_scale(t + 1)
                    f_integer(t)
                    if t:
                        f_copy(t - 1)
                f_copy(NB - 1)

        @block.vector
        def _(v):
            for signal in (c_t, c_gd, c_acc, d_pto, d_o):
                v.sem_inc(signal, AHEAD)
            count = [0]

            def link(ins):
                count[0] += 1
                ins.then_inc(dve, 1)
                v.wait_ge(dve, count[0])

            roots = [0]

            def inverse_root(ins, t=slice(0, NB)):
                roots[0] += 1
                ins.then_inc(root_asked, 1)
                v.wait_ge(root_done, roots[0])
                x, y, z = rstd[:, t], root[:, t], rtmp[:, t]
                link(v.reciprocal(y, y))
                link(v.tensor_tensor(z, y, y, ALU.mult))
                link(v.tensor_tensor(z, z, x, ALU.mult))
                link(v.tensor_scalar(z, z, -0.5, 1.5, ALU.mult, ALU.add))
                link(v.tensor_tensor(x, y, z, ALU.mult))

            def layernorm(n, rms=None):
                for t in range(NB):
                    last = v.bn_stats(st[:, t, :], X[:, t, :])
                link(last)
                for t in range(NB):
                    last = v.bn_aggr(mv[:, t, :], st[:, t, :])
                link(last)
                inverse_root(v.tensor_scalar(rstd[:, :], mv[:, :, 1], 1e-5, None, ALU.add))
                for t in range(NB):
                    last = v.tensor_scalar(Y[:, t, :], X[:, t, :], mv[:, t, 0:1], rstd[:, t:t + 1],
                                           ALU.subtract, ALU.mult)
                    if rms is None:
                        last.then_inc(ln_done, 1)
                if rms is None:
                    return
                link(last)
                for t in range(NB):
                    last = v.bn_stats(st[:, t, :], Y[:, t, :])
                link(last)
                for t in range(NB):
                    last = v.bn_aggr(mv[:, t, :], st[:, t, :])
                link(last)
                link(v.tensor_tensor(rstd[:, :], mv[:, :, 0], mv[:, :, 0], ALU.mult))
                inverse_root(v.scalar_tensor_tensor(rstd[:, :], rstd[:, :], rms, mv[:, :, 1], ALU.add, ALU.add))
                for t in range(NB):
                    v.tensor_scalar(Y[:, t, :], Y[:, t, :], rstd[:, t:t + 1], None, ALU.mult).then_inc(ln_done, 1)

            def xt_chunks(n):
                v.wait_ge(ln_turned, n + 1)
                for c in range(2, 4):
                    v.tensor_copy(XT[:, c, :], bank(c)).then_inc(xt_dve, 1)

            def out_chunks(n):
                v.wait_ge(o_turned, n + 1)
                for c in range(2, 4):
                    v.tensor_copy(XT[:, c, :], bank(c)).then_inc(o_dve, 1)

            def add_projection(n, first=4):
                for t in range(NB):
                    v.wait_ge(proj_done, NB * n + t + 1)
                    v.tensor_tensor(X[:, t, :], X[:, t, :], bank(first + t), ALU.add).then_inc(x_added, 1)
                v.wait_ge(x_added, NB * (n + 1))

            v.wait_ge(x_landed, 16)
            layernorm(0)
            xt_chunks(0)
            for oc in range(2, 4):
                v.wait_ge(a_qpd, oc + 1)
                v.tensor_copy(a_qp[:, oc, :], bank(oc)).then_inc(a_qpe_dve, 1)
            v.wait_ge(a_qb, 1)
            v.tensor_copy(sm[:, 0:4], bank(4)[:, 0:4]).then_inc(a_qpe_dve, 1)
            v.wait_ge(a_qpe_dve, 3)

            def a_take(b):
                link(v.tensor_tensor(sm[:, 24 + b:25 + b], sm[:, 16 + 2 * b:17 + 2 * b],
                                     sm[:, 17 + 2 * b:18 + 2 * b], ALU.add))
                link(v.reciprocal(sm[:, 28 + b:29 + b], sm[:, 24 + b:25 + b]))
                v.wait_ge(a_pv, 4 * (b + 1))
                v.tensor_scalar(a_ao[:, b, :], bank(4), sm[:, 28 + b:29 + b], None, ALU.mult).then_inc(a_o, 1)

            for b in range(NB):
                for f in range(2):
                    v.wait_ge(a_s, 4 * b + 2 * f + 2)
                    last = v.tensor_reduce(sm[:, 32 + 2 * b + f:33 + 2 * b + f], bank(2 * f, 2), AX, ALU.max)
                link(last)
                link(v.tensor_scalar(sm[:, 40 + b:41 + b], sm[:, 32 + 2 * b:33 + 2 * b], sm[:, 33 + 2 * b:34 + 2 * b],
                                     sm[:, b:b + 1], ALU.max, ALU.add))
                v.tensor_scalar(sm[:, 8 + b:9 + b], sm[:, 40 + b:41 + b], sm[:, b:b + 1], -1.0 / 32,
                                ALU.subtract, ALU.mult).then_inc(a_nb, 1)
                if b:
                    a_take(b - 1)
                for g in (1, 3):
                    v.wait_ge(a_t, 4 * b + g + 1)
                    v.tensor_copy(a_pt[:, 4 * g:4 * g + 4, :], v3(bank(6), 4)).then_inc(a_pto, 1)
                v.wait_ge(a_exp, 2 * b + 2)
            a_take(NB - 1)
            out_chunks(0)
            add_projection(0)

            if stages >= 2:
                layernorm(1)
                xt_chunks(1)
                v.wait_ge(bb_landed, 80)
                v.wait_ge(b_beta, 1)
                link(v.tensor_scalar(sm[:, 96:112], sm[:, 80:96], float(DH0) ** 0.5, None, ALU.mult))
                link(v.reciprocal(sm[:, 80:96], sm[:, 96:112]))
                for t in range(NB):
                    last = v.tensor_tensor(X[:, t, :], X[:, t, :], BI[:, 3 * D:4 * D], ALU.add)
                link(last)
                for m in range(2):
                    for t in range(NB):
                        n = 4 * m + t
                        v.wait_ge(b_p, n + 1)
                        v.tensor_tensor(b_z[:, n, :], bank(n), BI[:, D * m:D * (m + 1)], ALU.add).then_inc(b_zq, 1)
                    v.wait_ge(b_zq, 4 * (m + 1))
                    z4 = b_z[:, 4 * m:4 * m + 4, :].rearrange("p a (h d) -> p a h d", h=H0)
                    sc = sm[:, 80:96].unsqueeze(1).unsqueeze(3).broadcast_to([P, 4, H0, DH0])
                    v.tensor_tensor(z4, z4, sc, ALU.mult).then_inc(b_zs, 1)
                for t in range(NB):
                    v.wait_ge(b_p, 8 + t + 1)
                    v.tensor_tensor(b_v[:, t, :], bank(t), BI[:, 2 * D:3 * D], ALU.add).then_inc(b_zq, 1)
                for m in range(2):
                    hf = slice(2048 * m, 2048 * (m + 1))
                    v.wait_ge(b_u, 2 * m + 2)
                    v.tensor_scalar(b_s2[:, hf], b_s1[:, hf], 1.0, None, ALU.add).then_inc(b_w1p, 1)
                for m in range(2):
                    hf = slice(2048 * m, 2048 * (m + 1))
                    v.wait_ge(b_ln, m + 1)
                    link(v.scalar_tensor_tensor(b_s2[:, hf], b_s2[:, hf], -1.0, b_s1[:, hf], ALU.add, ALU.subtract))
                    link(v.tensor_tensor(b_s3[:, hf], b_s3[:, hf], b_s2[:, hf], ALU.subtract))
                    zf = fa(32 + 8 * m, 8)
                    link(v.scalar_tensor_tensor(zf, zf, 0.0, b_s3[:, hf], ALU.max, ALU.add))
                v.wait_ge(b_zq, 12)
                pr = v3(b_s1[:, 0:2048], 4)
                att = b_s2[:, 0:256].rearrange("p (s t h) -> p s t h", s=4, t=4)
                den = b_s2[:, 256:320].rearrange("p (s h) -> p s h", s=4)
                rden = b_s2[:, 320:384].rearrange("p (s h) -> p s h", s=4)
                for s in range(NB):
                    n = s + 1
                    link(v.tensor_tensor(pr[:, 0:n, :], b_z[:, s:s + 1, :].broadcast_to([P, n, D]), b_z[:, 4:4 + n, :],
                                         ALU.mult))
                    link(v.tensor_reduce(att[:, s, 0:n, :], pr[:, 0:n, :].rearrange("p a (h d) -> p a h d", h=H0),
                                         AX, ALU.add))
                    link(v.tensor_reduce(den[:, s, :], att[:, s, 0:n, :].rearrange("p t h -> p h t"), AX, ALU.add))
                    link(v.reciprocal(rden[:, s, :], den[:, s, :]))
                    link(v.tensor_tensor(pr[:, 0:n, :].rearrange("p a (h d) -> p a h d", h=H0),
                                         att[:, s, 0:n, :].unsqueeze(3).broadcast_to([P, n, H0, DH0]),
                                         b_v[:, 0:n, :].rearrange("p a (h d) -> p a h d", h=H0), ALU.mult))
                    link(v.tensor_reduce(b_ao[:, s, :], pr[:, 0:n, :].rearrange("p t n -> p n t"), AX, ALU.add))
                    o3 = b_ao[:, s, :].rearrange("p (h d) -> p h d", h=H0)
                    v.tensor_tensor(o3, o3, rden[:, s, :].unsqueeze(2).broadcast_to([P, H0, DH0]), ALU.mult) \
                        .then_inc(b_o, 1)
                out_chunks(1)
                add_projection(1)

            if stages >= 3:
                layernorm(2)
                xt_chunks(2)
                v.wait_ge(xt_dve, 6)
                v.wait_ge(xt_act, 6)
                v.wait_ge(c_xhd, 1)
                v.tensor_tensor(c_xl, XT[:, :, :], c_xh.bitcast(F32), ALU.subtract).then_inc(c_xld, 1)
                v.wait_ge(c_gate, 1)
                v.wait_ge(const_ready, N_CONST)
                gt = g_[:, 0:32].rearrange("p (t e) -> p t e", t=NB)
                oh = [g_[:, 32 * (i + 1):32 * (i + 2)].rearrange("p (t e) -> p t e", t=NB) for i in range(2)]
                g2 = g_[:, 96:128].rearrange("p (t e) -> p t e", t=NB)
                wt = g_[:, 128:160].rearrange("p (t e) -> p t e", t=NB)
                m12 = [sm[:, 100:104], sm[:, 104:108]]
                mxi = sm[:, 108:112]

                def over_e(ap):
                    return ap.unsqueeze(2).broadcast_to([P, NB, NE])

                rv = rev8[:, :].unsqueeze(1).broadcast_to([P, NB, NE])
                link(v.tensor_copy(gt, bank(7)[:, 0:NB * NE].rearrange("p (t e) -> p t e", t=NB)))
                src = gt
                for i in range(2):
                    link(v.tensor_reduce(m12[i], src, AX, ALU.max))
                    link(v.tensor_tensor(oh[i], src, over_e(m12[i]), ALU.is_equal))
                    link(v.tensor_tensor(oh[i], oh[i], rv, ALU.mult))
                    link(v.tensor_reduce(mxi, oh[i], AX, ALU.max))
                    link(v.tensor_tensor(oh[i], oh[i], over_e(mxi), ALU.is_equal))
                    if i == 0:
                        link(v.scalar_tensor_tensor(g2, oh[0], NEG, gt, ALU.mult, ALU.add))
                        src = g2
                v.tensor_tensor(sm[:, 116:120], m12[1], m12[0], ALU.subtract).then_inc(c_diff, 1)
                v.wait_ge(c_e, 1)
                link(v.tensor_scalar(sm[:, 112:116], sm[:, 120:124], 1.0, None, ALU.add))
                link(v.reciprocal(sm[:, 100:104], sm[:, 112:116]))
                link(v.tensor_tensor(sm[:, 104:108], sm[:, 100:104], sm[:, 120:124], ALU.mult))
                for i in range(2):
                    link(v.tensor_tensor(oh[i], oh[i], over_e(m12[i]), ALU.mult))
                link(v.tensor_tensor(wt, oh[0], oh[1], ALU.add))

                def c_low12(u, k):
                    v.wait_ge(c_hi12, u + 1)
                    v.tensor_tensor(c_wl[k % 2][:, 0:2, :], c_st[k % NST][:, 0:2, :],
                                    c_wh[k % 2][:, 0:2, :].bitcast(F32), ALU.subtract).then_inc(c_lo12, 1)

                def c_low3(u, k):
                    v.wait_ge(c_hi3, u + 1)
                    v.tensor_tensor(c_wl[k % 2][:, 2, :], c_st[k % NST][:, 2, :],
                                    c_wh[k % 2][:, 2, :].bitcast(F32), ALU.subtract).then_inc(c_lo3, 1)

                def c_unit(e, j, final=False):
                    u = e * UE + j
                    s = j % 2
                    if not final:
                        c_low12(e * UE + (j + 1), j + 1)
                    c_low3(u, j)
                    v.wait_ge(c_sig, u + 1)
                    v.tensor_tensor(c_tt, c_sg, bank(2 * s), ALU.mult).then_inc(c_t, 1)
                    v.wait_ge(c_t, u + 1 + AHEAD)
                    v.tensor_tensor(c_g, c_tt, bank(2 * s + 1), ALU.mult).then_inc(c_gd, 1)
                    v.wait_ge(c_gd, u + 1 + AHEAD)
                    v.tensor_copy(c_gh[s], c_g).then_inc(c_ghd, 1)
                    v.wait_ge(c_ghd, u + 1)
                    v.tensor_tensor(c_gl[s], c_g, c_gh[s].bitcast(F32), ALU.subtract).then_inc(c_gld, 1)

                def c_accumulate(e):
                    v.wait_ge(c_y, e * UE + UE + AHEAD)
                    for t in range(NB):
                        last = v.scalar_tensor_tensor(X[:, t, :], bank(4 + t), wt[:, t, bass.ds(e, 1)], X[:, t, :],
                                                      ALU.mult, ALU.add)
                    last.then_inc(c_acc, 1)
                    v.wait_ge(c_acc, e + 1 + AHEAD)

                def d_low_weights(i):
                    v.wait_ge(d_whd, 2 - i)
                    v.tensor_tensor(d_wl[i], d_ws[i], d_wh[i].bitcast(F32), ALU.subtract).then_inc(d_wld, 1)

                c_low12(0, 0)
                c_unit(0, 0)
                with v.Fori(0, NE - 1) as e:
                    for j in range(UE):
                        c_unit(e, j + 1)
                    c_accumulate(e)
                if stages >= 4:
                    d_low_weights(1)
                for j in range(1, UE):
                    c_unit(NE - 1, j, final=(j == UE - 1))
                c_accumulate(NE - 1)

            if stages >= 4:

                def d_low(n, s):
                    v.wait_ge(d_hi, n + 1)
                    v.tensor_tensor(d_cl[s], d_st[s], d_ch[s].bitcast(F32), ALU.subtract).then_inc(d_lo, 1)

                layernorm(3)
                d_low_weights(0)
                d_low(0, 0)
                xt_chunks(3)
                d_low(1, 1)

                def evac(b, h, g):
                    v.wait_ge(d_t, b * (4 * H0) + (4 * h + g + 1))
                    v.tensor_copy(d_pt[:, 4 * g:4 * g + 4, :], v3(bank(TB[g]), 4)).then_inc(d_pto, 1)

                def d_batch(b, final):
                    for c in range(NCH):
                        for j in range(4):
                            n = 8 * c + 2 * j + 1
                            v.wait_ge(d_pj, b * 32 + (n + 1))
                            v.tensor_copy(d_v[:, 4 * c + j, :], bank(n % 4)).then_inc(d_vev, 1)
                        if c < 2:
                            d_low(b * NCH + (c + 2), c)
                    for h in range(H0):
                        for c in range(NCH):
                            v.wait_ge(d_s, b * (4 * H0) + (4 * h + c + 1) + AHEAD)
                            v.tensor_reduce(sm[:, 130 + c:131 + c], bank(c), AX, ALU.max).then_inc(d_mx, 1)
                        v.wait_ge(d_mx, b * (5 * H0) + (5 * h + 4))
                        v.tensor_reduce(sm[:, 134:135], sm[:, 130:134], AX, ALU.max).then_inc(d_mx, 1)
                        v.wait_ge(d_mx, b * (5 * H0) + (5 * h + 5))
                        v.tensor_scalar(sm[:, 128 + h % 2:129 + h % 2], sm[:, 134:135],
                                        -float(DH0) ** -0.5, None, ALU.mult).then_inc(d_nb, 1)
                        if h:
                            evac(b, h - 1, 1)
                            evac(b, h - 1, 3)
                        if not final and h in (5, 10):
                            d_low(b * NCH + (NCH + h // 5 - 1), h // 5 - 1)
                    evac(b, H0 - 1, 1)
                    evac(b, H0 - 1, 3)
                    v.wait_ge(d_exp, b * (4 * H0) + 4 * H0 + AHEAD)
                    rs = sm[:, 136:200].rearrange("p (h c) -> p h c", c=NCH)
                    v.tensor_reduce(sm[:, 64:80], rs, AX, ALU.add).then_inc(d_sum, 1)
                    v.wait_ge(d_sum, b * 3 + 1)
                    v.reciprocal(sm[:, 80:96], sm[:, 64:80]).then_inc(d_sum, 1)
                    v.wait_ge(d_sum, b * 3 + 2)
                    v.tensor_copy(d_rx[:, :].rearrange("p (h d) -> p h d", h=H0),
                                  sm[:, 80:96].unsqueeze(2).broadcast_to([P, H0, DH0])).then_inc(d_rxd, 1)
                    v.wait_ge(d_rt, b + 1)
                    v.tensor_copy(d_rx[:, :], bank(7)).then_inc(d_sum, 1)
                    v.wait_ge(d_sum, b * 3 + 3)
                    v.wait_ge(d_pv, b * H0 + H0)
                    v.tensor_tensor(XT[:, :, bass.ds(b * P, P)], v3(bank(6), KC), v3(d_rx[:, :], KC), ALU.mult) \
                        .then_inc(d_o, 1)

                with v.Fori(0, NB - 1) as b:
                    d_batch(b, False)
                d_batch(NB - 1, True)
                add_projection(2, first=0)

            if stages >= 5:
                layernorm(4, rms=1.1920929e-07)
                xt_chunks(4)
                v.wait_ge(eb_landed, 32)
                for t in range(NB):
                    last = v.tensor_tensor(X[:, t, :], X[:, t, :], BI[:, DQ:DQ + D], ALU.add)
                link(last)
                for m in range(2):
                    for oc in range(1, 8, 2):
                        n = 8 * m + oc
                        v.wait_ge(e_pj, n + 1)
                        v.tensor_scalar((e_qt, e_kt)[m][:, oc, :], bank((4 + n) % 8),
                                        (bqc, bkc)[m][:, oc:oc + 1], None, ALU.add).then_inc(e_evd, 1)
                for n in range(8):
                    v.wait_ge(e_pj, 16 + n + 1)
                    f = n % 2
                    v.tensor_tensor(e_v[:, n // 2, D * f:D * (f + 1)], bank((4 + n) % 8), BI[:, D * f:D * (f + 1)],
                                    ALU.add).then_inc(e_evd, 1)

                def e_scale(b):
                    v.wait_ge(e_exp, 16 * (b + 1))
                    link(v.reciprocal(e_ri[:, 16 * b:16 * (b + 1)], e_rs[:, 16 * b:16 * (b + 1)]))
                    for f in range(2):
                        v4 = e_v[:, b, D * f:D * (f + 1)].rearrange("p (j q d) -> p j q d", j=4, q=2)
                        ri = e_ri[:, 16 * b + 8 * f:16 * b + 8 * f + 8].rearrange("p (q j) -> p j q", q=2)
                        last = v.tensor_tensor(v4, v4, ri.unsqueeze(3).broadcast_to([P, 4, 2, DH1]), ALU.mult)
                    last.then_inc(e_vs, 1)

                for g in range(16):
                    v.wait_ge(e_s, g + 1)
                    eg = e_e[:, 4 * g:4 * g + 4, :]
                    v.tensor_tensor(eg, v3(bank((4 + g) % 8), 4), caus[:, :].unsqueeze(1).broadcast_to([P, 4, P]),
                                    ALU.add).then_inc(e_m, 1)
                    v.wait_ge(e_m, g + 1)
                    v.tensor_reduce(e_nm[:, 4 * g:4 * g + 4], eg, AX, ALU.max, negate=True).then_inc(e_mx, 1)
                    if g % 4 == 1 and g > 4:
                        e_scale(g // 4 - 1)
                e_scale(3)
                v.wait_ge(e_z, 1)
                for i in range(1, 8, 2):
                    v.tensor_copy(e_zt[:, i, :], bank(i)).then_inc(e_zevd, 1)
                add_projection(3)

            if stages >= 6:
                layernorm(5, rms=1e-5)
                v.wait_ge(ln_done, 24)
                link(v.tensor_reduce(sm[:, 212:216], Y[:, :, :], AX, ALU.max, apply_absolute_value=True))

                def int8_scale(m, dq, dqs, n):
                    link(v.tensor_scalar(m, m, 1e-5, None, ALU.max))
                    link(v.reciprocal(dq, m))
                    v.tensor_scalar(dqs, m, 1.0 / 127.0, wmean[:, n:n + 1], ALU.mult, ALU.mult)
                    link(v.tensor_scalar(dq, dq, 127.0, None, ALU.mult))

                int8_scale(sm[:, 212:216], sm[:, 220:224], sm[:, 224:228], 0)
                for t in range(NB):
                    last = v.tensor_scalar(Y[:, t, :], Y[:, t, :], sm[:, 220 + t:221 + t], 127.0, ALU.mult, ALU.min)
                link(last)
                link(v.tensor_scalar(Y[:, :, :], Y[:, :, :], -128.0, MAGIC, ALU.max, ALU.add))
                v.tensor_scalar(f_yb, Y[:, :, :], MAGIC, None, ALU.subtract).then_inc(f_ybd, 1)
                v.wait_ge(fb_landed, 32)
                for t in range(NB):
                    last = v.tensor_tensor(X[:, t, :], X[:, t, :], d_rx[:, :], ALU.add)
                link(last)
                v.wait_ge(f_yt_t, 1)
                for i in range(2):
                    last = v.tensor_copy(f_yt[:, 2 * i:2 * i + 2, :], v3(bank(4 + i).bitcast(BF16), 2))
                last.then_inc(f_ytd, 1)

                def f_take(t):
                    v.wait_ge(f_m1, t + 1)
                    v.scalar_tensor_tensor(f_h[t], bank(4 * (t % 2), 4), sm[:, 224 + t:225 + t], f_b1,
                                           ALU.mult, ALU.add).then_inc(f_hd, 1)

                def f_max(t):
                    v.wait_ge(f_gel, t + 1)
                    return v.tensor_reduce(sm[:, 232 + t:233 + t], f_h[t], AX, ALU.max, apply_absolute_value=True)

                f_take(0)
                for t in range(1, NB):
                    f_take(t)
                    f_max(t - 1)
                link(f_max(NB - 1))
                v.wait_ge(f_hsq, NB)
                inverse_root(v.tensor_scalar(rstd[:, :], sm[:, 216:220], 1.0 / FF, 1e-5, ALU.mult, ALU.add))
                link(v.tensor_tensor(sm[:, 232:236], sm[:, 232:236], rstd[:, :], ALU.mult))
                v.sem_inc(f_ready, 1)
                int8_scale(sm[:, 232:236], sm[:, 244:248], sm[:, 248:252], 1)

                def f_round(t):
                    v.wait_ge(f_hr, t + 1)
                    link(v.tensor_scalar(f_h[t], f_h[t], sm[:, 244 + t:245 + t], 127.0, ALU.mult, ALU.min))
                    v.tensor_scalar(f_h[t], f_h[t], -128.0, MAGIC, ALU.max, ALU.add).then_inc(f_hc, 1)

                def f_copy(t):
                    v.wait_ge(f_t, t + 1)
                    if t >= 2:
                        v.wait_ge(f_m2, t - 1)
                    v.tensor_copy(f_ht[t % 2][:, 8:16, :], v3(bank(4 * (t % 2) + 1).bitcast(BF16), 8)).then_inc(f_htd, 1)

                def f_add(t):
                    v.wait_ge(f_m2, t + 1)
                    v.scalar_tensor_tensor(X[:, t, :], bank(4 * (t % 2) + 2), sm[:, 248 + t:249 + t], X[:, t, :],
                                           ALU.mult, ALU.add).then_inc(x_added, 1)

                f_round(0)
                for t in range(NB):
                    if t + 1 < NB:
                        f_round(t + 1)
                    f_copy(t)
                    if t:
                        f_add(t - 1)
                f_add(NB - 1)


def kernel(**inputs):
    import numpy as np
    import concourse.bacc as bacc
    from concourse.bass_utils import run_bass_kernel_spmd

    a = {k: np.asarray(v) for k, v in inputs.items()}

    def rows(w):
        return np.ascontiguousarray(w.reshape(-1, P, w.shape[1]).transpose(1, 0, 2))

    def columns(v):
        return v.reshape(-1, P).T

    c = a["ctx_1024"].reshape(NB * NCH, CH, D)
    qkv = a["L1_attn_W_qkv"].reshape(DQ, 3, D)
    bqkv = a["L1_attn_b_qkv"].reshape(DQ, 3)
    ins = {
        "x": a["x"],
        "ctx_n": c.reshape(NB * NCH, 4, P, D).transpose(0, 2, 1, 3),
        "ctx_t": c.transpose(0, 2, 1).reshape(NB * NCH, KC, P, CH).transpose(0, 2, 1, 3),
        "w1t": rows(a["L0_xattn_W1"].T), "w2n": rows(a["L0_xattn_W2"]), "w3t": rows(a["L0_xattn_W3"].T),
        "bcols": np.concatenate([columns(a["L0_xattn_b1"]), columns(a["L0_xattn_b2"]), columns(bqkv[:, 0]),
                                 columns(bqkv[:, 1]), np.zeros((P, 8), np.float32)], axis=1),
        "beta": a["L0_attn_beta"],
        "l0a_w": np.stack([rows(a[f"L0_attn_W{n}"].T) for n in "qkvo"]),
        "l0a_bq": a["L0_attn_bq"], "l0a_bk": a["L0_attn_bk"], "l0a_bv": a["L0_attn_bv"], "l0a_bo": a["L0_attn_bo"],
        "wgt": rows(a["L0_ffn_Wg"].T),
        "moe_w": np.stack([
            a["L0_ffn_W1"].reshape(NE * UE, P, KC, P).transpose(0, 3, 2, 1).reshape(NE * UE, P, D),
            a["L0_ffn_W2"].reshape(NE * UE, P, KC, P).transpose(0, 3, 2, 1).reshape(NE * UE, P, D),
            a["L0_ffn_W3"].reshape(NE, D, UE, P).transpose(0, 2, 3, 1).reshape(NE * UE, P, D)], axis=2),
        "l1x_w": np.stack([rows(a[f"L1_xattn_W{n}"].T) for n in "qkvo"]),
        "l1a_w": np.stack([rows(qkv[:, i].T) for i in range(3)]),
        "l1a_bv": bqkv[:, 2], "l1a_bo": a["L1_attn_b_o"], "l1a_wo": rows(a["L1_attn_W_o"].T),
        "w1t_f": rows(a["L1_ffn_w1"].T), "w2t_f": rows(a["L1_ffn_w2"].T),
        "l1f_b1": a["L1_ffn_b1"], "l1f_b2": a["L1_ffn_b2"],
    }
    nc = bacc.Bacc("TRN2", target_bir_lowering=False, num_devices=1)
    arrays, aps = {}, {}
    for name, v in ins.items():
        v = np.ascontiguousarray(v)
        arrays[f"in_{name}"] = v
        aps[name] = nc.dram_tensor(f"in_{name}", v.shape, mybir.dt.from_np(v.dtype), kind="ExternalInput").ap()
    out = nc.dram_tensor("out_x", (NB, P, D), F32, kind="ExternalOutput").ap()
    build(nc, aps, out)
    r = run_bass_kernel_spmd(nc, [arrays], core_ids=[0])
    return r.results[0]["out_x"]
```

```python
from contextlib import ExitStack

import concourse.bass as bass
from concourse import mybir
from concourse.alu_op_type import AluOpType as ALU

ACT = mybir.ActivationFunctionType
AX = mybir.AxisListType.X
F32 = mybir.dt.float32
F32R = mybir.dt.float32r
BF16 = mybir.dt.bfloat16

P = 128
D = 512
KC = D // P
NB = 4
T = NB * P
SK = 2048
CH = 512
NCH = SK // CH
NE = 8
HE = 1024
UE = HE // P
H0, DH0 = 16, 32
H1, DH1 = 16, 64
DQ = H1 * DH1
FF = 2048
FC = FF // P
KB = 256
MAGIC = 1.5 * 2.0 ** 23
NEG = -3.0e38
AHEAD = 2
LAST = 6


def build(nc, a, out, stages=LAST):
    ctx = ExitStack()
    with ctx:
        def sb(name, shape, dt=F32):
            return ctx.enter_context(nc.sbuf_tensor(name, shape, dt))

        def sem(name):
            return ctx.enter_context(nc.semaphore(name))

        X = sb("X", [P, NB, D])
        Y = sb("Y", [P, NB, D])
        XT = sb("XT", [P, KC, T])
        BI = sb("BI", [P, 8 * KB])
        FA = sb("FA", [P, 104 * KB])
        RA = sb("RA", [P, 64 * KB], F32R)
        ident = sb("ident", [P, P])
        identb = sb("identb", [P, P], BF16)
        caus = sb("caus", [P, P])
        rev8 = sb("rev8", [P, NE])
        st = sb("st", [P, NB, 6])
        mv = sb("mv", [P, NB, 2])
        rstd = sb("rstd", [P, NB])
        root = sb("root", [P, NB])
        rtmp = sb("rtmp", [P, NB])
        first_root = sb("first_root", [P, NB])
        sm = sb("sm", [P, 256])
        bcol = sb("bcol", [P, 32])
        PS = ctx.enter_context(nc.psum_tensor("PS", [P, 8 * 512], F32))

        TB = (4, 5, 7, 4)

        def bank(i, n=1):
            return PS[:, 512 * i:512 * (i + n)]

        def fa(kb, n):
            return FA[:, kb * KB:(kb + n) * KB]

        def ra(kb, n):
            return RA[:, kb * KB:(kb + n) * KB]

        def v3(ap, n):
            return ap.rearrange("p (a n) -> p a n", a=n)

        b1c, b2c = bcol[:, 0:4], bcol[:, 4:8]
        bqc, bkc = bcol[:, 8:16], bcol[:, 16:24]

        a_ct = [v3(fa(8 * i, 8), KC) for i in range(4)]
        a_cn = [v3(fa(32 + 8 * i, 8), 4) for i in range(4)]
        a_p = fa(64, 8)
        a_pt = v3(fa(72, 8), 16)
        a_qt = v3(fa(80, 8), KC)
        a_ao = v3(fa(80, 8), NB)
        a_wa = v3(fa(88, 8), KC)
        a_wb = v3(fa(96, 8), KC)
        a_qp = v3(BI[:, :], KC)
        b_w = [v3(fa(8 * i, 8), KC) for i in range(4)]
        b_z = v3(fa(32, 16), 8)
        b_v = v3(fa(48, 8), NB)
        b_s1, b_s2, b_s3 = fa(56, 16), fa(72, 16), fa(88, 16)
        b_ao = v3(fa(88, 8), NB)
        b_qks = [v3(fa(96, 6), 3), v3(fa(64, 8), 4)]
        NST = 4
        c_st = [v3(fa(6 * i, 6), 3) for i in range(NST)]
        c_sg, c_tt, c_g = fa(24, 2), fa(26, 2), fa(28, 2)
        c_wg = fa(30, 1)[:, 0:KC * NE].rearrange("p (k e) -> p k e", k=KC)
        c_xh, c_xl = v3(ra(0, 8), KC), v3(ra(8, 8), KC)
        c_wh = [v3(ra(16 + 12 * i, 6), 3) for i in range(2)]
        c_wl = [v3(ra(22 + 12 * i, 6), 3) for i in range(2)]
        c_gh = [ra(40 + 4 * i, 2) for i in range(2)]
        c_gl = [ra(42 + 4 * i, 2) for i in range(2)]
        d_st = [v3(fa(8 * i, 8), KC) for i in range(2)]
        d_kt = v3(fa(16, 32), KC)
        d_v = v3(fa(48, 32), 16)
        d_p = [fa(80 + 8 * i, 8) for i in range(2)]
        d_wq = v3(fa(80, 8), KC)
        d_ws = [v3(fa(48 + 8 * i, 8), KC) for i in range(2)]
        d_pt = v3(BI[:, :], 16)
        d_qz = v3(fa(96, 8), 16)
        d_wo = v3(fa(16, 8), KC)
        d_wh = [v3(ra(48 * i, 8), KC) for i in range(2)]
        d_wl = [v3(ra(8 + 48 * i, 8), KC) for i in range(2)]
        d_ch = [v3(ra(16 + 16 * i, 8), KC) for i in range(2)]
        d_cl = [v3(ra(24 + 16 * i, 8), KC) for i in range(2)]
        d_rx = sb("d_rx", [P, D])
        g_ = sb("per_token", [P, 192])
        e_w = [v3(fa(16 * i, 16), KC) for i in range(3)]
        e_qt, e_kt = v3(fa(48, 16), 8), v3(fa(64, 16), 8)
        e_v = v3(fa(80, 16), NB)
        e_wo = v3(fa(32, 16), 8)
        e_xh, e_xl = v3(ra(0, 8), KC), v3(ra(8, 8), KC)
        NSR = 4
        e_wh = [v3(ra(16 + 4 * i, 2), KC) for i in range(NSR)]
        e_wl = [v3(ra(18 + 4 * i, 2), KC) for i in range(NSR)]
        e_vh, e_vl = v3(ra(32, 16), KC), v3(ra(48, 16), KC)

        def e_e(i, n):
            return v3(fa(16 - 16 * (i // 32), 16), 32)[:, i % 32:i % 32 + n, :]

        e_zt = v3(fa(48, 16), 8)

        def e_head(g, j):
            return 8 * (g // 2) + 2 * j + g % 2

        def e_place(h):
            return 8 * (h // 8) + 4 * (h % 2) + h % 8 // 2

        e_nm, e_rs, e_ri = g_[:, 0:64], g_[:, 64:128], g_[:, 128:192]
        QC = 2048
        NQ = D * FF // P // QC
        q_w = [fa(31 + 32 * i, 32) for i in range(2)]
        q_abs, q_acc = fa(95, 4), fa(99, 4)
        q_all = v3(fa(95, 1), P)
        q_st = [fa(95 + 4 * i, 4).bitcast(BF16) for i in range(2)]
        wq = nc.dram_tensor("ternary_weights", (2, P, NQ * QC), BF16, kind="Internal").ap()
        wsum = nc.dram_tensor("weight_sums", (P, 2), F32, kind="Internal").ap()
        f_wb = [ra(16 * i, 16).bitcast(BF16) for i in range(2)]
        f_w1b, f_w2b = v3(f_wb[0], KC), v3(f_wb[1], FC)
        f_h = [fa(8 * i, 8) for i in range(NB)]
        f_sq = fa(32, 8)
        f_hb = [fa(40 + 4 * i, 4).bitcast(BF16) for i in range(2)]
        f_ht = [v3(fa(48 + 4 * i, 4).bitcast(BF16), FC) for i in range(2)]
        f_yb = v3(fa(56, 4).bitcast(BF16), NB)
        f_yt = v3(fa(60, 4).bitcast(BF16), KC)
        f_b1 = fa(96, 8)
        wmean = sm[:, 240:242]

        const_ready = sem("const_ready")
        const_step = sem("const_step")
        x_landed = sem("x_landed")
        out_stored = sem("out_stored")
        dve = sem("dve_chain")
        root_asked = sem("root_asked")
        root_done = sem("root_done")
        ln_done = sem("ln_done")
        ln_turned = sem("ln_turned")
        xt_act = sem("xt_act")
        xt_dve = sem("xt_dve")

        aw_landed = [sem(f"a_w{i}_landed") for i in range(3)]
        ab_landed = sem("a_b_landed")
        act_landed = [sem(f"a_ct{i}_landed") for i in range(4)]
        acn_landed = [sem(f"a_cn{i}_landed") for i in range(4)]
        a_q = sem("a_q")
        a_qev = sem("a_qev")
        a_qpd = sem("a_qpd")
        a_qb = sem("a_qb")
        a_qpe_act = sem("a_qpe_act")
        a_qpe_dve = sem("a_qpe_dve")
        a_s = sem("a_s")
        a_nb = sem("a_nb")
        a_exp = sem("a_exp")
        a_t = sem("a_t")
        a_pte = sem("a_pte")
        a_pto = sem("a_pto")
        a_pv = sem("a_pv")
        a_o = sem("a_o")
        o_turned = sem("o_turned")
        o_act = sem("o_act")
        o_dve = sem("o_dve")
        proj_done = sem("proj_done")
        x_added = sem("x_added")

        bw_landed = [sem(f"b_w{i}_landed") for i in range(4)]
        bb_landed = sem("b_b_landed")
        b_p = sem("b_p")
        b_zq = sem("b_zq")
        b_beta = sem("b_beta")
        b_zs = sem("b_zs")
        b_u = sem("b_u")
        b_w1p = sem("b_w1p")
        b_ln = sem("b_ln")
        b_o = sem("b_o")
        b_sp = sem("b_sp")
        b_qk = sem("b_qk")

        cg_landed = sem("c_wg_landed")
        c_landed = [sem(f"c_w{i}_landed") for i in range(NST)]
        c_gate = sem("c_gate")
        c_diff = sem("c_diff")
        c_e = sem("c_e")
        c_xhd = sem("c_xh_done")
        c_xld = sem("c_xl_done")
        c_hi12 = sem("c_hi12")
        c_lo12 = sem("c_lo12")
        c_hi3 = sem("c_hi3")
        c_lo3 = sem("c_lo3")
        c_h = sem("c_h")
        c_sig = sem("c_sig")
        c_t = sem("c_t")
        c_gd = sem("c_gd")
        c_ghd = sem("c_ghd")
        c_gld = sem("c_gld")
        c_y = sem("c_y")
        c_acc = sem("c_acc")

        dw_landed = [sem(f"d_w{i}_landed") for i in range(4)]
        d_landed = [sem(f"d_ct{i}_landed") for i in range(2)]
        d_whd = sem("d_whd")
        d_wld = sem("d_wld")
        d_hi = sem("d_hi")
        d_lo = sem("d_lo")
        d_q = sem("d_q")
        d_qev = sem("d_qev")
        d_zero = sem("d_zero")
        d_qzd = sem("d_qzd")
        d_pj = sem("d_pj")
        d_kev = sem("d_kev")
        d_vev = sem("d_vev")
        d_s = sem("d_s")
        d_mx = sem("d_mx")
        d_nb = sem("d_nb")
        d_exp = sem("d_exp")
        d_t = sem("d_t")
        d_pte = sem("d_pte")
        d_pto = sem("d_pto")
        d_pv = sem("d_pv")
        d_sum = sem("d_sum")
        d_rxd = sem("d_rxd")
        d_rt = sem("d_rt")
        d_o = sem("d_o")

        ew_landed = [sem(f"e_w{i}_landed") for i in range(4)]
        eb_landed = sem("e_b_landed")
        e_xhd = sem("e_xh_done")
        e_xld = sem("e_xl_done")
        e_whd = sem("e_wh_done")
        e_wld = sem("e_wl_done")
        e_vhd = sem("e_vh_done")
        e_vld = sem("e_vl_done")
        e_pj = sem("e_pj")
        e_eva = sem("e_eva")
        e_evd = sem("e_evd")
        e_s = sem("e_s")
        e_m = sem("e_m")
        e_mx = sem("e_mx")
        e_exp = sem("e_exp")
        e_vs = sem("e_vs")
        e_z = sem("e_z")
        e_zev = sem("e_zev")
        e_zevd = sem("e_zevd")

        fw_landed = [sem(f"f_w{i}_landed") for i in range(2)]
        fb_landed = sem("f_b_landed")
        q_landed = [sem(f"q_w{i}_landed") for i in range(3)]
        q_step = sem("q_step")
        q_sums = sem("q_sums")
        q_stored = [sem(f"q_stored{i}") for i in range(2)]
        q_done = sem("q_done")
        f_ybd = sem("f_ybd")
        f_yt_t = sem("f_yt_t")
        f_ytd = sem("f_ytd")
        f_m1 = sem("f_m1")
        f_hd = sem("f_hd")
        f_gel = sem("f_gel")
        f_hsq = sem("f_hsq")
        f_hbd = sem("f_hbd")
        f_t = sem("f_t")
        f_htd = sem("f_htd")
        f_m2 = sem("f_m2")

        block = ctx.enter_context(nc.Block())

        @block.sync
        def _(sp):
            sp.dma_start(X[:, :, :], a["x"].rearrange("b p d -> p b d")).then_inc(x_landed, 16)
            sp.dma_start(a_wa, a["w1t"]).then_inc(aw_landed[0], 16)
            sp.dma_start(bcol[:, :], a["bcols"]).then_inc(ab_landed, 16)
            sp.dma_start(a_wb, a["w2n"]).then_inc(aw_landed[1], 16)

            def a_load_t(b):
                for c in range(NCH):
                    if b:
                        sp.wait_ge(a_s, 4 * (b - 1) + c + 1)
                    sp.dma_start(a_ct[c], a["ctx_t"][NCH * b + c]).then_inc(act_landed[c], 16)

            a_load_t(0)
            sp.wait_ge(a_q, 4)
            sp.dma_start(a_wa, a["w3t"]).then_inc(aw_landed[2], 16)
            for b in range(NB):
                if 0 < b < NB - 1:
                    a_load_t(b + 1)
                for c in range(NCH):
                    if b:
                        sp.wait_ge(a_pv, 4 * (b - 1) + c + 1)
                    sp.dma_start(a_cn[c], a["ctx_n"][NCH * b + c]).then_inc(acn_landed[c], 16)
                if b == 0:
                    a_load_t(1)
            if stages >= 2:
                for i in range(4):
                    sp.wait_ge(a_s, 4 * (NB - 1) + i + 1)
                    sp.dma_start(b_w[i], a["l0a_w"][i]).then_inc(bw_landed[i], 16)
                sp.wait_ge(a_s, 16)
                for i, name in enumerate(("l0a_bq", "l0a_bk", "l0a_bv", "l0a_bo")):
                    sp.dma_start(BI[:, D * i:D * (i + 1)], a[name].partition_broadcast(P)).then_inc(bb_landed, 16)
                sp.dma_start(sm[:, 64:80], a["beta"].partition_broadcast(P)).then_inc(bb_landed, 16)
            if stages >= 3:
                sp.wait_ge(b_p, 12)
                for u in range(NST):
                    sp.dma_start(c_st[u], a["moe_w"][u]).then_inc(c_landed[u], 16)
                sp.wait_ge(proj_done, 8)
                sp.dma_start(c_wg, a["wgt"]).then_inc(cg_landed, 16)
                with sp.Fori(1, NE * UE // NST) as q:
                    for j in range(NST):
                        sp.wait_ge(c_lo3, q * NST + (j - NST + 1))
                        sp.dma_start(c_st[j].unsqueeze(1), a["moe_w"][bass.ds(q * NST + j, 1)].rearrange(
                            "u p a n -> p u a n")).then_inc(c_landed[j], 16)
            if stages >= 4:
                sp.wait_ge(c_lo3, NE * UE)
                for j in range(2):
                    sp.dma_start(d_st[j], a["ctx_t"][j]).then_inc(d_landed[j], 16)
                with sp.Fori(1, NB * NCH // 2) as q:
                    for j in range(2):
                        sp.wait_ge(d_lo, q * 2 + (j - 1))
                        sp.dma_start(d_st[j].unsqueeze(1), a["ctx_t"][bass.ds(q * 2 + j, 1)].rearrange(
                            "u p a n -> p u a n")).then_inc(d_landed[j], 16)
                sp.wait_ge(d_s, 4 * H0 * NB + AHEAD)
                sp.dma_start(d_wo, a["l1x_w"][3]).then_inc(dw_landed[3], 16)
            if stages >= 5:
                sp.wait_ge(d_lo, NB * NCH)
                sp.dma_start(e_w[0], a["l1a_w"][0]).then_inc(ew_landed[0], 16)
                sp.wait_ge(proj_done, 12)
                for i in range(1, 3):
                    sp.dma_start(e_w[i], a["l1a_w"][i]).then_inc(ew_landed[i], 16)
                sp.dma_start(BI[:, 0:DQ], a["l1a_bv"].partition_broadcast(P)).then_inc(eb_landed, 16)
                sp.dma_start(BI[:, DQ:DQ + D], a["l1a_bo"].partition_broadcast(P)).then_inc(eb_landed, 16)
                sp.wait_ge(e_pj, 24)
                sp.dma_start(e_wo, a["l1a_wo"]).then_inc(ew_landed[3], 16)
            if stages >= 6:
                sp.dma_start(f_b1, a["l1f_b1"].partition_broadcast(P)).then_inc(fb_landed, 16)
                sp.dma_start(d_rx[:, :], a["l1f_b2"].partition_broadcast(P)).then_inc(fb_landed, 16)
                sp.wait_ge(e_pj, 24)
                sp.wait_ge(q_done, 1)
                for i in range(2):
                    sp.dma_start(f_wb[i], wq[i]).then_inc(fw_landed[i], 16)
                for t in range(NB):
                    sp.wait_ge(x_added, 16 + t + 1)
                    sp.dma_start(out[t], X[:, t, :]).then_inc(out_stored, 16)
                sp.wait_ge(out_stored, 16 * NB)
                return
            sp.wait_ge(x_added, 4 * stages if stages < 3 else 4 * (stages - 1))
            if stages == 3:
                sp.wait_ge(c_acc, NE + AHEAD)
            sp.dma_start(out.rearrange("b p d -> p b d"), X[:, :, :]).then_inc(out_stored, 16)
            sp.wait_ge(out_stored, 16)

        @block.gpsimd
        def _(pool):
            pool.memset(ident[:, :], 0.0).then_inc(const_step, 1)
            pool.memset(caus[:, :], 0.0).then_inc(const_step, 1)
            for e in range(NE):
                pool.memset(rev8[:, e:e + 1], float(NE - e)).then_inc(const_ready, 1)
            pool.wait_ge(const_step, 2)
            pool.affine_select(out=ident[:, :], in_=ident[:, :], compare_op=ALU.not_equal, fill=1.0, base=0,
                               pattern=[[-1, P]], channel_multiplier=1).then_inc(const_step, 1)
            pool.affine_select(out=caus[:, :], in_=caus[:, :], compare_op=ALU.is_ge, fill=NEG, base=0,
                               pattern=[[1, P]], channel_multiplier=-1).then_inc(const_ready, 1)
            pool.wait_ge(const_step, 3)
            pool.tensor_copy(identb[:, :], ident[:, :]).then_inc(const_ready, 1)
            if stages >= 2:
                pool.wait_ge(b_sp, 2)
                for s in range(2, NB):
                    n = s + 1
                    pool.tensor_tensor(b_qks[s - 2], b_z[:, s:s + 1, :].broadcast_to([P, n, D]), b_z[:, 4:4 + n, :],
                                       ALU.mult).then_inc(b_qk, 1)
            if stages >= 4:
                pool.wait_ge(proj_done, 8)
            if stages >= 6:
                steps = [0]

                def q_link(ins):
                    steps[0] += 1
                    ins.then_inc(q_step, 1)
                    pool.wait_ge(q_step, steps[0])

                def q_load(k):
                    i, part = k // NQ, slice(QC * (k % NQ), QC * (k % NQ + 1))
                    src = a[("w1t_f", "w2t_f")[i]].rearrange("p a n -> p (a n)")
                    pool.dma_start(q_w[i][:, part], src[:, part]).then_inc(q_landed[k % 3], 16)

                half = QC // 2
                for k in range(3):
                    q_load(k)
                for k in range(2 * NQ):
                    pool.wait_ge(q_landed[k % 3], 16 * (k // 3 + 1))
                    for f in range(2):
                        o = QC * (k % NQ) + half * f
                        w = q_w[k // NQ][:, o:o + half]
                        first = k % NQ == 0 and f == 0
                        q_link(pool.tensor_scalar(q_abs, w, 0.0, 2.0, ALU.max, ALU.mult))
                        q_link(pool.tensor_tensor(q_acc if first else q_abs, q_abs, w, ALU.subtract))
                        if not first:
                            q_link(pool.tensor_tensor(q_acc, q_acc, q_abs, ALU.add))
                    if k + 3 < 2 * NQ:
                        q_load(k + 3)
                    if k % NQ == NQ - 1:
                        n, i = half // 2, k // NQ
                        while n:
                            dst = q_acc[:, 0:n] if n > 1 else sm[:, 200 + i:201 + i]
                            q_link(pool.tensor_tensor(dst, q_acc[:, 0:n], q_acc[:, n:2 * n], ALU.add))
                            n //= 2
                pool.dma_start(wsum, sm[:, 200:202]).then_inc(q_sums, 16)
                pool.wait_ge(q_sums, 16)
                pool.dma_start(fa(95, 1), wsum.rearrange("p i -> (p i)").partition_broadcast(P)).then_inc(q_sums, 16)
                pool.wait_ge(q_sums, 32)
                n = P // 2
                while n:
                    q_link(pool.tensor_tensor(q_all[:, 0:n, :], q_all[:, 0:n, :], q_all[:, n:2 * n, :], ALU.add))
                    n //= 2
                q_link(pool.tensor_scalar(wmean, q_all[:, 0, :], 1.0 / (D * FF), 1e-5, ALU.mult, ALU.max))
                pool.tensor_scalar(sm[:, 204:206], wmean, 0.5, None, ALU.mult)
                q_link(pool.tensor_scalar(sm[:, 206:208], wmean, -0.5, None, ALU.mult))
                for k in range(2 * NQ):
                    i, part = k // NQ, slice(QC * (k % NQ), QC * (k % NQ + 1))
                    if k >= 2:
                        pool.wait_ge(q_stored[k % 2], 16 * (k // 2))
                    w = q_w[i][:, part]
                    q_link(pool.tensor_scalar(q_st[k % 2], w, sm[:, 204 + i:205 + i], 1.0, ALU.is_gt, ALU.subtract))
                    q_link(pool.tensor_scalar(w, w, sm[:, 206 + i:207 + i], None, ALU.is_ge))
                    q_link(pool.tensor_tensor(q_st[k % 2], q_st[k % 2], w, ALU.add))
                    pool.dma_start(wq[i][:, part], q_st[k % 2]).then_inc(q_stored[k % 2], 16)
                for i in range(2):
                    pool.wait_ge(q_stored[i], 16 * NQ)
                pool.sem_inc(q_done, 1)
            if stages >= 4:
                for i in range(2):
                    pool.dma_start(d_ws[i], a["l1x_w"][1 + i]).then_inc(dw_landed[1 + i], 16)
                pool.dma_start(d_wq, a["l1x_w"][0]).then_inc(dw_landed[0], 16)
                pool.memset(fa(96, 8), 0.0).then_inc(d_zero, 1)
                pool.wait_ge(d_zero, 1)
                pool.wait_ge(d_qev, 4)
                with pool.Fori(0, NB) as b:
                    pool.wait_ge(d_s, b * (4 * H0) + AHEAD)
                    for j in range(4):
                        dst = d_qz.rearrange("p (g j) n -> p g j n", j=4)[32 * j:32 * j + 32, :, j, :]
                        pool.tensor_copy(dst, Y[32 * j:32 * j + 32, :, bass.ds(b * P, P)]).then_inc(d_qzd, 1)

        N_CONST = NE + 2

        @block.tensor
        def _(pe):
            for signal in (c_h, c_y, d_s):
                pe.sem_inc(signal, AHEAD)
            def turn_tokens(n):
                for t in range(NB):
                    pe.wait_ge(ln_done, NB * n + t + 1)
                    for c in range(KC):
                        last = pe.transpose(bank(c)[:, P * t:P * (t + 1)], Y[:, t, P * c:P * (c + 1)], ident[:, :])
                last.then_inc(ln_turned, 1)

            def wait_xt(n):
                pe.wait_ge(xt_act, 2 * n + 2)
                pe.wait_ge(xt_dve, 2 * n + 2)

            def gemm(dst, lhs, rhs, k):
                for i in range(k):
                    last = pe.matmul(dst, lhs(i), rhs(i), start=(i == 0), stop=(i == k - 1))
                return last

            def three(dst, k, lh, ll, rh, rl):
                for i in range(k):
                    pe.matmul(dst, lh(i), rh(i), start=(i == 0), stop=False)
                    pe.matmul(dst, lh(i), rl(i), start=False, stop=False)
                    last = pe.matmul(dst, ll(i), rh(i), start=False, stop=(i == k - 1))
                return last

            def turn_out(src, n):
                for t in range(NB):
                    for c in range(KC):
                        last = pe.transpose(bank(c)[:, P * t:P * (t + 1)], src[:, t, P * c:P * (c + 1)], ident[:, :])
                last.then_inc(o_turned, 1)

            def project_out(w, k, src=XT, first=4):
                for t in range(NB):
                    gemm(bank(first + t), lambda i: src[:, i, P * t:P * (t + 1)], lambda i: w[:, i, :], k) \
                        .then_inc(proj_done, 1)

            pe.wait_ge(const_ready, N_CONST)
            turn_tokens(0)
            pe.wait_ge(aw_landed[0], 16)
            wait_xt(0)
            for oc in range(KC):
                gemm(bank(4 + oc), lambda i: a_wa[:, i, P * oc:P * (oc + 1)], lambda i: XT[:, i, :], KC).then_inc(a_q, 1)
            pe.wait_ge(a_qev, 4)
            pe.wait_ge(aw_landed[1], 16)
            for oc in range(KC):
                gemm(bank(oc), lambda i: a_wb[:, i, P * oc:P * (oc + 1)], lambda i: a_qt[:, i, :], KC).then_inc(a_qpd, 1)
            for t in range(NB):
                last = gemm(bank(4)[:, t:t + 1], lambda i: a_qt[:, i, P * t:P * (t + 1)],
                            lambda i: b2c[:, i:i + 1], KC)
            last.then_inc(a_qb, 1)
            pe.wait_ge(a_qpe_act, 2)
            pe.wait_ge(a_qpe_dve, 3)

            def a_scores(b):
                for c in range(NCH):
                    pe.wait_ge(act_landed[c], 16 * (b + 1))
                    if b:
                        pe.wait_ge(a_exp, 2 * (b - 1) + 1 + c // 2)
                    gemm(bank(c), lambda i: a_qp[:, i, P * b:P * (b + 1)], lambda i: a_ct[c][:, i, :], KC).then_inc(a_s, 1)

            def a_turn(b):
                for g in range(4):
                    pe.wait_ge(a_exp, 2 * b + 1 + g // 2)
                    if 2 * b + g // 2 > 0:
                        pe.wait_ge(a_pto if g % 2 else a_pte, 2 * b + g // 2)
                    for j in range(4):
                        last = pe.transpose(bank(5 + g % 2)[:, P * j:P * (j + 1)],
                                            a_p[:, CH * g + P * j:CH * g + P * (j + 1)], ident[:, :])
                    last.then_inc(a_t, 1)

            def a_mix(b):
                if b:
                    pe.wait_ge(a_o, b)
                for g in range(4):
                    pe.wait_ge(a_pto if g % 2 else a_pte, 2 * b + g // 2 + 1)
                    pe.wait_ge(acn_landed[g], 16 * (b + 1))
                    for j in range(4):
                        last = pe.matmul(bank(4), a_pt[:, 4 * g + j, :], a_cn[g][:, j, :],
                                         start=(g == 0 and j == 0), stop=(g == 3 and j == 3))
                    last.then_inc(a_pv, 1)

            a_scores(0)
            a_turn(0)
            for b in range(1, NB):
                a_scores(b)
                a_mix(b - 1)
                a_turn(b)
            a_mix(NB - 1)
            pe.wait_ge(a_o, NB)
            turn_out(a_ao, 0)
            pe.wait_ge(o_act, 2)
            pe.wait_ge(o_dve, 2)
            pe.wait_ge(aw_landed[2], 16)
            project_out(a_wa, KC)

            if stages >= 2:
                turn_tokens(1)
                wait_xt(1)
                for m in range(3):
                    pe.wait_ge(bw_landed[m], 16)
                    for t in range(NB):
                        n = 4 * m + t
                        if m == 1:
                            pe.wait_ge(x_added, t + 1)
                        if m == 2:
                            pe.wait_ge(b_zq, t + 1)
                        gemm(bank(n % 8), lambda i: XT[:, i, P * t:P * (t + 1)], lambda i: b_w[m][:, i, :], KC) \
                            .then_inc(b_p, 1)
                pe.wait_ge(b_o, NB)
                turn_out(b_ao, 1)
                pe.wait_ge(o_act, 4)
                pe.wait_ge(o_dve, 4)
                pe.wait_ge(bw_landed[3], 16)
                project_out(b_w[3], KC)

            if stages >= 3:
                turn_tokens(2)
                wait_xt(2)
                pe.wait_ge(cg_landed, 16)
                for t in range(NB):
                    last = gemm(bank(7)[:, NE * t:NE * (t + 1)], lambda i: XT[:, i, P * t:P * (t + 1)],
                                lambda i: c_wg[:, i, :], KC)
                last.then_inc(c_gate, 1)
                pe.wait_ge(c_xld, 1)

                def c_hidden(before, j):
                    s = j % 2
                    pe.wait_ge(c_lo12, before + (j + 1))
                    if j:
                        pe.wait_ge(c_gd, before + (j - 1) + AHEAD)
                    for m in range(2):
                        w = lambda x, i: x[s][:, m, P * i:P * (i + 1)]
                        last = three(bank(2 * s + m), KC, lambda i: w(c_wh, i), lambda i: w(c_wl, i),
                                     lambda i: c_xh[:, i, :], lambda i: c_xl[:, i, :])
                    last.then_inc(c_h, 1)

                def c_out(u, j):
                    s = j % 2
                    pe.wait_ge(c_gld, u + 1)
                    pe.wait_ge(c_lo3, u + 1)
                    for t in range(NB):
                        tk = slice(P * t, P * (t + 1))
                        pe.matmul(bank(4 + t), c_gh[s][:, tk], c_wh[s][:, 2, :], start=(j == 0), stop=False)
                        pe.matmul(bank(4 + t), c_gh[s][:, tk], c_wl[s][:, 2, :], start=False, stop=False)
                        last = pe.matmul(bank(4 + t), c_gl[s][:, tk], c_wh[s][:, 2, :], start=False, stop=(j == UE - 1))
                    last.then_inc(c_y, 1)

                def c_expert(e, final):
                    for j in range(UE):
                        if not (final and j == UE - 1):
                            c_hidden(e * UE, j + 1)
                        if j == 0:
                            pe.wait_ge(c_acc, e + AHEAD)
                        c_out(e * UE + j, j)

                c_hidden(0, 0)
                pe.wait_ge(c_e, 1)
                with pe.Fori(0, NE - 1) as e:
                    c_expert(e, False)
                c_expert(NE - 1, True)

            if stages >= 4:
                turn_tokens(3)
                wait_xt(3)
                pe.wait_ge(dw_landed[0], 16)
                for oc in range(KC):
                    gemm(bank(4 + oc), lambda i: d_wq[:, i, P * oc:P * (oc + 1)], lambda i: XT[:, i, :], KC) \
                        .then_inc(d_q, 1)
                pe.wait_ge(d_wld, 2)

                def d_keys(c, j, bank_of):
                    s = c % 2
                    w = lambda x, i: x[0][:, i, P * j:P * (j + 1)]
                    three(bank_of, KC, lambda i: w(d_wh, i), lambda i: w(d_wl, i),
                          lambda i: d_ch[s][:, i, :], lambda i: d_cl[s][:, i, :]).then_inc(d_pj, 1)

                def d_values(c, j, bank_of):
                    s, k = c % 2, slice(P * j, P * (j + 1))
                    three(bank_of, KC, lambda i: d_ch[s][:, i, k], lambda i: d_cl[s][:, i, k],
                          lambda i: d_wh[1][:, i, :], lambda i: d_wl[1][:, i, :]).then_inc(d_pj, 1)

                def d_first_keys(before, chunk, j):
                    pe.wait_ge(d_lo, chunk)
                    pe.wait_ge(d_exp, before + (j + 1) + AHEAD)
                    d_keys(0, j, bank(j))

                def d_project(b):
                    for j in range(2, 4):
                        pe.wait_ge(d_exp, b * (4 * H0) + AHEAD)
                        d_keys(0, j, bank(j))
                    for j in range(4):
                        pe.wait_ge(d_kev, b * 16 + (j + 1))
                        d_values(0, j, bank(j))
                    for c in range(1, NCH - 1):
                        pe.wait_ge(d_lo, b * NCH + (c + 1))
                        for j in range(4):
                            for m in range(2):
                                n = 8 * c + 2 * j + m
                                if n < 12:
                                    pe.wait_ge(d_vev, b * 16 + (n - 7))
                                else:
                                    pe.wait_ge(d_vev if m else d_kev, b * 16 + (n // 2 - 1))
                                (d_values if m else d_keys)(c, j, bank(n % 4))
                    pe.wait_ge(d_lo, b * NCH + NCH)
                    for j in range(4):
                        pe.wait_ge(d_vev if j % 2 else d_kev, b * 16 + (11 + j // 2))
                        d_keys(NCH - 1, j, bank(j))
                    pe.wait_ge(d_o, b + AHEAD)
                    for j in range(2):
                        d_values(NCH - 1, j, bank(4 + j))

                def score(b, h, c):
                    if h:
                        pe.wait_ge(d_exp, b * (4 * H0) + (4 * (h - 1) + c + 1) + AHEAD)
                    pe.matmul(bank(c), d_qz[:, h, :], d_kt[:, h // 4, CH * c:CH * (c + 1)],
                              start=True, stop=True).then_inc(d_s, 1)

                def turn(b, h, g):
                    pe.wait_ge(d_exp, b * (4 * H0) + (4 * h + g + 1) + AHEAD)
                    if g == 3:
                        pe.wait_ge(d_pte, b * (2 * H0) + (2 * h + 1) + AHEAD)
                    else:
                        pe.wait_ge((d_pto, d_pto, d_pte)[g], b * (2 * H0) + 2 * h + AHEAD)
                    for j in range(4):
                        last = pe.transpose(bank(TB[g])[:, P * j:P * (j + 1)],
                                            d_p[h % 2][:, CH * g + P * j:CH * g + P * (j + 1)], ident[:, :])
                    last.then_inc(d_t, 1)

                def mix(b, h, g):
                    r, q = 32 * (h % 4), P * (h // 4)
                    pe.wait_ge(d_pto if g % 2 else d_pte, b * (2 * H0) + (2 * h + g // 2 + 1) + AHEAD)
                    for j in range(4):
                        last = pe.matmul(bank(6)[r:r + 32, q:q + P], d_v[:, 4 * g + j, DH0 * h:DH0 * (h + 1)],
                                         d_pt[:, 4 * g + j, :], start=(g == 0 and j == 0),
                                         stop=(g == 3 and j == 3))
                    if g == 3:
                        last.then_inc(d_pv, 1)

                def d_batch(b, final):
                    d_project(b)
                    pe.wait_ge(d_kev, b * 16 + 16)
                    pe.wait_ge(d_qzd, b * 4 + 4)
                    for h in range(H0):
                        for c in range(NCH):
                            score(b, h, c)
                            if h >= 2:
                                mix(b, h - 2, c)
                        if h == 0:
                            for j in range(2, 4):
                                d_values(NCH - 1, j, bank(4 + j))
                        if h == 1:
                            pe.wait_ge(d_vev, b * 16 + 16)
                        if h:
                            for g in range(4):
                                turn(b, h - 1, g)
                    for g in range(4):
                        mix(b, H0 - 2, g)
                    if not final:
                        d_first_keys(b * (4 * H0) + 4 * (H0 - 1), b * NCH + (NCH + 1), 0)
                    for g in range(4):
                        turn(b, H0 - 1, g)
                    if not final:
                        d_first_keys(b * (4 * H0) + 4 * (H0 - 1), b * NCH + (NCH + 1), 1)
                    for g in range(4):
                        mix(b, H0 - 1, g)
                    pe.wait_ge(d_rxd, b + 1)
                    for g in range(KC):
                        last = pe.transpose(bank(7)[:, P * g:P * (g + 1)], d_rx[:, P * g:P * (g + 1)], ident[:, :])
                    last.then_inc(d_rt, 1)
                pe.wait_ge(d_lo, 1)
                for j in range(2):
                    d_keys(0, j, bank(j))
                with pe.Fori(0, NB - 1) as b:
                    d_batch(b, False)
                d_batch(NB - 1, True)
                pe.wait_ge(d_o, NB + AHEAD)
                pe.wait_ge(dw_landed[3], 16)
                project_out(d_wo, KC, first=0)

            if stages >= 5:
                pe.wait_ge(x_added, 12)
                turn_tokens(4)
                pe.wait_ge(e_xld, KC)
                for n in range(16):
                    pe.wait_ge(e_wld, n + 1)
                    if n >= 8:
                        pe.wait_ge(e_evd if n % 2 else e_eva, (n - 8) // 2 + 1)
                    three(bank((4 + n) % 8), KC, lambda i: e_wh[n % NSR][:, i, :], lambda i: e_wl[n % NSR][:, i, :],
                          lambda i: e_xh[:, i, :], lambda i: e_xl[:, i, :]).then_inc(e_pj, 1)

                def e_values(n):
                    t, f = n // 2, n % 2
                    if n < 2:
                        pe.wait_ge(e_evd if n else e_eva, 7)
                    elif n >= 4:
                        pe.wait_ge(e_evd, 8 + n - 3)
                    pe.wait_ge(e_vld, f + 1)
                    tk, half = slice(P * t, P * (t + 1)), slice(D * f, D * (f + 1))
                    three(bank(n % 4), KC, lambda i: e_xh[:, i, tk], lambda i: e_xl[:, i, tk],
                          lambda i: e_vh[:, i, half], lambda i: e_vl[:, i, half]).then_inc(e_pj, 1)

                e_values(0)
                e_values(1)
                pe.wait_ge(e_eva, 8)
                pe.wait_ge(e_evd, 8)
                for g in range(16):
                    if g >= 4:
                        pe.wait_ge(e_m, g - 3)
                    for j in range(4):
                        b, h = g // 4, e_head(g % 4, j)
                        r = slice(64 * (h % 2), 64 * (h % 2) + 64)
                        tk = slice(P * b, P * (b + 1))
                        last = pe.matmul(bank(4 + g % 4)[:, P * j:P * (j + 1)], e_kt[r, h // 2, tk],
                                         e_qt[r, h // 2, tk], start=True, stop=True)
                    last.then_inc(e_s, 1)
                    if g % 2 and g < 12:
                        e_values(2 + g // 2)
                pe.wait_ge(e_m, 16)
                pe.wait_ge(e_evd, 16)
                for b in range(NB):
                    pe.wait_ge(e_vs, b + 1)
                    for h in range(H1):
                        r = 64 * (h % 2)
                        last = pe.matmul(bank(h // 2)[r:r + 64, P * b:P * (b + 1)], e_v[:, b, DH1 * h:DH1 * (h + 1)],
                                         e_e(H1 * b + e_place(h), 1)[:, 0, :], start=True, stop=True)
                last.then_inc(e_z, 1)
                pe.wait_ge(e_zev, 4)
                pe.wait_ge(e_zevd, 4)
                pe.wait_ge(ew_landed[3], 16)
                project_out(e_wo, 8, src=e_zt, first=4)

            if stages >= 6:
                yt_ps = [bank(4 + i).bitcast(BF16) for i in range(2)]
                for t in range(NB):
                    pe.wait_ge(f_ybd, t // 2 + 1)
                    for c in range(KC):
                        last = pe.transpose(yt_ps[c // 2][:, 512 * (c % 2) + P * t:512 * (c % 2) + P * (t + 1)],
                                            f_yb[:, t, P * c:P * (c + 1)], identb[:, :])
                last.then_inc(f_yt_t, 1)
                pe.wait_ge(f_ytd, 1)

                pe.wait_ge(fw_landed[0], 16)
                for t in range(NB):
                    if t >= 2:
                        pe.wait_ge(f_hd, t - 1)
                    for f in range(4):
                        gemm(bank(4 * (t % 2) + f), lambda i: f_yt[:, i, P * t:P * (t + 1)],
                             lambda i: f_w1b[:, i, 512 * f:512 * (f + 1)], KC).then_inc(f_m1, 1)
                pe.wait_ge(fw_landed[1], 16)
                pe.wait_ge(f_hd, NB)

                def f_turn(t):
                    pe.wait_ge(f_hbd, t + 1)
                    tp = [bank(4 * (t % 2) + i).bitcast(BF16) for i in range(2)]
                    for j in range(FC):
                        last = pe.transpose(tp[j // 8][:, P * (j % 8):P * (j % 8 + 1)],
                                            f_hb[t % 2][:, P * j:P * (j + 1)], identb[:, :])
                    last.then_inc(f_t, 1)

                def f_down(t):
                    pe.wait_ge(f_htd, 2 * t + 2)
                    if t >= 2:
                        pe.wait_ge(x_added, 16 + t - 1)
                    gemm(bank(4 * (t % 2) + 2), lambda i: f_ht[t % 2][:, i, :], lambda i: f_w2b[:, i, :], FC) \
                        .then_inc(f_m2, 1)

                f_turn(0)
                for t in range(NB):
                    if t + 1 < NB:
                        f_turn(t + 1)
                    f_down(t)

        @block.scalar
        def _(act):
            for signal in (d_exp, d_pte):
                act.sem_inc(signal, AHEAD)
            def copy(dst, src):
                return act.activation(dst, src, ACT.Copy)

            roots = [0]

            def take_root(t=slice(0, NB)):
                roots[0] += 1
                act.wait_ge(root_asked, roots[0])
                act.activation(root[:, t], rstd[:, t], ACT.Sqrt).then_inc(root_done, 1)

            def xt_chunks(n):
                act.wait_ge(ln_turned, n + 1)
                for c in range(2):
                    copy(XT[:, c, :], bank(c)).then_inc(xt_act, 1)

            def out_chunks(n):
                act.wait_ge(o_turned, n + 1)
                for c in range(2):
                    copy(XT[:, c, :], bank(c)).then_inc(o_act, 1)

            take_root()
            xt_chunks(0)
            act.wait_ge(ab_landed, 16)
            for oc in range(KC):
                act.wait_ge(a_q, oc + 1)
                act.activation(a_qt[:, oc, :], bank(4 + oc), ACT.Identity, bias=b1c[:, oc:oc + 1]).then_inc(a_qev, 1)
            for oc in range(2):
                act.wait_ge(a_qpd, oc + 1)
                copy(a_qp[:, oc, :], bank(oc)).then_inc(a_qpe_act, 1)
            for b in range(NB):
                act.wait_ge(a_nb, b + 1)
                if b:
                    act.wait_ge(a_t, 4 * b)
                for f in range(2):
                    act.activation(a_p[:, 1024 * f:1024 * (f + 1)], bank(2 * f, 2), ACT.Exp, bias=sm[:, 8 + b:9 + b],
                                   scale=1.0 / 32, accum_out=sm[:, 16 + 2 * b + f:17 + 2 * b + f]).then_inc(a_exp, 1)
                for g in (0, 2):
                    act.wait_ge(a_t, 4 * b + g + 1)
                    copy(a_pt[:, 4 * g:4 * g + 4, :], v3(bank(5), 4)).then_inc(a_pte, 1)
            out_chunks(0)

            if stages >= 2:
                take_root()
                xt_chunks(1)
                act.wait_ge(bb_landed, 80)
                act.activation(sm[:, 80:96], sm[:, 64:80], ACT.Exp).then_inc(b_beta, 1)
                for m in range(2):
                    hf = slice(2048 * m, 2048 * (m + 1))
                    act.wait_ge(b_zs, m + 1)
                    act.activation(b_s1[:, hf], fa(32 + 8 * m, 8), ACT.Abs).then_inc(b_u, 1)
                    act.wait_ge(b_u, 2 * m + 1)
                    act.activation(b_s1[:, hf], b_s1[:, hf], ACT.Exp, scale=-1.0).then_inc(b_u, 1)
                    act.wait_ge(b_w1p, m + 1)
                    act.activation(b_s3[:, hf], b_s2[:, hf], ACT.Ln).then_inc(b_ln, 1)
                out_chunks(1)

            if stages >= 3:
                take_root()
                xt_chunks(2)
                act.wait_ge(xt_act, 6)
                act.wait_ge(xt_dve, 6)
                copy(c_xh, XT[:, :, :]).then_inc(c_xhd, 1)
                act.wait_ge(c_diff, 1)
                act.activation(sm[:, 120:124], sm[:, 116:120], ACT.Exp).then_inc(c_e, 1)

                def c_split12(before, k):
                    act.wait_ge(c_landed[k % NST], before * (16 // NST) + (16 * (k // NST) + 16))
                    if k:
                        act.wait_ge(c_h, before + (k - 1) + AHEAD)
                    copy(c_wh[k % 2][:, 0:2, :], c_st[k % NST][:, 0:2, :]).then_inc(c_hi12, 1)

                def c_expert(e, final):
                    for j in range(UE):
                        if not (final and j == UE - 1):
                            c_split12(e * UE, j + 1)
                        act.wait_ge(c_y, e * UE + (j - 1 + AHEAD))
                        copy(c_wh[j % 2][:, 2, :], c_st[j % NST][:, 2, :]).then_inc(c_hi3, 1)
                        act.wait_ge(c_h, e * UE + (j + 1) + AHEAD)
                        act.wait_ge(c_t, e * UE + j + AHEAD)
                        act.activation(c_sg, bank(2 * (j % 2)), ACT.Sigmoid).then_inc(c_sig, 1)

                def d_split_weights(i):
                    act.wait_ge(dw_landed[1 + i], 16)
                    copy(d_wh[i], d_ws[i]).then_inc(d_whd, 1)

                c_split12(0, 0)
                with act.Fori(0, NE - 1) as e:
                    c_expert(e, False)
                if stages >= 4:
                    d_split_weights(1)
                c_expert(NE - 1, True)

            if stages >= 4:
                act.wait_ge(c_h, NE * UE + AHEAD)
                d_split_weights(0)

                def d_split(b, c):
                    act.wait_ge(d_landed[c % 2], b * 32 + (16 * (c // 2) + 16))
                    if isinstance(b, int) and c < 2:
                        pass
                    else:
                        act.wait_ge(d_pj, b * 32 + (8 * (c - 1)))
                    copy(d_ch[c % 2], d_st[c % 2]).then_inc(d_hi, 1)

                take_root()
                act.wait_ge(c_y, NE * UE + AHEAD)
                d_split(0, 0)
                xt_chunks(3)
                d_split(0, 1)
                for oc in range(KC):
                    act.wait_ge(d_q, oc + 1)
                    copy(Y[:, oc, :], bank(4 + oc)).then_inc(d_qev, 1)

                def d_batch(b, final):
                    for c in range(NCH):
                        for j in range(4):
                            n = 8 * c + (j if c in (0, NCH - 1) else 2 * j)
                            act.wait_ge(d_pj, b * 32 + (n + 1))
                            copy(d_kt[:, j, CH * c:CH * (c + 1)], bank(n % 4)).then_inc(d_kev, 1)
                        if c < 2:
                            act.wait_ge(d_landed[c], b * 32 + 32)
                            act.wait_ge(d_pj, b * 32 + (8 * (c + 1)))
                            copy(d_ch[c], d_st[c]).then_inc(d_hi, 1)
                    for h in range(H0):
                        if h:
                            evac(b, h - 1, 0)
                        act.wait_ge(d_nb, b * H0 + (h + 1))
                        if h >= 2:
                            act.wait_ge(d_t, b * (4 * H0) + 4 * (h - 1))
                        for c in range(NCH):
                            act.activation(d_p[h % 2][:, CH * c:CH * (c + 1)], bank(c), ACT.Exp,
                                           bias=sm[:, 128 + h % 2:129 + h % 2], scale=float(DH0) ** -0.5,
                                           accum_out=sm[:, 136 + 4 * h + c:137 + 4 * h + c]).then_inc(d_exp, 1)
                            if c == 0 and h:
                                evac(b, h - 1, 2)
                        if not final and 2 <= h < 10:
                            c, k = (h - 2) // 4, (h - 2) % 4
                            if k == 0:
                                act.wait_ge(d_landed[c], b * 32 + 48)
                                act.wait_ge(d_pj, b * 32 + 32)
                            part = copy(d_ch[c][:, k, :], d_st[c][:, k, :])
                            if k == 3:
                                part.then_inc(d_hi, 1)
                    evac(b, H0 - 1, 0)
                    evac(b, H0 - 1, 2)

                def evac(b, h, g):
                    act.wait_ge(d_t, b * (4 * H0) + (4 * h + g + 1))
                    copy(d_pt[:, 4 * g:4 * g + 4, :], v3(bank(TB[g]), 4)).then_inc(d_pte, 1)

                with act.Fori(0, NB - 1) as b:
                    d_batch(b, False)
                d_batch(NB - 1, True)

            if stages >= 5:
                def e_high(n):
                    act.wait_ge(ew_landed[n // 8], 16)
                    if n >= NSR:
                        act.wait_ge(e_pj, n - NSR + 1)
                    else:
                        act.wait_ge(d_pj, 8 * NCH * NB)
                    copy(e_wh[n % NSR], e_w[n // 8][:, :, P * (n % 8):P * (n % 8 + 1)]).then_inc(e_whd, 1)

                for n in range(NSR):
                    e_high(n)
                take_root()
                take_root()
                act.wait_ge(ln_turned, 5)
                for c in range(KC):
                    copy(e_xh[:, c, :], bank(c)).then_inc(e_xhd, 1)
                for n in range(16):
                    if n % 2 == 0:
                        act.wait_ge(e_pj, n + 1)
                        act.activation((e_qt, e_kt)[n // 8][:, n % 8, :], bank((4 + n) % 8), ACT.Identity,
                                       bias=(bqc, bkc)[n // 8][:, n % 8:n % 8 + 1]).then_inc(e_eva, 1)
                    if n + NSR < 16:
                        e_high(n + NSR)
                    if n in (9, 11):
                        half = slice(D * (n // 11), D * (n // 11 + 1))
                        act.wait_ge(ew_landed[2], 16)
                        copy(e_vh[:, :, half], e_w[2][:, :, half]).then_inc(e_vhd, 1)
                for i in range(64):
                    act.wait_ge(e_mx, i // 4 + 1)
                    act.activation(e_e(i, 1)[:, 0, :], e_e(i, 1)[:, 0, :], ACT.Exp, bias=e_nm[:, i:i + 1],
                                   accum_out=e_rs[:, i:i + 1]).then_inc(e_exp, 1)
                act.wait_ge(e_z, 1)
                for i in range(0, 8, 2):
                    copy(e_zt[:, i, :], bank(i)).then_inc(e_zev, 1)

            if stages >= 6:
                take_root()
                take_root()
                for t in range(NB):
                    act.wait_ge(f_hd, t + 1)
                    act.activation(f_h[t], f_h[t], ACT.Gelu).then_inc(f_gel, 1)
                    act.wait_ge(f_gel, t + 1)
                    act.activation(f_sq, f_h[t], ACT.Square, accum_out=sm[:, 216 + t:217 + t]).then_inc(f_hsq, 1)
                take_root()

                for t in range(NB):
                    act.wait_ge(f_t, t + 1)
                    if t >= 2:
                        act.wait_ge(f_m2, t - 1)
                    for i in range(2):
                        copy(f_ht[t % 2][:, 8 * i:8 * i + 8, :], v3(bank(4 * (t % 2) + i).bitcast(BF16), 8)) \
                            .then_inc(f_htd, 1)

        @block.vector
        def _(v):
            for signal in (c_t, c_gd, c_acc, d_pto, d_o):
                v.sem_inc(signal, AHEAD)
            count = [0]

            def link(ins):
                count[0] += 1
                ins.then_inc(dve, 1)
                v.wait_ge(dve, count[0])

            roots = [0]

            def inverse_root(ins, t=slice(0, NB)):
                roots[0] += 1
                ins.then_inc(root_asked, 1)
                v.wait_ge(root_done, roots[0])
                x, y, z = rstd[:, t], root[:, t], rtmp[:, t]
                link(v.reciprocal(y, y))
                link(v.tensor_tensor(z, y, y, ALU.mult))
                link(v.tensor_tensor(z, z, x, ALU.mult))
                link(v.tensor_scalar(z, z, -0.5, 1.5, ALU.mult, ALU.add))
                link(v.tensor_tensor(x, y, z, ALU.mult))

            def statistics(t):
                link(v.bn_stats(st[:, t, :], X[:, t, :]))
                link(v.bn_aggr(mv[:, t, :], st[:, t, :]))

            def layernorm(n, rms=None, known=True):
                if not known:
                    for t in range(NB):
                        last = v.bn_stats(st[:, t, :], X[:, t, :])
                    link(last)
                    for t in range(NB):
                        last = v.bn_aggr(mv[:, t, :], st[:, t, :])
                    link(last)
                inverse_root(v.tensor_scalar(rstd[:, :], mv[:, :, 1], 1e-5, None, ALU.add))
                if rms is not None:
                    v.tensor_copy(first_root[:, :], rstd[:, :])
                    link(v.tensor_tensor(rtmp[:, :], rstd[:, :], mv[:, :, 1], ALU.mult))
                    link(v.tensor_tensor(rstd[:, :], rtmp[:, :], rstd[:, :], ALU.mult))
                    inverse_root(v.tensor_scalar(rstd[:, :], rstd[:, :], rms, None, ALU.add))
                    link(v.tensor_tensor(rstd[:, :], rstd[:, :], first_root[:, :], ALU.mult))
                for t in range(NB):
                    v.tensor_scalar(Y[:, t, :], X[:, t, :], mv[:, t, 0:1], rstd[:, t:t + 1],
                                    ALU.subtract, ALU.mult).then_inc(ln_done, 1)

            def xt_chunks(n):
                v.wait_ge(ln_turned, n + 1)
                for c in range(2, 4):
                    v.tensor_copy(XT[:, c, :], bank(c)).then_inc(xt_dve, 1)

            def out_chunks(n):
                v.wait_ge(o_turned, n + 1)
                for c in range(2, 4):
                    v.tensor_copy(XT[:, c, :], bank(c)).then_inc(o_dve, 1)

            def add_projection(n, first=4):
                for t in range(NB):
                    v.wait_ge(proj_done, NB * n + t + 1)
                    v.tensor_tensor(X[:, t, :], X[:, t, :], bank(first + t), ALU.add).then_inc(x_added, 1)
                    v.wait_ge(x_added, NB * n + t + 1)
                    statistics(t)

            v.wait_ge(x_landed, 16)
            layernorm(0, known=False)
            xt_chunks(0)
            for oc in range(2, 4):
                v.wait_ge(a_qpd, oc + 1)
                v.tensor_copy(a_qp[:, oc, :], bank(oc)).then_inc(a_qpe_dve, 1)
            v.wait_ge(a_qb, 1)
            v.tensor_copy(sm[:, 0:4], bank(4)[:, 0:4]).then_inc(a_qpe_dve, 1)
            v.wait_ge(a_qpe_dve, 3)

            def a_take(b):
                link(v.tensor_tensor(sm[:, 24 + b:25 + b], sm[:, 16 + 2 * b:17 + 2 * b],
                                     sm[:, 17 + 2 * b:18 + 2 * b], ALU.add))
                link(v.reciprocal(sm[:, 28 + b:29 + b], sm[:, 24 + b:25 + b]))
                v.wait_ge(a_pv, 4 * (b + 1))
                v.tensor_scalar(a_ao[:, b, :], bank(4), sm[:, 28 + b:29 + b], None, ALU.mult).then_inc(a_o, 1)

            for b in range(NB):
                for f in range(2):
                    v.wait_ge(a_s, 4 * b + 2 * f + 2)
                    last = v.tensor_reduce(sm[:, 32 + 2 * b + f:33 + 2 * b + f], bank(2 * f, 2), AX, ALU.max)
                link(last)
                link(v.tensor_scalar(sm[:, 40 + b:41 + b], sm[:, 32 + 2 * b:33 + 2 * b], sm[:, 33 + 2 * b:34 + 2 * b],
                                     sm[:, b:b + 1], ALU.max, ALU.add))
                v.tensor_scalar(sm[:, 8 + b:9 + b], sm[:, 40 + b:41 + b], sm[:, b:b + 1], -1.0 / 32,
                                ALU.subtract, ALU.mult).then_inc(a_nb, 1)
                if b:
                    a_take(b - 1)
                for g in (1, 3):
                    v.wait_ge(a_t, 4 * b + g + 1)
                    v.tensor_copy(a_pt[:, 4 * g:4 * g + 4, :], v3(bank(6), 4)).then_inc(a_pto, 1)
                v.wait_ge(a_exp, 2 * b + 2)
            a_take(NB - 1)
            out_chunks(0)
            add_projection(0)

            if stages >= 2:
                layernorm(1)
                xt_chunks(1)
                v.wait_ge(bb_landed, 80)
                v.wait_ge(b_beta, 1)
                link(v.tensor_scalar(sm[:, 96:112], sm[:, 80:96], float(DH0) ** 0.5, None, ALU.mult))
                link(v.reciprocal(sm[:, 80:96], sm[:, 96:112]))
                for t in range(NB):
                    last = v.tensor_tensor(X[:, t, :], X[:, t, :], BI[:, 3 * D:4 * D], ALU.add)
                link(last)

                def b_add(m, t):
                    n = 4 * m + t
                    v.wait_ge(b_p, n + 1)
                    v.tensor_tensor(b_z[:, n, :], bank(n), BI[:, D * m:D * (m + 1)], ALU.add).then_inc(b_zq, 1)

                def b_scale(m):
                    v.wait_ge(b_zq, 4 * (m + 1))
                    z4 = b_z[:, 4 * m:4 * m + 4, :].rearrange("p a (h d) -> p a h d", h=H0)
                    sc = sm[:, 80:96].unsqueeze(1).unsqueeze(3).broadcast_to([P, 4, H0, DH0])
                    v.tensor_tensor(z4, z4, sc, ALU.mult).then_inc(b_zs, 1)

                def b_add_v(t):
                    v.wait_ge(b_p, 8 + t + 1)
                    v.tensor_tensor(b_v[:, t, :], bank(t), BI[:, 2 * D:3 * D], ALU.add).then_inc(b_zq, 1)

                def b_one_more(m):
                    hf = slice(2048 * m, 2048 * (m + 1))
                    v.wait_ge(b_u, 2 * m + 2)
                    v.tensor_scalar(b_s2[:, hf], b_s1[:, hf], 1.0, None, ALU.add).then_inc(b_w1p, 1)
                    v.wait_ge(b_w1p, m + 1)
                    link(v.scalar_tensor_tensor(b_s1[:, hf], b_s2[:, hf], -1.0, b_s1[:, hf], ALU.add, ALU.subtract))

                def b_softplus(m):
                    hf = slice(2048 * m, 2048 * (m + 1))
                    v.wait_ge(b_ln, m + 1)
                    link(v.tensor_tensor(b_s3[:, hf], b_s3[:, hf], b_s1[:, hf], ALU.subtract))
                    zf = fa(32 + 8 * m, 8)
                    v.scalar_tensor_tensor(zf, zf, 0.0, b_s3[:, hf], ALU.max, ALU.add).then_inc(b_sp, 1)

                for t in range(NB):
                    b_add(0, t)
                b_scale(0)
                b_add(1, 0)
                b_add(1, 1)
                b_one_more(0)
                b_add(1, 2)
                b_add(1, 3)
                b_scale(1)
                b_softplus(0)
                b_add_v(0)
                b_one_more(1)
                b_add_v(1)
                b_add_v(2)
                b_softplus(1)
                b_add_v(3)
                v.wait_ge(b_sp, 2)
                v.wait_ge(b_zq, 12)
                pr = v3(b_s1[:, 0:2048], 4)
                att = b_s2[:, 0:256].rearrange("p (s t h) -> p s t h", s=4, t=4)
                den = b_s2[:, 256:320].rearrange("p (s h) -> p s h", s=4)
                rden = b_s2[:, 320:384].rearrange("p (s h) -> p s h", s=4)
                for s in range(NB):
                    n = s + 1
                    qk = pr[:, 0:n, :]
                    if s < 2:
                        link(v.tensor_tensor(qk, b_z[:, s:s + 1, :].broadcast_to([P, n, D]), b_z[:, 4:4 + n, :],
                                             ALU.mult))
                    else:
                        v.wait_ge(b_qk, s - 1)
                        qk = b_qks[s - 2]
                    link(v.tensor_reduce(att[:, s, 0:n, :], qk.rearrange("p a (h d) -> p a h d", h=H0),
                                         AX, ALU.add))
                    link(v.tensor_reduce(den[:, s, :], att[:, s, 0:n, :].rearrange("p t h -> p h t"), AX, ALU.add))
                    link(v.reciprocal(rden[:, s, :], den[:, s, :]))
                    link(v.tensor_tensor(pr[:, 0:n, :].rearrange("p a (h d) -> p a h d", h=H0),
                                         att[:, s, 0:n, :].unsqueeze(3).broadcast_to([P, n, H0, DH0]),
                                         b_v[:, 0:n, :].rearrange("p a (h d) -> p a h d", h=H0), ALU.mult))
                    link(v.tensor_reduce(b_ao[:, s, :], pr[:, 0:n, :].rearrange("p t n -> p n t"), AX, ALU.add))
                    o3 = b_ao[:, s, :].rearrange("p (h d) -> p h d", h=H0)
                    v.tensor_tensor(o3, o3, rden[:, s, :].unsqueeze(2).broadcast_to([P, H0, DH0]), ALU.mult) \
                        .then_inc(b_o, 1)
                out_chunks(1)
                add_projection(1)

            if stages >= 3:
                layernorm(2)
                xt_chunks(2)
                v.wait_ge(xt_dve, 6)
                v.wait_ge(xt_act, 6)
                v.wait_ge(c_xhd, 1)
                v.tensor_tensor(c_xl, XT[:, :, :], c_xh.bitcast(F32), ALU.subtract).then_inc(c_xld, 1)
                v.wait_ge(c_gate, 1)
                v.wait_ge(const_ready, N_CONST)
                gt = g_[:, 0:32].rearrange("p (t e) -> p t e", t=NB)
                oh = [g_[:, 32 * (i + 1):32 * (i + 2)].rearrange("p (t e) -> p t e", t=NB) for i in range(2)]
                g2 = g_[:, 96:128].rearrange("p (t e) -> p t e", t=NB)
                wt = g_[:, 128:160].rearrange("p (t e) -> p t e", t=NB)
                m12 = [sm[:, 100:104], sm[:, 104:108]]
                mxi = sm[:, 108:112]

                def over_e(ap):
                    return ap.unsqueeze(2).broadcast_to([P, NB, NE])

                rv = rev8[:, :].unsqueeze(1).broadcast_to([P, NB, NE])
                link(v.tensor_copy(gt, bank(7)[:, 0:NB * NE].rearrange("p (t e) -> p t e", t=NB)))
                src = gt
                for i in range(2):
                    link(v.tensor_reduce(m12[i], src, AX, ALU.max))
                    link(v.tensor_tensor(oh[i], src, over_e(m12[i]), ALU.is_equal))
                    link(v.tensor_tensor(oh[i], oh[i], rv, ALU.mult))
                    link(v.tensor_reduce(mxi, oh[i], AX, ALU.max))
                    link(v.tensor_tensor(oh[i], oh[i], over_e(mxi), ALU.is_equal))
                    if i == 0:
                        link(v.scalar_tensor_tensor(g2, oh[0], NEG, gt, ALU.mult, ALU.add))
                        src = g2
                v.tensor_tensor(sm[:, 116:120], m12[1], m12[0], ALU.subtract).then_inc(c_diff, 1)
                v.wait_ge(c_e, 1)
                link(v.tensor_scalar(sm[:, 112:116], sm[:, 120:124], 1.0, None, ALU.add))
                link(v.reciprocal(sm[:, 100:104], sm[:, 112:116]))
                link(v.tensor_tensor(sm[:, 104:108], sm[:, 100:104], sm[:, 120:124], ALU.mult))
                for i in range(2):
                    link(v.tensor_tensor(oh[i], oh[i], over_e(m12[i]), ALU.mult))
                link(v.tensor_tensor(wt, oh[0], oh[1], ALU.add))

                def c_low12(u, k):
                    v.wait_ge(c_hi12, u + 1)
                    v.tensor_tensor(c_wl[k % 2][:, 0:2, :], c_st[k % NST][:, 0:2, :],
                                    c_wh[k % 2][:, 0:2, :].bitcast(F32), ALU.subtract).then_inc(c_lo12, 1)

                def c_low3(u, k):
                    v.wait_ge(c_hi3, u + 1)
                    v.tensor_tensor(c_wl[k % 2][:, 2, :], c_st[k % NST][:, 2, :],
                                    c_wh[k % 2][:, 2, :].bitcast(F32), ALU.subtract).then_inc(c_lo3, 1)

                def c_unit(e, j, final=False):
                    u = e * UE + j
                    s = j % 2
                    if not final:
                        c_low12(e * UE + (j + 1), j + 1)
                    c_low3(u, j)
                    v.wait_ge(c_sig, u + 1)
                    v.tensor_tensor(c_tt, c_sg, bank(2 * s), ALU.mult).then_inc(c_t, 1)
                    v.wait_ge(c_t, u + 1 + AHEAD)
                    v.tensor_tensor(c_g, c_tt, bank(2 * s + 1), ALU.mult).then_inc(c_gd, 1)
                    v.wait_ge(c_gd, u + 1 + AHEAD)
                    v.tensor_copy(c_gh[s], c_g).then_inc(c_ghd, 1)
                    v.wait_ge(c_ghd, u + 1)
                    v.tensor_tensor(c_gl[s], c_g, c_gh[s].bitcast(F32), ALU.subtract).then_inc(c_gld, 1)

                def c_accumulate(e):
                    v.wait_ge(c_y, e * UE + UE + AHEAD)
                    for t in range(NB):
                        last = v.scalar_tensor_tensor(X[:, t, :], bank(4 + t), wt[:, t, bass.ds(e, 1)], X[:, t, :],
                                                      ALU.mult, ALU.add)
                    last.then_inc(c_acc, 1)
                    v.wait_ge(c_acc, e + 1 + AHEAD)

                def d_low_weights(i):
                    v.wait_ge(d_whd, 2 - i)
                    v.tensor_tensor(d_wl[i], d_ws[i], d_wh[i].bitcast(F32), ALU.subtract).then_inc(d_wld, 1)

                c_low12(0, 0)
                c_unit(0, 0)
                with v.Fori(0, NE - 1) as e:
                    for j in range(UE):
                        c_unit(e, j + 1)
                    c_accumulate(e)
                if stages >= 4:
                    d_low_weights(1)
                for j in range(1, UE):
                    c_unit(NE - 1, j, final=(j == UE - 1))
                c_accumulate(NE - 1)

            if stages >= 4:

                def d_low(n, s):
                    v.wait_ge(d_hi, n + 1)
                    v.tensor_tensor(d_cl[s], d_st[s], d_ch[s].bitcast(F32), ALU.subtract).then_inc(d_lo, 1)

                layernorm(3, known=False)
                xt_chunks(3)
                d_low_weights(0)
                d_low(0, 0)
                d_low(1, 1)

                def evac_v(b, c, j):
                    n = 8 * c + (4 + j if c in (0, NCH - 1) else 2 * j + 1)
                    v.wait_ge(d_pj, b * 32 + (n + 1))
                    v.tensor_copy(d_v[:, 4 * c + j, :], bank(n % 4 if c < NCH - 1 else 4 + j)).then_inc(d_vev, 1)

                def e_low(n):
                    v.wait_ge(e_whd, n + 1)
                    v.tensor_tensor(e_wl[n % NSR], e_w[n // 8][:, :, P * (n % 8):P * (n % 8 + 1)],
                                    e_wh[n % NSR].bitcast(F32), ALU.subtract).then_inc(e_wld, 1)

                def evac(b, h, g):
                    v.wait_ge(d_t, b * (4 * H0) + (4 * h + g + 1))
                    v.tensor_copy(d_pt[:, 4 * g:4 * g + 4, :], v3(bank(TB[g]), 4)).then_inc(d_pto, 1)

                def d_batch(b, final):
                    for c in range(NCH):
                        for j in range(4 if c < NCH - 1 else 2):
                            evac_v(b, c, j)
                        if c < 2:
                            d_low(b * NCH + (c + 2), c)
                    for h in range(H0):
                        for c in range(NCH):
                            v.wait_ge(d_s, b * (4 * H0) + (4 * h + c + 1) + AHEAD)
                            v.tensor_reduce(sm[:, 130 + c:131 + c], bank(c), AX, ALU.max).then_inc(d_mx, 1)
                        v.wait_ge(d_mx, b * (5 * H0) + (5 * h + 4))
                        v.tensor_reduce(sm[:, 134:135], sm[:, 130:134], AX, ALU.max).then_inc(d_mx, 1)
                        v.wait_ge(d_mx, b * (5 * H0) + (5 * h + 5))
                        v.tensor_scalar(sm[:, 128 + h % 2:129 + h % 2], sm[:, 134:135],
                                        -float(DH0) ** -0.5, None, ALU.mult).then_inc(d_nb, 1)
                        if h == 0:
                            for j in range(2, 4):
                                evac_v(b, NCH - 1, j)
                        if h:
                            evac(b, h - 1, 1)
                            evac(b, h - 1, 3)
                        if not final and 6 <= h < 14:
                            c, k = (h - 6) // 4, (h - 6) % 4
                            if k == 0:
                                v.wait_ge(d_hi, b * NCH + (NCH + c + 1))
                            part = v.tensor_tensor(d_cl[c][:, k, :], d_st[c][:, k, :], d_ch[c][:, k, :].bitcast(F32),
                                                   ALU.subtract)
                            if k == 3:
                                part.then_inc(d_lo, 1)
                    evac(b, H0 - 1, 1)
                    evac(b, H0 - 1, 3)
                    v.wait_ge(d_exp, b * (4 * H0) + 4 * H0 + AHEAD)
                    rs = sm[:, 136:200].rearrange("p (h c) -> p h c", c=NCH)
                    v.tensor_reduce(sm[:, 64:80], rs, AX, ALU.add).then_inc(d_sum, 1)
                    v.wait_ge(d_sum, b * 3 + 1)
                    v.reciprocal(sm[:, 80:96], sm[:, 64:80]).then_inc(d_sum, 1)
                    v.wait_ge(d_sum, b * 3 + 2)
                    v.tensor_copy(d_rx[:, :].rearrange("p (h d) -> p h d", h=H0),
                                  sm[:, 80:96].unsqueeze(2).broadcast_to([P, H0, DH0])).then_inc(d_rxd, 1)
                    v.wait_ge(d_rt, b + 1)
                    v.tensor_copy(d_rx[:, :], bank(7)).then_inc(d_sum, 1)
                    v.wait_ge(d_sum, b * 3 + 3)
                    v.wait_ge(d_pv, b * H0 + H0)
                    v.tensor_tensor(XT[:, :, bass.ds(b * P, P)], v3(bank(6), KC), v3(d_rx[:, :], KC), ALU.mult) \
                        .then_inc(d_o, 1)

                with v.Fori(0, NB - 1) as b:
                    d_batch(b, False)
                d_batch(NB - 1, True)
                if stages >= 5:
                    for n in range(NSR):
                        e_low(n)
                add_projection(2, first=0)

            if stages >= 5:
                layernorm(4, rms=1.1920929e-07)
                for c in range(KC):
                    v.wait_ge(e_xhd, c + 1)
                    v.tensor_tensor(e_xl[:, c, :], bank(c), e_xh[:, c, :].bitcast(F32), ALU.subtract).then_inc(e_xld, 1)
                v.wait_ge(eb_landed, 32)
                for t in range(NB):
                    last = v.tensor_tensor(X[:, t, :], X[:, t, :], BI[:, DQ:DQ + D], ALU.add)
                link(last)
                for n in range(16):
                    if n % 2:
                        v.wait_ge(e_pj, n + 1)
                        v.tensor_scalar((e_qt, e_kt)[n // 8][:, n % 8, :], bank((4 + n) % 8),
                                        (bqc, bkc)[n // 8][:, n % 8:n % 8 + 1], None, ALU.add).then_inc(e_evd, 1)
                    if n + NSR < 16:
                        e_low(n + NSR)
                    if n in (9, 11):
                        half = slice(D * (n // 11), D * (n // 11 + 1))
                        v.wait_ge(e_vhd, n // 11 + 1)
                        v.tensor_tensor(e_vl[:, :, half], e_w[2][:, :, half], e_vh[:, :, half].bitcast(F32),
                                        ALU.subtract).then_inc(e_vld, 1)

                def e_add_v(n):
                    v.wait_ge(e_pj, 16 + n + 1)
                    f = n % 2
                    v.tensor_tensor(e_v[:, n // 2, D * f:D * (f + 1)], bank(n % 4), BI[:, D * f:D * (f + 1)],
                                    ALU.add).then_inc(e_evd, 1)

                def e_scale(b):
                    v.wait_ge(e_exp, 16 * (b + 1))
                    link(v.reciprocal(e_ri[:, 16 * b:16 * (b + 1)], e_rs[:, 16 * b:16 * (b + 1)]))
                    for f in range(2):
                        v4 = e_v[:, b, D * f:D * (f + 1)].rearrange("p (j q d) -> p j q d", j=4, q=2)
                        ri = e_ri[:, 16 * b + 8 * f:16 * b + 8 * f + 8].rearrange("p (q j) -> p j q", q=2)
                        last = v.tensor_tensor(v4, v4, ri.unsqueeze(3).broadcast_to([P, 4, 2, DH1]), ALU.mult)
                    last.then_inc(e_vs, 1)

                e_add_v(0)
                e_add_v(1)
                for g in range(16):
                    v.wait_ge(e_s, g + 1)
                    eg = e_e(4 * g, 4)
                    v.tensor_tensor(eg, v3(bank(4 + g % 4), 4), caus[:, :].unsqueeze(1).broadcast_to([P, 4, P]),
                                    ALU.add).then_inc(e_m, 1)
                    v.wait_ge(e_m, g + 1)
                    v.tensor_reduce(e_nm[:, 4 * g:4 * g + 4], eg, AX, ALU.max, negate=True).then_inc(e_mx, 1)
                    if g % 2 and g < 12:
                        e_add_v(2 + g // 2)
                    if g % 4 == 1 and g > 4:
                        e_scale(g // 4 - 1)
                e_scale(3)
                v.wait_ge(e_z, 1)
                for i in range(1, 8, 2):
                    v.tensor_copy(e_zt[:, i, :], bank(i)).then_inc(e_zevd, 1)
                add_projection(3)

            if stages >= 6:
                layernorm(5, rms=1e-5)
                v.wait_ge(ln_done, 24)
                link(v.tensor_reduce(sm[:, 212:216], Y[:, :, :], AX, ALU.max, apply_absolute_value=True))

                def int8_scale(m, dq, dqs, n):
                    link(v.tensor_scalar(m, m, 1e-5, None, ALU.max))
                    link(v.reciprocal(dq, m))
                    v.tensor_scalar(dqs, m, 1.0 / 127.0, wmean[:, n:n + 1], ALU.mult, ALU.mult)
                    link(v.tensor_scalar(dq, dq, 127.0, None, ALU.mult))

                int8_scale(sm[:, 212:216], sm[:, 220:224], sm[:, 224:228], 0)
                for t in range(NB):
                    last = v.tensor_scalar(Y[:, t, :], Y[:, t, :], sm[:, 220 + t:221 + t], 127.0, ALU.mult, ALU.min)
                link(last)
                for i in range(2):
                    y = Y[:, 2 * i:2 * i + 2, :]
                    link(v.tensor_scalar(y, y, -128.0, MAGIC, ALU.max, ALU.add))
                    v.tensor_scalar(f_yb[:, 2 * i:2 * i + 2, :], y, MAGIC, None, ALU.subtract).then_inc(f_ybd, 1)
                v.wait_ge(f_yt_t, 1)
                for i in range(2):
                    last = v.tensor_copy(f_yt[:, 2 * i:2 * i + 2, :], v3(bank(4 + i).bitcast(BF16), 2))
                last.then_inc(f_ytd, 1)
                v.wait_ge(fb_landed, 32)
                for t in range(NB):
                    last = v.tensor_tensor(X[:, t, :], X[:, t, :], d_rx[:, :], ALU.add)
                link(last)

                def f_take(t):
                    for f in range(2):
                        half = slice(1024 * f, 1024 * (f + 1))
                        v.wait_ge(f_m1, 4 * t + 2 * f + 2)
                        last = v.scalar_tensor_tensor(f_h[t][:, half], bank(4 * (t % 2) + 2 * f, 2),
                                                      sm[:, 224 + t:225 + t], f_b1[:, half], ALU.mult, ALU.add)
                    last.then_inc(f_hd, 1)

                def f_max(t):
                    v.wait_ge(f_gel, t + 1)
                    return v.tensor_reduce(sm[:, 232 + t:233 + t], f_h[t], AX, ALU.max, apply_absolute_value=True)

                f_take(0)
                for t in range(1, NB):
                    f_take(t)
                    f_max(t - 1)
                link(f_max(NB - 1))
                v.wait_ge(f_hsq, NB)
                inverse_root(v.tensor_scalar(rstd[:, :], sm[:, 216:220], 1.0 / FF, 1e-5, ALU.mult, ALU.add))
                link(v.tensor_tensor(sm[:, 232:236], sm[:, 232:236], rstd[:, :], ALU.mult))
                int8_scale(sm[:, 232:236], sm[:, 244:248], sm[:, 248:252], 1)

                def f_round(t):
                    h = f_h[t]
                    link(v.tensor_scalar(h, h, rstd[:, t:t + 1], sm[:, 244 + t:245 + t], ALU.mult, ALU.mult))
                    link(v.tensor_scalar(h, h, 127.0, -128.0, ALU.min, ALU.max))
                    if t >= 2:
                        v.wait_ge(f_t, t - 1)
                    v.tensor_scalar(f_hb[t % 2], h, MAGIC, MAGIC, ALU.add, ALU.subtract).then_inc(f_hbd, 1)

                def f_add(t):
                    v.wait_ge(f_m2, t + 1)
                    v.scalar_tensor_tensor(X[:, t, :], bank(4 * (t % 2) + 2), sm[:, 248 + t:249 + t], X[:, t, :],
                                           ALU.mult, ALU.add).then_inc(x_added, 1)

                for t in range(NB):
                    f_round(t)
                    if t >= 2:
                        f_add(t - 2)
                f_add(NB - 2)
                f_add(NB - 1)


def kernel(**inputs):
    import numpy as np
    import concourse.bacc as bacc
    from concourse.bass_utils import run_bass_kernel_spmd

    a = {k: np.asarray(v) for k, v in inputs.items()}

    def rows(w):
        return np.ascontiguousarray(w.reshape(-1, P, w.shape[1]).transpose(1, 0, 2))

    def columns(v):
        return v.reshape(-1, P).T

    c = a["ctx_1024"].reshape(NB * NCH, CH, D)
    qkv = a["L1_attn_W_qkv"].reshape(DQ, 3, D)
    bqkv = a["L1_attn_b_qkv"].reshape(DQ, 3)
    ins = {
        "x": a["x"],
        "ctx_n": c.reshape(NB * NCH, 4, P, D).transpose(0, 2, 1, 3),
        "ctx_t": c.transpose(0, 2, 1).reshape(NB * NCH, KC, P, CH).transpose(0, 2, 1, 3),
        "w1t": rows(a["L0_xattn_W1"].T), "w2n": rows(a["L0_xattn_W2"]), "w3t": rows(a["L0_xattn_W3"].T),
        "bcols": np.concatenate([columns(a["L0_xattn_b1"]), columns(a["L0_xattn_b2"]), columns(bqkv[:, 0]),
                                 columns(bqkv[:, 1]), np.zeros((P, 8), np.float32)], axis=1),
        "beta": a["L0_attn_beta"],
        "l0a_w": np.stack([rows(a[f"L0_attn_W{n}"].T) for n in "qkvo"]),
        "l0a_bq": a["L0_attn_bq"], "l0a_bk": a["L0_attn_bk"], "l0a_bv": a["L0_attn_bv"], "l0a_bo": a["L0_attn_bo"],
        "wgt": rows(a["L0_ffn_Wg"].T),
        "moe_w": np.stack([
            a["L0_ffn_W1"].reshape(NE * UE, P, KC, P).transpose(0, 3, 2, 1).reshape(NE * UE, P, D),
            a["L0_ffn_W2"].reshape(NE * UE, P, KC, P).transpose(0, 3, 2, 1).reshape(NE * UE, P, D),
            a["L0_ffn_W3"].reshape(NE, D, UE, P).transpose(0, 2, 3, 1).reshape(NE * UE, P, D)], axis=2),
        "l1x_w": np.stack([rows(a[f"L1_xattn_W{n}"].T) for n in "qkvo"]),
        "l1a_w": np.stack([rows(qkv[:, i].T) for i in range(3)]),
        "l1a_bv": bqkv[:, 2], "l1a_bo": a["L1_attn_b_o"], "l1a_wo": rows(a["L1_attn_W_o"].T),
        "w1t_f": rows(a["L1_ffn_w1"].T), "w2t_f": rows(a["L1_ffn_w2"].T),
        "l1f_b1": a["L1_ffn_b1"], "l1f_b2": a["L1_ffn_b2"],
    }
    nc = bacc.Bacc("TRN2", target_bir_lowering=False, num_devices=1)
    arrays, aps = {}, {}
    for name, v in ins.items():
        v = np.ascontiguousarray(v)
        arrays[f"in_{name}"] = v
        aps[name] = nc.dram_tensor(f"in_{name}", v.shape, mybir.dt.from_np(v.dtype), kind="ExternalInput").ap()
    out = nc.dram_tensor("out_x", (NB, P, D), F32, kind="ExternalOutput").ap()
    build(nc, aps, out)
    r = run_bass_kernel_spmd(nc, [arrays], core_ids=[0])
    return r.results[0]["out_x"]
```
